# Optimizing a Trainium2 kernel written in Bass

```python
import numpy as np
import jax
import jax.numpy as jnp

def _softmax(x, axis=-1):
    return jax.nn.softmax(x, axis=axis)

def _gelu(x):
    return jax.nn.gelu(x, approximate=True)

def _silu(x):
    return jax.nn.silu(x)

def _sigmoid(x):
    return jax.nn.sigmoid(x)

def _layernorm(x, axis=-1, eps=1e-05):
    m = jnp.mean(x, axis=axis, keepdims=True)
    v = jnp.var(x, axis=axis, keepdims=True)
    return (x - m) / jnp.sqrt(v + eps)

def _scatter_add(tgt, idx, src, axis=0):
    return tgt.at[idx].add(src)

def _segment_sum(src, seg, n):
    return jax.ops.segment_sum(src, seg, n)
kernel_name = 'mk_vit_tower_postln_d1_tok_img768_r4_c46509'

def setup_inputs(seed: int=0):
    np.random.seed(seed)
    _w = jnp.asarray

    def _rec_inputs():
        import jax
        import jax.numpy as jnp
        _rk = jax.random.key(seed)
        x = 7.57192e-06 + 1.00007 * jax.random.normal(jax.random.fold_in(_rk, 1), (64, 3, 96, 96), jnp.float32)
        return x
    x = _rec_inputs()

    def _L0_tok_setup():
        import jax, jax.numpy as jnp
        import numpy as np
        PATCH = 16
        HALF = PATCH // 2
        DIM = 192
        CH = 3
        PATCH_DIM = PATCH * PATCH * 5 * CH
        LN_EPS = 1e-05

        def _shift2d(x, t, l):
            H, W = (x.shape[-2], x.shape[-1])
            at, al = (abs(t), abs(l))
            xp = jnp.pad(x, ((0, 0), (0, 0), (at, at), (al, al)))
            return xp[:, :, at - t:at - t + H, al - l:al - l + W]
        key = jax.random.key(seed)
        k1, k2 = jax.random.split(key, 2)
        x = jax.random.normal(k1, (64, CH, 224, 224), dtype=jnp.float32)
        ln_gamma = jnp.ones((PATCH_DIM,), dtype=jnp.float32)
        ln_beta = jnp.zeros((PATCH_DIM,), dtype=jnp.float32)
        W = jax.random.normal(k2, (DIM, PATCH_DIM), dtype=jnp.float32) * np.float32(1.0 / np.sqrt(PATCH_DIM))
        b = jnp.zeros((DIM,), dtype=jnp.float32)
        return {'x': x, 'ln_gamma': ln_gamma, 'ln_beta': ln_beta, 'W': W, 'b': b}
    _L0_tok_all = _L0_tok_setup()
    _L0_tok_in = {k: v for k, v in _L0_tok_all.items() if k in ('ln_gamma', 'ln_beta', 'W', 'b')}
    del _L0_tok_all

    def _L0_attn_setup():
        import math
        import jax, jax.numpy as jnp
        import numpy as np
        B, S, IN_DIM, EMB, H, MAX_LEN = (4, 128, 192, 192, 12, 128)
        D = EMB // H
        key = jax.random.key(seed)
        ks = jax.random.split(key, 16)

        def lin(k, fan_in, fan_out):
            lim = math.sqrt(6.0 / (fan_in + fan_out))
            W = jax.random.uniform(k, (fan_in, fan_out), minval=-lim, maxval=lim, dtype=jnp.float32)
            return (W, jnp.zeros((fan_out,), jnp.float32))
        Wq, bq = lin(ks[0], IN_DIM, EMB)
        Wk, bk = lin(ks[1], IN_DIM, EMB)
        Wv, bv = lin(ks[2], IN_DIM, EMB)
        Wpk, bpk = lin(ks[3], IN_DIM, EMB)
        Wpq, bpq = lin(ks[4], IN_DIM, EMB)
        Wo, bo = lin(ks[5], EMB, IN_DIM)
        rel_table = jax.random.normal(ks[6], (2 * MAX_LEN - 1, IN_DIM), jnp.float32)
        x = jax.random.normal(ks[7], (B, S, IN_DIM), jnp.float32)
        return {'x': x, 'Wq': Wq, 'bq': bq, 'Wk': Wk, 'bk': bk, 'Wv': Wv, 'bv': bv, 'rel_table': rel_table, 'Wpk': Wpk, 'bpk': bpk, 'Wpq': Wpq, 'bpq': bpq, 'Wo': Wo, 'bo': bo}
    _L0_attn_all = _L0_attn_setup()
    _L0_attn_in = {k: v for k, v in _L0_attn_all.items() if k in ('Wq', 'bq', 'Wk', 'bk', 'Wv', 'bv', 'rel_table', 'Wpk', 'bpk', 'Wpq', 'bpq', 'Wo', 'bo')}
    del _L0_attn_all

    def _L0_ffn_setup():
        import jax, jax.numpy as jnp
        import numpy as np
        B, L, D, H, F = (4, 512, 192, 12, 768)
        ROUTE_FRAC = 0.15
        LN_EPS = 1e-05

        def _ln(x, g, b):
            m = jnp.mean(x, axis=-1, keepdims=True)
            v = jnp.mean((x - m) ** 2, axis=-1, keepdims=True)
            return (x - m) * jax.lax.rsqrt(v + LN_EPS) * g + b
        key = jax.random.key(seed)
        ks = jax.random.split(key, 20)
        s = 0.02
        return {'hidden_states': jax.random.normal(ks[0], (B, L, D), dtype=jnp.float32), 'g1': jnp.ones((D,), jnp.float32), 'b1': jnp.zeros((D,), jnp.float32), 'g2': jnp.ones((D,), jnp.float32), 'b2': jnp.zeros((D,), jnp.float32), 'Wr': jax.random.normal(ks[1], (D,), jnp.float32) * s, 'br': jnp.zeros((), jnp.float32), 'Wq': jax.random.normal(ks[2], (D, D), jnp.float32) * s, 'bq': jnp.zeros((D,), jnp.float32), 'Wk': jax.random.normal(ks[3], (D, D), jnp.float32) * s, 'bk': jnp.zeros((D,), jnp.float32), 'Wv': jax.random.normal(ks[4], (D, D), jnp.float32) * s, 'bv': jnp.zeros((D,), jnp.float32), 'Wo': jax.random.normal(ks[5], (D, D), jnp.float32) * s, 'bo': jnp.zeros((D,), jnp.float32), 'Wm': jax.random.normal(ks[6], (D, D), jnp.float32) * s, 'bm': jnp.zeros((D,), jnp.float32), 'W1': jax.random.normal(ks[7], (D, F), jnp.float32) * s, 'bf1': jnp.zeros((F,), jnp.float32), 'W2': jax.random.normal(ks[8], (F, D), jnp.float32) * s, 'bf2': jnp.zeros((D,), jnp.float32)}
    _L0_ffn_all = _L0_ffn_setup()
    _L0_ffn_in = {k: v for k, v in _L0_ffn_all.items() if k in ('g1', 'b1', 'g2', 'b2', 'Wr', 'br', 'Wq', 'bq', 'Wk', 'bk', 'Wv', 'bv', 'Wo', 'bo', 'Wm', 'bm', 'W1', 'bf1', 'W2', 'bf2')}
    del _L0_ffn_all
    return {'x': x, 'L0_tok_ln_gamma': _L0_tok_in['ln_gamma'], 'L0_tok_ln_beta': _L0_tok_in['ln_beta'], 'L0_tok_W': _L0_tok_in['W'], 'L0_tok_b': _L0_tok_in['b'], 'L0_attn_Wq': _L0_attn_in['Wq'], 'L0_attn_bq': _L0_attn_in['bq'], 'L0_attn_Wk': _L0_attn_in['Wk'], 'L0_attn_bk': _L0_attn_in['bk'], 'L0_attn_Wv': _L0_attn_in['Wv'], 'L0_attn_bv': _L0_attn_in['bv'], 'L0_attn_rel_table': _L0_attn_in['rel_table'], 'L0_attn_Wpk': _L0_attn_in['Wpk'], 'L0_attn_bpk': _L0_attn_in['bpk'], 'L0_attn_Wpq': _L0_attn_in['Wpq'], 'L0_attn_bpq': _L0_attn_in['bpq'], 'L0_attn_Wo': _L0_attn_in['Wo'], 'L0_attn_bo': _L0_attn_in['bo'], 'L0_ffn_g1': _L0_ffn_in['g1'], 'L0_ffn_b1': _L0_ffn_in['b1'], 'L0_ffn_g2': _L0_ffn_in['g2'], 'L0_ffn_b2': _L0_ffn_in['b2'], 'L0_ffn_Wr': _L0_ffn_in['Wr'], 'L0_ffn_br': _L0_ffn_in['br'], 'L0_ffn_Wq': _L0_ffn_in['Wq'], 'L0_ffn_bq': _L0_ffn_in['bq'], 'L0_ffn_Wk': _L0_ffn_in['Wk'], 'L0_ffn_bk': _L0_ffn_in['bk'], 'L0_ffn_Wv': _L0_ffn_in['Wv'], 'L0_ffn_bv': _L0_ffn_in['bv'], 'L0_ffn_Wo': _L0_ffn_in['Wo'], 'L0_ffn_bo': _L0_ffn_in['bo'], 'L0_ffn_Wm': _L0_ffn_in['Wm'], 'L0_ffn_bm': _L0_ffn_in['bm'], 'L0_ffn_W1': _L0_ffn_in['W1'], 'L0_ffn_bf1': _L0_ffn_in['bf1'], 'L0_ffn_W2': _L0_ffn_in['W2'], 'L0_ffn_bf2': _L0_ffn_in['bf2']}

def reference(x, L0_tok_ln_gamma, L0_tok_ln_beta, L0_tok_W, L0_tok_b, L0_attn_Wq, L0_attn_bq, L0_attn_Wk, L0_attn_bk, L0_attn_Wv, L0_attn_bv, L0_attn_rel_table, L0_attn_Wpk, L0_attn_bpk, L0_attn_Wpq, L0_attn_bpq, L0_attn_Wo, L0_attn_bo, L0_ffn_g1, L0_ffn_b1, L0_ffn_g2, L0_ffn_b2, L0_ffn_Wr, L0_ffn_br, L0_ffn_Wq, L0_ffn_bq, L0_ffn_Wk, L0_ffn_bk, L0_ffn_Wv, L0_ffn_bv, L0_ffn_Wo, L0_ffn_bo, L0_ffn_Wm, L0_ffn_bm, L0_ffn_W1, L0_ffn_bf1, L0_ffn_W2, L0_ffn_bf2):
    import jax
    import jax.numpy as jnp

    def _L0_tok_ref(x, ln_gamma, ln_beta, W, b):
        import jax, jax.numpy as jnp
        import numpy as np
        PATCH = 16
        HALF = PATCH // 2
        DIM = 192
        CH = 3
        PATCH_DIM = PATCH * PATCH * 5 * CH
        LN_EPS = 1e-05

        def _shift2d(x, t, l):
            H, W = (x.shape[-2], x.shape[-1])
            at, al = (abs(t), abs(l))
            xp = jnp.pad(x, ((0, 0), (0, 0), (at, at), (al, al)))
            return xp[:, :, at - t:at - t + H, al - l:al - l + W]
        p = PATCH
        shifts = ((1, -1, 1, -1), (-1, 1, -1, 1), (-1, 1, 1, -1), (1, -1, -1, 1))
        parts = [x] + [_shift2d(x, HALF * s[2], HALF * s[0]) for s in shifts]
        xc = jnp.concatenate(parts, axis=1)
        B, C5, H, Wd = xc.shape
        h, w = (H // p, Wd // p)
        patches = xc.reshape(B, C5, h, p, w, p)
        patches = patches.transpose(0, 2, 4, 3, 5, 1).reshape(B, h * w, p * p * C5)
        mu = patches.mean(axis=-1, keepdims=True)
        var = patches.var(axis=-1, keepdims=True)
        xn = (patches - mu) * jax.lax.rsqrt(var + LN_EPS) * ln_gamma + ln_beta
        return jnp.einsum('bnp,dp->bnd', xn, W) + b

    def _L0_attn_ref(x, Wq, bq, Wk, bk, Wv, bv, rel_table, Wpk, bpk, Wpq, bpq, Wo, bo):
        import math
        import jax, jax.numpy as jnp
        import numpy as np
        B, S, IN_DIM, EMB, H, MAX_LEN = (4, 128, 192, 192, 12, 128)
        D = EMB // H
        Bx, Sx, _ = x.shape

        def shape_heads(t):
            return t.reshape(Bx, Sx, H, D).transpose(0, 2, 1, 3)
        q = shape_heads(x @ Wq + bq)
        k = shape_heads(x @ Wk + bk)
        v = shape_heads(x @ Wv + bv)
        pos = jnp.arange(Sx)
        ids = jnp.clip(pos[:, None] - pos[None, :], -(MAX_LEN - 1), MAX_LEN - 1) + (MAX_LEN - 1)
        pos_k = (rel_table @ Wpk + bpk)[ids].reshape(Sx, Sx, H, D)
        pos_q = (rel_table @ Wpq + bpq)[ids].reshape(Sx, Sx, H, D)
        scores = jnp.einsum('bhid,bhjd->bhij', q, k)
        scores = scores + jnp.einsum('bhid,ijhd->bhij', q, pos_k)
        scores = scores + jnp.einsum('ijhd,bhjd->bhij', pos_q, k)
        scores = scores / math.sqrt(D * 3.0)
        attn = jax.nn.softmax(scores, axis=-1)
        out = jnp.einsum('bhij,bhjd->bhid', attn, v)
        out = out.transpose(0, 2, 1, 3).reshape(Bx, Sx, EMB)
        return out @ Wo + bo

    def _L0_ffn_ref(hidden_states, g1, b1, g2, b2, Wr, br, Wq, bq, Wk, bk, Wv, bv, Wo, bo, Wm, bm, W1, bf1, W2, bf2):
        import jax, jax.numpy as jnp
        import numpy as np
        B, L, D, H, F = (4, 512, 192, 12, 768)
        ROUTE_FRAC = 0.15
        LN_EPS = 1e-05

        def _ln(x, g, b):
            m = jnp.mean(x, axis=-1, keepdims=True)
            v = jnp.mean((x - m) ** 2, axis=-1, keepdims=True)
            return (x - m) * jax.lax.rsqrt(v + LN_EPS) * g + b
        b, l, d = hidden_states.shape
        dh = d // H
        normed = _ln(hidden_states, g1, b1)
        scores = jax.nn.sigmoid(jnp.einsum('bld,d->bl', normed, Wr) + br)
        k = max(1, int(round(ROUTE_FRAC * l)))
        _, idx = jax.lax.top_k(-scores, k)
        attn_mask = jnp.zeros((b, l), bool).at[jnp.arange(b)[:, None], idx].set(True)
        q = (normed @ Wq + bq).reshape(b, l, H, dh)
        kk = (normed @ Wk + bk).reshape(b, l, H, dh)
        v = (normed @ Wv + bv).reshape(b, l, H, dh)
        logits = jnp.einsum('blhd,bmhd->bhlm', q, kk) / jnp.sqrt(jnp.float32(dh))
        probs = jax.nn.softmax(logits, axis=-1)
        ctx = jnp.einsum('bhlm,bmhd->blhd', probs, v).reshape(b, l, d)
        attn_out = ctx @ Wo + bo
        w = scores / (jnp.sum(scores, axis=1, keepdims=True) + 1e-06)
        pooled = jnp.einsum('bl,bld->bd', w, normed)
        mix_out = (normed + scores[..., None] * pooled[:, None, :]) @ Wm + bm
        merged = jnp.where(attn_mask[..., None], attn_out, mix_out)
        h = hidden_states + merged
        n2 = _ln(h, g2, b2)
        ffn = jax.nn.gelu(n2 @ W1 + bf1, approximate=False) @ W2 + bf2
        return h + ffn
    h = _L0_tok_ref(x, L0_tok_ln_gamma, L0_tok_ln_beta, L0_tok_W, L0_tok_b)
    h = _layernorm(h + _L0_attn_ref(h, L0_attn_Wq, L0_attn_bq, L0_attn_Wk, L0_attn_bk, L0_attn_Wv, L0_attn_bv, L0_attn_rel_table, L0_attn_Wpk, L0_attn_bpk, L0_attn_Wpq, L0_attn_bpq, L0_attn_Wo, L0_attn_bo), axis=-1)
    h = _layernorm(h + _L0_ffn_ref(h, L0_ffn_g1, L0_ffn_b1, L0_ffn_g2, L0_ffn_b2, L0_ffn_Wr, L0_ffn_br, L0_ffn_Wq, L0_ffn_bq, L0_ffn_Wk, L0_ffn_bk, L0_ffn_Wv, L0_ffn_bv, L0_ffn_Wo, L0_ffn_bo, L0_ffn_Wm, L0_ffn_bm, L0_ffn_W1, L0_ffn_bf1, L0_ffn_W2, L0_ffn_bf2), axis=-1)
    return h

_drawn_inputs = setup_inputs


def setup_inputs(seed=0):
    import zlib

    import numpy as np

    out = dict(_drawn_inputs(seed))
    spreads = {'L0_tok_ln_gamma': (1.0, 0.2),
     'L0_tok_ln_beta': (0.0, 0.1),
     'L0_tok_b': (0.0, 0.1),
     'L0_attn_bq': (0.0, 0.404),
     'L0_attn_bk': (0.0, 0.468),
     'L0_attn_bv': (0.0, 0.1),
     'L0_attn_bpk': (0.0, 2.0),
     'L0_attn_bpq': (0.0, 0.52),
     'L0_attn_bo': (0.0, 0.1),
     'L0_ffn_g1': (1.0, 0.2),
     'L0_ffn_b1': (0.0, 0.427),
     'L0_ffn_g2': (1.0, 0.6),
     'L0_ffn_b2': (0.0, 0.8),
     'L0_ffn_bq': (0.0, 0.8),
     'L0_ffn_bk': (0.0, 2.0),
     'L0_ffn_bv': (0.0, 0.8),
     'L0_ffn_bo': (0.0, 1.113),
     'L0_ffn_bm': (0.0, 0.1),
     'L0_ffn_bf1': (0.0, 0.517),
     'L0_ffn_bf2': (0.0, 0.1)}
    factors = {'L0_ffn_Wq': 8.0, 'L0_ffn_Wk': 8.0, 'L0_ffn_Wv': 8.0, 'L0_ffn_Wo': 8.0}
    for name, (base, spread) in spreads.items():
        noise = np.random.default_rng([zlib.crc32(name.encode()), seed]).standard_normal(out[name].shape)
        drawn = base * np.exp(spread * noise) if base else spread * noise
        out[name] = jnp.asarray(drawn.astype(out[name].dtype))
    for name, factor in factors.items():
        out[name] = (out[name] * factor).astype(out[name].dtype)
    return out
```

```python
from contextlib import ExitStack

import concourse.bass as bass
from concourse import mybir

F32 = mybir.dt.float32
ALU = mybir.AluOpType
ACT = mybir.ActivationFunctionType
AX = mybir.AxisListType

P = 128
B = 64
GRID = 6
T = GRID * GRID
D = 192
HALF = D // 2
H = 12
DH = D // H
FF = 4 * D
CH = 3
PATCH = 16
PDIM = PATCH * PATCH * 5 * CH
EPS = 1e-5
NT = B * T // P
TPR = NT // GRID
TOK = B * T
CHUNK = TPR * P
REL = 2 * T - 1
WIN = T + 1
NB = 12
NQ = NB // 2 + 1
ROW = CH * NQ * B
QW = NQ * B
GQ = 3
HT_COLS = H * T
PAIRS = B // 2
NSEL = 5
SLOT = NSEL + 1
BIAS_ROWS = ["tok_b", "bv1", "bo1", "g1", "b1", "bv2", "bm", "bo2", "g2", "b2", "bf2"]
WCH = 24
WRAW = WCH + 6


def build(nc, x, wtok, gam, bet, watt, relt, wffn, w2, brow, col, bf1, wr, br, cst, lower, out):
    with ExitStack() as ctx:
        def sb(name, shape):
            return ctx.enter_context(nc.sbuf_tensor(name, shape, F32))

        def sem(name):
            return ctx.enter_context(nc.semaphore(name))

        ax = sb("arena_x", [P, NB * ROW])
        aqk = sb("arena_qk", [P, 6 * TOK])
        aht = sb("arena_ht", [HALF, 2 * TOK])
        nat = sb("nat", [P, NT, D])
        ann = sb("arena_nn", [P, NT * D])
        arg = sb("arena_ring", [P, 2 * ROW + 48])
        wat = sb("wat", [HALF, 6, 2, D])
        bdt = sb("bdt", [HALF, 2, 2, 6, REL])
        bias = sb("bias", [P, len(BIAS_ROWS), D])
        cs = sb("cs", [P, 2 * P + 6 + 2 + 2])
        colb = sb("colb", [HALF, 12])
        bf1s = sb("bf1s", [P, FF // P])
        wrs = sb("wrs", [HALF, 2])
        brs = sb("brs", [P, 1])
        st = sb("st", [P, 128])

        ident = cs[:, 0:P]
        ident2 = cs[:, P:2 * P]
        hmask = cs[0:HALF, 2 * P:2 * P + 6]
        emask = cs[0:HALF, 2 * P + 6:2 * P + 8]
        sidem = cs[:, 2 * P + 8:2 * P + 10]

        def brow_bc(name):
            return bias[:, BIAS_ROWS.index(name), :]

        xs = ax[:, :].rearrange("p (r c q b) -> p r c q b", r=NB, c=CH, q=NQ)
        wraw = aqk[:, 0:WRAW * D].rearrange("p (k o) -> p k o", o=D)
        o0 = WRAW * D
        wg = aqk[:, o0:o0 + WCH * (D + 1)].rearrange("p (a s c o) -> p a s c o", a=4, s=2, c=CH)
        wgf = aqk[:, o0:o0 + WCH * (D + 1)].rearrange("p (k o) -> p k o", o=D + 1)
        o0 += WCH * (D + 1)
        wgc = aqk[:, o0:o0 + 6 * D].rearrange("p (a c o) -> p a c o", a=2, c=CH)
        o0 += 6 * D
        esum = [aqk[:, o0 + 2 * k * QW:o0 + (2 * k + 1) * QW] for k in range(2)]
        usum = [aqk[:, o0 + (2 * k + 1) * QW:o0 + (2 * k + 2) * QW] for k in range(2)]
        side1 = aqk[:, o0 + 4 * QW:o0 + 5 * QW]
        assert o0 + 5 * QW <= 6 * TOK
        gams = sb("gams", [P, WRAW])
        bets = sb("bets", [P, WRAW])
        rsq = ann[:, 0:6 * QW].rearrange("p (s q) -> p s q", s=6)
        ssum = ann[:, 6 * QW:6 * QW + 2 * CHUNK].rearrange("p (s c) -> p s c", s=2)
        sq = arg[:, 0:2 * ROW].rearrange("p (s c q) -> p s c q", s=2, c=CH)
        swb = sb("swb", [P, D])
        cb = sb("cb", [P, D])
        red = sb("red", [P, 2, D])
        ones = sb("ones", [P, P])

        ht = aht[:, :].rearrange("p (m t) -> p m t", m=2)
        qt = aqk[0:HALF, 0:2 * TOK].rearrange("p (m t b) -> p m t b", m=2, t=T)
        ke = aqk[0:HALF, 2 * TOK:6 * TOK].rearrange("p (m e t b) -> p m e t b", m=2, e=2, t=T)
        cmat = ax[0:B, 0:T * HT_COLS].rearrange("p (i h j) -> p i h j", i=T, j=T)
        vz = ann[:, 4 * HT_COLS:4 * HT_COLS + 8 * D].rearrange("p (s e o) -> p s e o", s=4, e=2)
        cring = ann[:, 0:4 * HT_COLS].rearrange("p (s n c) -> p s n c", s=2, n=2)
        sring = ann[:, 4 * HT_COLS:7 * HT_COLS].rearrange("p (s c) -> p s c", s=3)
        ptr = arg[0:2 * T, 0:1200].rearrange("p (s k c) -> p s k c", s=2, k=6)
        vbd = arg[0:2 * T, 1200:1200 + 8 * D].rearrange("p (s n o) -> p s n o", s=2, n=4)
        ot = aht[:, :].rearrange("p (m t b) -> p m t b", m=2, t=T)
        relts = arg[0:HALF, 0:4 * REL].rearrange("p (v m r) -> p v m r", v=2, m=2)
        pks = arg[0:HALF, 4 * REL:8 * REL].rearrange("p (v m r) -> p v m r", v=2, m=2)
        mx = st[:, 64:100].rearrange("p (s h) -> p s h", s=3)
        rs = sb("rs", [P, 3, H])
        stats = sb("stats", [P, 6])
        mv = sb("mv", [P, TPR, 2])
        nhalf = sb("nhalf", [P, TPR])
        rst = sb("rst", [P, TPR])

        norm = ann[:, :].rearrange("p (n o) -> p n o", o=D)
        nt_ = ht
        kt = aqk[0:HALF, 2 * TOK:4 * TOK].rearrange("p (m t b) -> p m t b", m=2, t=T)
        ktf = aqk[0:HALF, 2 * TOK:4 * TOK].rearrange("p (m t) -> p m t", m=2)
        wf = aqk[0:HALF, 4 * TOK:4 * TOK + 2 * (5 * D + FF)].rearrange("p (m o) -> p m o", m=2)
        w2s = aqk[:, 4 * TOK + 2 * (5 * D + FF):6 * TOK].rearrange("p (k o) -> p k o", o=D)
        WQ, WK, WV, WO, WM, W1 = (k * D for k in range(6))
        vring = arg[:, 0:2 * TPR * D].rearrange("p (s n o) -> p s n o", s=2, n=TPR)
        less = aqk[:, 0:T * T].rearrange("p (t u) -> p t u", u=T)
        same = aqk[:, T * T:2 * T * T].rearrange("p (t u) -> p t u", u=T)
        lows = aqk[:, 2 * T * T:3 * T * T].rearrange("p (t u) -> p t u", u=T)
        qe = aqk[0:HALF, 0:2 * B * 32].rearrange("p (m b c) -> p m b c", m=2, c=32)
        o1 = 2 * TPR * D
        dring = arg[:, o1:o1 + 3 * SLOT * B].rearrange("p (s k b) -> p s k b", s=3, k=SLOT)
        vj = ax[0:T, 0:B * D].rearrange("p (b o) -> p b o", o=D)
        o2 = B * D
        gt = ax[0:HALF, o2:o2 + 2 * (SLOT + 1) * B].rearrange("p (m s b) -> p m s b", m=2, b=B)
        o2 += 2 * (SLOT + 1) * B
        qs = ax[0:HALF, o2:o2 + 2 * NSEL * B].rearrange("p (m s b) -> p m s b", m=2, b=B)
        o2 += 2 * NSEL * B
        s2 = ax[:, o2:o2 + PAIRS * T].rearrange("p (n j) -> p n j", j=T)
        o2 += PAIRS * T
        pt2 = ax[0:T, o2:o2 + 2 * 4 * P].rearrange("p (s n c) -> p s n c", s=2, n=4)
        assert o2 + 8 * P <= NB * ROW
        o2t = arg[0:HALF, 0:2 * NSEL * B].rearrange("p (m s b) -> p m s b", m=2, b=B)
        asel = arg[:, 640:640 + 3 * D].rearrange("p (s o) -> p s o", o=D)
        otmp = arg[0:HALF, 1216:1216 + 2 * 480].rearrange("p (s n c) -> p s n c", s=2, n=16)
        pm = arg[:, 2240:2240 + D]
        dtr = aqk[:, 0:9 * P].rearrange("p (s k c) -> p s k c", s=3, k=3)
        mrg = aqk[:, 9 * P:9 * P + 4 * TPR * D].rearrange("p (v n o) -> p v n o", v=4, n=TPR)
        hid = ax[:, 0:FF // P * TOK].rearrange("p (k t) -> p k t", t=TOK)
        lnb = sb("lnb", [P, 4, NT, 3])
        zt = sb("zt", [P, NT])
        zz = sb("zz", [P, 2, NT])
        sc = sb("sc", [P, T])
        rt = sb("rt", [P, T])
        oh = sb("oh", [P, SLOT, T])
        gsl = sb("gsl", [P, SLOT, NT])
        ohs = sb("ohs", [P, 3, T])
        own = sb("own", [P, 2, NT])
        nbr = sb("nbr", [P, 1])
        mx2 = sb("mx2", [P, 2, PAIRS])
        rsum = sb("rsum", [P, 2])

        bank = ctx.enter_context(nc.psum_tensor("bank", [P, 8, 512], F32))

        vd = nc.dram_tensor("v_scratch", [TOK, 2 * D], F32, kind="Internal").ap()
        v2d = nc.dram_tensor("v2_scratch", [TOK, D], F32, kind="Internal").ap()
        cd = nc.dram_tensor("c_scratch", [B, T, HT_COLS], F32, kind="Internal").ap()

        s_cst = sem("consts_in")
        s_w = [sem(f"wtok_in{k}") for k in range(5)]
        s_gb = sem("gamma_beta_in")
        s_x = [sem(f"x_in{k}") for k in range(7)]
        s_wat = sem("watt_in")
        s_rel = sem("rel_in")
        s_bias = sem("bias_in")
        pads_left = sem("pads_left")
        pads_right = sem("pads_right")
        ones_set = sem("ones_set")
        nhalf_set = sem("nhalf_set")
        wg_ready = sem("wg_ready")
        wc_ready = sem("wc_ready")
        wb_ready = sem("wb_ready")
        red_ready = sem("red_ready")
        swcb_ps = sem("swcb_ps")
        swb_ready = sem("swb_ready")
        sq_ready = sem("sq_ready")
        rsq_ready = sem("rsq_ready")
        eu_ready = sem("eu_ready")
        esum_set = sem("esum_set")
        ss_part = sem("window_squares_part")
        ss_ready = sem("window_squares_ready")
        tok_ps = sem("tok_ps")
        tstat = sem("tstat")
        tvar = sem("tvar")
        trstd = sem("trstd")
        tcent = sem("tcent")
        h_ready = sem("h_ready")
        htr_ps = sem("htr_ps")
        ht_ready = sem("ht_ready")
        pk_ps = sem("pk_ps")
        pk_sb = sem("pk_sb")
        bd_ready = sem("bd_ready")
        qk_ps = sem("qk_ps")
        q_ready = sem("q_ready")
        k_ready = sem("k_ready")
        v_ps = sem("v_ps")
        vz_ready = sem("vz_ready")
        vz_out = [sem(f"vz_out{k}") for k in range(4)]
        p2c_ps = sem("p2c_ps")
        p2c_act = sem("p2c_act")
        p2c_dve = sem("p2c_dve")
        c2p_ps = sem("c2p_ps")
        c_ready = sem("c_ready")
        c_out = sem("c_out")
        ring_zero = sem("ring_zero")
        sbank_zero = sem("sbank_zero")
        c_in = [sem("c_in0"), sem("c_in1")]
        v_in = [sem("v_in0"), sem("v_in1")]
        s_ps = sem("scores_ps")
        s_sum = sem("scores_summed")
        s_max = sem("scores_max")
        s_sub = sem("scores_centred")
        s_exp = sem("probs_exp")
        s_tot = sem("probs_total")
        s_inv = sem("probs_inv")
        s_nrm = sem("probs_ready")
        pt_ps = sem("probsT_ps")
        pt_sb = sem("probsT_ready")
        o_ps = sem("attn_ps")
        o_sb = sem("attn_ready")
        hb_ready = sem("hb_ready")
        wo_ps = sem("wo_ps")
        r_ready = sem("resid_ready")
        ln_mv = sem("ln_mv")
        ln_var = sem("ln_var")
        ln_rstd = sem("ln_rstd")
        h1_ready = sem("h1_ready")
        ln1_mv = sem("ln1_mv")
        ln1_var = sem("ln1_var")
        ln1_rstd = sem("ln1_rstd")
        n_cent = sem("normed_centred")
        n_gain = sem("normed_gain")
        n_ready = sem("normed_ready")
        n_ps = sem("normedT_ps")
        nt_ready = sem("normedT_ready")
        s_wf = sem("wffn_in")
        s_low = sem("lower_in")
        k2_ps = sem("k2_ps")
        k2_ready = sem("k2_ready")
        v2_ps = sem("v2_ps")
        v2_ready = sem("v2_ready")
        z_ready = sem("z_ready")
        v2_out = [sem("v2_out0"), sem("v2_out1")]
        vj_in = sem("vj_in")
        zz_ready = sem("zz_ready")
        z_ps = sem("z_ps")
        nbr_ready = sem("nbr_ready")
        z_exp = sem("z_exp")
        dve_step = sem("dve_step")
        oh_ready = sem("onehot_ready")
        d_ready = sem("gather_diag_ready")
        d_used = sem("gather_diag_used")
        g_ready = sem("gathered_ready")
        q2_ps = sem("q2_ps")
        q2_part = sem("q2_part")
        q2_sb = sem("q2_sb")
        qe_ready = sem("qe_ready")
        pm_ps = sem("pooled_ps")
        pm_ready = sem("pooled_ready")
        l2_ps = sem("logits_ps")
        l2_cent = sem("logits_centred")
        l2_exp = sem("logits_exp")
        l2_ready = sem("probs2_ready")
        t2_ps = sem("probs2T_ps")
        t2_ready = sem("probs2T_ready")
        c2_ps = sem("context_ps")
        c2_tmp = sem("context_masked")
        c2_ready = sem("context_ready")
        as_ps = sem("chosen_ps")
        as_ready = sem("chosen_ready")
        dt_ready = sem("scatter_diag_ready")
        mg_ps = sem("merge_ps")
        mg_bias = sem("merge_bias")
        mg_c = sem("merge_sum")
        h2_ready = sem("h2_ready")
        ln2_mv = sem("ln2_mv")
        ln2_var = sem("ln2_var")
        ln2_rstd = sem("ln2_rstd")
        n2_cent = sem("n2_centred")
        n2_gain = sem("n2_gain")
        n2_ready = sem("n2_ready")
        n2_ps = sem("n2T_ps")
        n2t_ready = sem("n2T_ready")
        res_part = sem("res_part")
        res_ready = sem("res_ready")
        f1_ps = sem("ffn1_ps")
        f1_ready = sem("ffn1_ready")
        f2_ps = sem("ffn2_ps")
        y_ready = sem("y_ready")
        ln3_mv = sem("ln3_mv")
        ln3_var = sem("ln3_var")
        ln3_rstd = sem("ln3_rstd")
        y_out = sem("y_ready_out")
        s_out = sem("s_out")

        block = ctx.enter_context(nc.Block())
        XCH = [(0, 1), (1, 3), (3, 5), (5, 7), (7, 9), (9, 11), (11, 12)]
        xv = xs

        def window(i):
            return [(a, 2 * i - 1 + a) for a in range(4) if 0 <= 2 * i - 1 + a < NB]

        def load_x(eng, k):
            r0, r1 = XCH[k]
            for h in range(2):
                eng.dma_start(xs[64 * h:64 * h + 64, r0:r1, :, 1 - h:NQ - h, :],
                              x[64 * h:64 * h + 64, r0:r1, :, :, :]).then_inc(s_x[k], 16)

        @block.sync
        def _(sp):
            sp.dma_start(gams[:, :], gam).then_inc(s_gb, 16)
            sp.dma_start(bets[:, :], bet).then_inc(s_gb, 16)

            def load_w(k):
                sp.dma_start(wraw[:, 6 * k:6 * k + 6, :], wtok[:, 6 * k:6 * k + 6, :]).then_inc(s_w[k], 16)

            for k in (1, 4, 2, 3, 0):
                load_w(k)
            for k in range(2, len(XCH)):
                load_x(sp, k)
            sp.dma_start(bias[:, :, :], brow.partition_broadcast(P)).then_inc(s_bias, 16)
            sp.dma_start(colb[:, :], col).then_inc(s_bias, 16)
            sp.dma_start(bf1s[:, :], bf1).then_inc(s_bias, 16)
            sp.dma_start(wrs[:, :], wr).then_inc(s_bias, 16)
            sp.dma_start(brs[:, :], br.to_broadcast([P, 1])).then_inc(s_bias, 16)
            sp.dma_start(wat[:, :, :, :], watt).then_inc(s_wat, 16)
            sp.wait_ge(rsq_ready, NB)
            sp.dma_start(relts, relt).then_inc(s_rel, 16)
            for ip in range(T // 2):
                sp.wait_ge(c_ready, 2 * ip + 2)
                sp.dma_start(cd[:, 2 * ip:2 * ip + 2, :],
                             ax[0:B, 2 * ip * HT_COLS:(2 * ip + 2) * HT_COLS].rearrange("p (i c) -> p i c", i=2)
                             ).then_inc(c_out, 16)
            sp.wait_ge(c_out, 16 * (T // 2))
            sp.wait_ge(ring_zero, 1)

            def load_c(g):
                if g >= 2:
                    sp.wait_ge(s_sum, 2 * g - 2)
                for ib in range(2):
                    sp.dma_start(cring[64 * ib:64 * ib + T, g % 2, :, :],
                                 cd[4 * g + ib:4 * g + ib + 3:2, :, :].rearrange("n i c -> i n c")
                                 ).then_inc(c_in[g % 2], 16)

            def load_v(g):
                if g >= 2:
                    sp.wait_ge(o_ps, 2 * g - 2)
                for e in range(2):
                    sp.dma_start(vbd[T * e:T * e + T, g % 2, :, :],
                                 vd.rearrange("(t b) o -> t b o", b=B)[:, 4 * g:4 * g + 4, e * D:(e + 1) * D]
                                 ).then_inc(v_in[g % 2], 16)

            load_c(0)
            for g in range(PAIRS // 2):
                if g + 1 < PAIRS // 2:
                    load_c(g + 1)
                if g == 0:
                    for k in range(4):
                        sp.wait_ge(vz_out[k], 16 * len(range(k, NT, 4)))
                load_v(g)
            sp.wait_ge(s_ps, PAIRS)
            sp.dma_start(wf, wffn).then_inc(s_wf, 16)
            sp.dma_start(w2s, w2).then_inc(s_wf, 16)
            sp.dma_start(lows, lower.partition_broadcast(P)).then_inc(s_low, 16)
            for i in range(GRID):
                sp.wait_ge(v2_ready, TPR * (i + 1))
                sp.dma_start(v2d[i * CHUNK:(i + 1) * CHUNK, :].rearrange("(n p) o -> p n o", p=P),
                             vring[:, i % 2, :, :]).then_inc(v2_out[i % 2], 16)
            sp.wait_ge(v2_out[0], 48)
            sp.wait_ge(v2_out[1], 48)
            for k in range(4):
                sp.dma_start(vj[:, 16 * k:16 * k + 16, :],
                             v2d.rearrange("(t b) o -> t b o", b=B)[:, 16 * k:16 * k + 16, :]).then_inc(vj_in, 16)
            for n in range(NT):
                sp.wait_ge(y_out, n + 1)
                sp.dma_start(out[:, 2 * n:2 * n + 2, :].rearrange("b t o -> t b o"), nat[:, n, :]).then_inc(s_out, 16)
            sp.wait_ge(s_out, 16 * NT)

        @block.tensor
        def _(pe):
            def tok_product(n, a, r, first, last):
                k = 0
                for s in range(2):
                    for c in range(CH):
                        q0 = 2 * (n % TPR) + s
                        pe.matmul(bank[:, n % (2 * TPR), 0:D + 1], xs[:, r, c, q0:q0 + 2, :], wg[:, a, s, c, :],
                                  start=(first and k == 0), stop=(last and k == 2 * CH - 1))
                        k += 1

            def tok_squares(i):
                pe.wait_ge(ss_ready, i + 1)
                for n in range(TPR * i, TPR * i + TPR):
                    pe.matmul(bank[:, n % (2 * TPR), D + 8:D + 9], ssum[:, i % 2, n % TPR * P:n % TPR * P + P], ones[:, 0:1],
                              start=True, stop=True).then_inc(tok_ps, 1)

            def tok_row(i):
                rows = window(i)
                for k in range(7):
                    if XCH[k][0] <= rows[-1][1] < XCH[k][1]:
                        pe.wait_ge(s_x[k], 32)
                if i == 0:
                    for a, r in rows:
                        pe.wait_ge(s_x[(r + 1) // 2], 32)
                        pe.wait_ge(wg_ready, {1: 4, 2: 6, 3: 7}[a])
                        for n in range(TPR):
                            tok_product(n, a, r, a == 1, a == 3)
                else:
                    pe.wait_ge(wg_ready, 8)
                    for n in range(TPR * i, TPR * i + TPR):
                        if n >= 2 * TPR:
                            pe.wait_ge(h_ready, n - 2 * TPR + 1)
                        for a, r in rows:
                            tok_product(n, a, r, (a, r) == rows[0], (a, r) == rows[-1])
                        if n == TPR + 1:
                            pe.wait_ge(red_ready, 2)
                            for k in range(2):
                                mm = pe.matmul(bank[:, 6, k * D:(k + 1) * D], ones[:, :], red[:, k, :], start=True, stop=True)
                            mm.then_inc(swcb_ps, 1)
                tok_squares(i)

            def h_turn(n):
                pe.wait_ge(h_ready, n + 1)
                if n >= 2:
                    pe.wait_ge(ht_ready, n - 1)
                for m in range(2):
                    mm = pe.transpose(bank[0:HALF, 6 + n % 2, m * P:(m + 1) * P],
                                      nat[:, n, m * HALF:(m + 1) * HALF], ident)
                mm.then_inc(htr_ps, 1)

            pe.wait_ge(ones_set, 1)
            pe.wait_ge(pads_left, 1)
            pe.wait_ge(pads_right, 1)
            for i in range(GRID):
                tok_row(i)
                if i == 1:
                    pe.wait_ge(s_cst, 16)
                    pe.wait_ge(swb_ready, 2)
                if i:
                    for n in range(TPR * (i - 1), TPR * i):
                        h_turn(n)
            for jj in range(TPR):
                h_turn(TPR * (GRID - 1) + jj)

            pe.wait_ge(s_wat, 16)
            pe.wait_ge(s_rel, 16)
            pe.wait_ge(h_ready, NT)
            for v in range(2):
                for m in range(2):
                    for kk in range(2):
                        mm = pe.matmul(bank[0:HALF, 0, (2 * v + m) * REL:(2 * v + m + 1) * REL],
                                       wat[:, 4 + v, kk, m * HALF:(m + 1) * HALF], relts[:, v, kk, :],
                                       start=(kk == 0), stop=(kk == 1))
            mm.then_inc(pk_ps, 1)

            pe.wait_ge(pk_sb, 1)
            for i in range(GRID):
                pe.wait_ge(ht_ready, TPR * (i + 1))
                for which in range(2):
                    for m in range(2):
                        u = 4 * i + 2 * which + m
                        if u >= 6:
                            o = u - 6
                            if o % 4 < 2:
                                pe.wait_ge(q_ready, 2 * (o // 4) + o % 4 + 1)
                            else:
                                pe.wait_ge(k_ready, 2 * (2 * (o // 4) + o % 4 - 2) + 2)
                        for kk in range(2):
                            mm = pe.matmul(bank[0:HALF, u % 6, 0:CHUNK], wat[:, which, kk, m * HALF:(m + 1) * HALF],
                                           ht[:, kk, i * CHUNK:(i + 1) * CHUNK], start=(kk == 0), stop=(kk == 1))
                        mm.then_inc(qk_ps, 1)

            pe.wait_ge(q_ready, 2 * GRID)
            pe.wait_ge(k_ready, 4 * GRID)
            pe.wait_ge(bd_ready, 4)
            for jp in range(T // 2):
                if jp >= 4:
                    pe.wait_ge(p2c_act, jp - 3)
                    pe.wait_ge(p2c_dve, jp - 3)
                dst = bank[:, jp % 4, 0:H * WIN].rearrange("p (g m e w) -> p g m e w", g=GQ, m=2, e=2)
                for m in range(2):
                    for e in range(2):
                        mm = pe.matmul(dst[:, :, m, e, :],
                                       ke[:, m, e, 2 * jp:2 * jp + 2, :].rearrange("p t b -> p (t b)"),
                                       bdt[:, 1, m, e:6:2, T - 2 - 2 * jp:T - 2 - 2 * jp + WIN],
                                       start=True, stop=True)
                mm.then_inc(p2c_ps, 1)
            for ip in range(T // 2):
                u = ip + T // 2
                if ip < 4:
                    pe.wait_ge(p2c_act, u - 3)
                    pe.wait_ge(p2c_dve, u - 3)
                else:
                    pe.wait_ge(c_ready, 2 * (ip - 3))
                dst = bank[:, u % 4, 0:H * WIN].rearrange("p (g m e w) -> p g m e w", g=GQ, m=2, e=2)
                for m in range(2):
                    mm = pe.matmul(dst[:, :, m, :, :],
                                   qt[:, m, 2 * ip:2 * ip + 2, :].rearrange("p t b -> p (t b)"),
                                   bdt[:, 0, m, :, T - 2 - 2 * ip:T - 2 - 2 * ip + WIN].rearrange("p (g e) w -> p g e w", e=2),
                                   start=True, stop=True)
                mm.then_inc(c2p_ps, 1)

            for n in range(NT):
                if n >= 2:
                    pe.wait_ge(vz_ready, n - 1)
                for kk in range(2):
                    mm = pe.matmul(bank[:, 6 + n % 2, 0:D], ht[:, kk, n * P:(n + 1) * P], wat[:, 2, kk, :],
                                   start=(kk == 0), stop=(kk == 1))
                mm.then_inc(v_ps, 1)

            def scores(n):
                if n:
                    pe.wait_ge(s_sum, n)
                for m in range(2):
                    for ib in range(2):
                        for g in range(GQ):
                            mm = pe.matmul(bank[64 * ib:64 * ib + T, g, m * 2 * T:(m + 1) * 2 * T],
                                           qt[32 * g:32 * g + 32, m, :, 2 * n + ib],
                                           ke[32 * g:32 * g + 32, m, :, :, 2 * n + ib], start=True, stop=True)
                mm.then_inc(s_ps, 1)

            def turn(n):
                pe.wait_ge(s_nrm, n + 1)
                if n >= 2:
                    pe.wait_ge(pt_sb, n - 1)
                for k in range(6):
                    mm = pe.transpose(bank[0:2 * T, 3 + 2 * (n % 2) + k // 3, (k % 3) * 100:(k % 3) * 100 + 100],
                                      sring[0:100, n % 3, k * 2 * T:(k + 1) * 2 * T], ident[0:100, 0:100])
                mm.then_inc(pt_ps, 1)

            def mix(n):
                pe.wait_ge(pt_sb, n + 1)
                pe.wait_ge(v_in[n // 2 % 2], 32 * (n // 4 + 1))
                if n:
                    pe.wait_ge(o_sb, n)
                for ib in range(2):
                    for m in range(2):
                        for g in range(GQ):
                            mm = pe.matmul(bank[32 * g:32 * g + 32, 7, (2 * m + ib) * T:(2 * m + ib + 1) * T],
                                           vbd[:, n // 2 % 2, 2 * (n % 2) + ib, m * HALF + 32 * g:m * HALF + 32 * g + 32],
                                           ptr[:, n % 2, 2 * g + m, 64 * ib:64 * ib + T], start=True, stop=True)
                mm.then_inc(o_ps, 1)

            pe.wait_ge(sbank_zero, 1)
            pe.wait_ge(c_ready, T)
            for n in range(PAIRS + 3):
                if n < PAIRS:
                    scores(n)
                if 0 <= n - 2 < PAIRS:
                    turn(n - 2)
                if n >= 3:
                    mix(n - 3)

            pe.wait_ge(o_sb, PAIRS)
            for n in range(NT):
                if n >= 6:
                    pe.wait_ge(r_ready, n - 5)
                for m in range(2):
                    mm = pe.matmul(bank[:, n % 6, 0:D], ot[:, m, 2 * n:2 * n + 2, :].rearrange("p t b -> p (t b)"),
                                   wat[:, 3, m, :], start=(m == 0), stop=(m == 1))
                mm.then_inc(wo_ps, 1)

            pe.wait_ge(s_wf, 32)
            for i in range(GRID):
                for n in range(TPR * i, TPR * i + TPR):
                    pe.wait_ge(n_ready, n + 1)
                    if n >= 2:
                        pe.wait_ge(nt_ready, n - 1)
                    for m in range(2):
                        mm = pe.transpose(bank[0:HALF, 6 + n % 2, m * P:(m + 1) * P],
                                          norm[:, n, m * HALF:(m + 1) * HALF], ident)
                    mm.then_inc(n_ps, 1)
                pe.wait_ge(nt_ready, TPR * (i + 1))
                if i == 0:
                    pe.wait_ge(r_ready, NT)
                for m in range(2):
                    u = 2 * i + m
                    if u >= 4:
                        pe.wait_ge(k2_ready, u - 3)
                    for kk in range(2):
                        mm = pe.matmul(bank[0:HALF, u % 4, 0:CHUNK], wf[:, kk, WK + m * HALF:WK + (m + 1) * HALF],
                                       nt_[:, kk, i * CHUNK:(i + 1) * CHUNK], start=(kk == 0), stop=(kk == 1))
                    mm.then_inc(k2_ps, 1)
                for n in range(TPR * i, TPR * i + TPR):
                    if n >= 2:
                        pe.wait_ge(v2_ready, n - 1)
                    for kk in range(2):
                        pe.matmul(bank[:, 4 + n % 2, 0:D], nt_[:, kk, n * P:(n + 1) * P], wf[:, kk, WV:WV + D],
                                  start=(kk == 0), stop=(kk == 1))
                    for kk in range(2):
                        mm = pe.matmul(bank[:, 4 + n % 2, D:D + 1], nt_[:, kk, n * P:(n + 1) * P], wrs[:, kk:kk + 1],
                                       start=(kk == 0), stop=(kk == 1))
                    mm.then_inc(v2_ps, 1)

            pe.wait_ge(zz_ready, 1)
            pe.wait_ge(k2_ready, 2 * GRID)
            pe.matmul(bank[:, 0, 0:T], ident2, zz[:, :, :].rearrange("p e n -> p (e n)"), start=True, stop=True).then_inc(z_ps, 1)
            for n in range(NT):
                pe.wait_ge(d_ready, n + 1)
                for m in range(2):
                    mm = pe.matmul(bank[0:HALF, 1 + m, 0:SLOT * B], norm[:, n, m * HALF:(m + 1) * HALF],
                                   dring[:, n % 3, :, :].rearrange("p k b -> p (k b)"), start=(n == 0), stop=(n == NT - 1))
                mm.then_inc(d_used, 1)
            pe.wait_ge(g_ready, 1)
            for m in range(2):
                for kk in range(2):
                    mm = pe.matmul(bank[0:HALF, 3 + 3 * m, 0:NSEL * B], wf[:, kk, WQ + m * HALF:WQ + (m + 1) * HALF],
                                   gt[:, kk, 0:NSEL, :].rearrange("p s b -> p (s b)"), start=(kk == 0), stop=(kk == 1))
            mm.then_inc(q2_ps, 1)
            pe.wait_ge(v2_ready, NT)
            for kk in range(2):
                mm = pe.matmul(bank[:, 5, 0:D], gt[:, kk, NSEL:NSEL + 2, :].rearrange("p s b -> p (s b)"),
                               wf[:, kk, WM:WM + D], start=(kk == 0), stop=(kk == 1))
            mm.then_inc(pm_ps, 1)

            pe.wait_ge(qe_ready, 6)
            pe.wait_ge(z_exp, 1)
            for n in range(PAIRS):
                for ib in range(2):
                    for m in range(2):
                        q0 = 32 * (2 * ib + m)
                        mm = pe.matmul(bank[q0:q0 + 32, n // 12, n % 12 * T:n % 12 * T + T], qe[:, m, 2 * n + ib, :],
                                       kt[:, m, :, 2 * n + ib], start=True, stop=True)
                if n % 12 == 11 or n == PAIRS - 1:
                    mm.then_inc(l2_ps, 1)

            def turn2(k):
                pe.wait_ge(l2_ready, k // 3 + 1)
                if k >= 2:
                    pe.wait_ge(t2_ready, k - 1)
                for n in range(4):
                    mm = pe.transpose(bank[0:T, 3 + k % 2, n * P:(n + 1) * P], s2[:, 4 * k + n, :], ident)
                mm.then_inc(t2_ps, 1)

            def context(k):
                pe.wait_ge(t2_ready, k + 1)
                if k >= 2:
                    pe.wait_ge(c2_tmp, k - 1)
                for n in range(4):
                    for ib in range(2):
                        for m in range(2):
                            c0 = (8 * m + 2 * n + ib) * 32
                            q0 = 32 * (2 * ib + m)
                            mm = pe.matmul(bank[0:HALF, 6 + k % 2, c0:c0 + 32], vj[:, 8 * k + 2 * n + ib, m * HALF:(m + 1) * HALF],
                                           pt2[:, k % 2, n, q0:q0 + 32], start=True, stop=True)
                mm.then_inc(c2_ps, 1)

            pe.wait_ge(vj_in, 64)
            for k in range(PAIRS // 4 + 1):
                if k < PAIRS // 4:
                    turn2(k)
                if k:
                    context(k - 1)
            pe.wait_ge(c2_ready, PAIRS // 4)
            pe.wait_ge(pm_ready, 1)
            for k in range(3):
                rows = P if k < 2 else B
                for m in range(2):
                    mm = pe.matmul(bank[0:rows, 3 + k, 0:D], o2t[:, m, :, :].rearrange("p s b -> p (s b)")[:, k * P:k * P + rows],
                                   wf[:, m, WO:WO + D], start=(m == 0), stop=(m == 1))
                mm.then_inc(as_ps, 1)

            def merge(n):
                pe.wait_ge(dt_ready, n + 1)
                if n >= 3:
                    pe.wait_ge(mg_c, n - 2)
                for kk in range(2):
                    pe.matmul(bank[:, n % 3, 0:D], nt_[:, kk, n * P:(n + 1) * P], wf[:, kk, WM:WM + D],
                              start=(kk == 0), stop=(kk == 1))
                for k in range(3):
                    mm = pe.matmul(bank[:, n % 3, D:2 * D], dtr[:, n % 3, k, :], asel[:, k, :], start=(k == 0), stop=(k == 2))
                mm.then_inc(mg_ps, 1)

            def n2_turn(n):
                pe.wait_ge(n2_ready, n + 1)
                for m in range(2):
                    mm = pe.transpose(bank[0:HALF, 6, m * P:(m + 1) * P],
                                      mrg[:, 2 + n // TPR % 2, n % TPR, m * HALF:(m + 1) * HALF], ident)
                mm.then_inc(n2_ps, 1)
                pe.wait_ge(n2t_ready, n + 1)

            def ffn1(i):
                for k in range(FF // P):
                    u = 6 * i + k
                    if u >= 3:
                        pe.wait_ge(f1_ready, u - 2)
                    for kk in range(2):
                        mm = pe.matmul(bank[:, 3 + u % 3, 0:CHUNK], wf[:, kk, W1 + k * P:W1 + (k + 1) * P],
                                       nt_[:, kk, i * CHUNK:(i + 1) * CHUNK], start=(kk == 0), stop=(kk == 1))
                    mm.then_inc(f1_ps, 1)

            def ffn2(n):
                pe.wait_ge(f1_ready, 6 * (n // TPR + 1))
                if n:
                    pe.wait_ge(y_ready, n)
                for k in range(FF // P):
                    mm = pe.matmul(bank[:, 7, 0:D], hid[:, k, n * P:(n + 1) * P], w2s[:, k, :],
                                   start=(k == 0), stop=(k == FF // P - 1))
                mm.then_inc(f2_ps, 1)

            pe.wait_ge(as_ready, 4)
            for i in range(GRID + 2):
                if i < GRID:
                    for n in range(TPR * i, TPR * i + TPR):
                        merge(n)
                if i >= 2:
                    for n in range(TPR * (i - 2), TPR * (i - 1)):
                        ffn2(n)
                if 1 <= i <= GRID:
                    for n in range(TPR * (i - 1), TPR * i):
                        n2_turn(n)
                    ffn1(i - 1)

        @block.vector
        def _(dve):
            dve.memset(xs[0:64, :, :, 0, :].rearrange("p r c b -> p (r c) b"), 0.0).then_inc(pads_left, 1)
            dve.memset(wgf[:, :, D:D + 1], 1.0).then_inc(wc_ready, 1)
            dve.wait_ge(wc_ready, 1)
            dve.memset(wg[0:64, 1:3, 1, :, D:D + 1], 2.0).then_inc(wg_ready, 1)
            dve.memset(wg[64:128, 1:3, 0, :, D:D + 1], 2.0).then_inc(wg_ready, 1)
            dve.wait_ge(s_gb, 32)

            def gained(k):
                dve.wait_ge(s_w[k], 16)
                scale = gams[:, 6 * k:6 * k + 6].unsqueeze(2).to_broadcast([P, 6, D])
                dst = wgf[:, 6 * k:6 * k + 6, 0:D] if k < 4 else wgc.rearrange("p a c o -> p (a c) o")
                return dve.tensor_tensor(dst, wraw[:, 6 * k:6 * k + 6, :], scale, ALU.mult)

            def centre_in(a):
                s0, s1 = wg[64:128, 1 + a, 0, :, 0:D], wg[0:64, 1 + a, 1, :, 0:D]
                dve.tensor_tensor(s0, s0, wgc[64:128, a, :, :], ALU.add).then_inc(wg_ready, 1)
                dve.tensor_tensor(s1, s1, wgc[0:64, a, :, :], ALU.add).then_inc(wg_ready, 1)

            gained(1).then_inc(wc_ready, 1)
            gained(4).then_inc(wc_ready, 1)
            dve.wait_ge(wc_ready, 3)
            centre_in(0)
            gained(2).then_inc(wc_ready, 1)
            dve.wait_ge(wc_ready, 4)
            centre_in(1)
            gained(3).then_inc(wg_ready, 1)
            gained(0).then_inc(wg_ready, 1)

            def channel_sum(r):
                dve.wait_ge(sq_ready, r + 1)
                dve.tensor_reduce(rsq[:, r % 6, :], sq[:, r % 2, :, :].rearrange("p c q -> p q c"), AX.X,
                                  ALU.add).then_inc(rsq_ready, 1)

            def window_squares(i):
                dve.wait_ge(eu_ready, i + 1)
                if i >= 2:
                    dve.wait_ge(tok_ps, TPR * (i - 1))
                dve.scalar_tensor_tensor(side1, esum[i % 2], sidem[:, 1:2], usum[i % 2], ALU.mult, ALU.add).then_inc(ss_part, 1)
                dve.scalar_tensor_tensor(esum[i % 2], esum[i % 2], sidem[:, 0:1], usum[i % 2], ALU.mult,
                                         ALU.add).then_inc(ss_part, 1)
                dve.wait_ge(ss_part, 2 * i + 2)
                dve.tensor_tensor(ssum[:, i % 2, :], side1[:, 0:CHUNK], esum[i % 2][:, B:B + CHUNK], ALU.add).then_inc(ss_ready, 1)

            def tok_out(i):
                b0 = TPR * (i % 2)
                raw = bank[:, b0:b0 + TPR, :]
                dve.wait_ge(tok_ps, TPR * (i + 1))
                neg, e2, msq, var = (st[:, TPR * k:TPR * k + TPR] for k in range(4))
                dve.tensor_scalar(neg, raw[:, :, D], -1.0 / PDIM, None, ALU.mult).then_inc(tstat, 1)
                dve.tensor_scalar(e2, raw[:, :, D + 8], 1.0 / PDIM, EPS, ALU.mult, ALU.add).then_inc(tstat, 1)
                dve.wait_ge(tstat, 3 * i + 2)
                dve.tensor_tensor(msq, neg, neg, ALU.mult).then_inc(tstat, 1)
                dve.wait_ge(tstat, 3 * i + 3)
                dve.tensor_tensor(var, e2, msq, ALU.subtract).then_inc(tvar, 1)
                for jj in range(TPR):
                    n = TPR * i + jj
                    dve.scalar_tensor_tensor(nat[:, n, :], swb[:, :], st[:, jj:jj + 1], raw[:, jj, 0:D],
                                             ALU.mult, ALU.add).then_inc(tcent, 1)
                dve.wait_ge(trstd, i + 1)
                for jj in range(TPR):
                    n = TPR * i + jj
                    dve.wait_ge(tcent, n + 1)
                    dve.scalar_tensor_tensor(nat[:, n, :], nat[:, n, :], rst[:, jj:jj + 1], cb[:, :],
                                             ALU.mult, ALU.add).then_inc(h_ready, 1)

            for r in range(3):
                channel_sum(r)
            dve.wait_ge(s_cst, 16)
            window_squares(0)
            dve.wait_ge(wg_ready, 8)
            dve.tensor_reduce(red[:, 0, :], wgf[:, :, 0:D].rearrange("p k o -> p o k"), AX.X, ALU.add).then_inc(red_ready, 1)
            for r in range(3, 5):
                channel_sum(r)
            dve.wait_ge(wb_ready, 1)
            dve.tensor_reduce(red[:, 1, :], wraw.rearrange("p k o -> p o k"), AX.X, ALU.add).then_inc(red_ready, 1)
            window_squares(1)
            dve.wait_ge(swcb_ps, 1)
            dve.wait_ge(s_bias, 80)
            dve.tensor_copy(swb[:, :], bank[:, 6, 0:D]).then_inc(swb_ready, 1)
            dve.tensor_tensor(cb[:, :], bank[:, 6, D:2 * D], brow_bc("tok_b"), ALU.add).then_inc(swb_ready, 1)
            dve.wait_ge(swb_ready, 2)
            for i in range(GRID):
                if i:
                    for r in (2 * i + 3, 2 * i + 4):
                        if r < NB:
                            if r >= 6:
                                dve.wait_ge(eu_ready, (r - 6) // 2 + 1 + (r % 2))
                            channel_sum(r)
                    if i + 1 < GRID:
                        window_squares(i + 1)
                tok_out(i)

            dve.wait_ge(pk_ps, 1)
            for v in range(2):
                for m in range(2):
                    ins = dve.tensor_scalar(pks[:, v, m, :], bank[0:HALF, 0, (2 * v + m) * REL:(2 * v + m + 1) * REL],
                                            colb[:, 4 + 2 * v + m:5 + 2 * v + m], None, ALU.add)
            ins.then_inc(pk_sb, 1)
            dve.wait_ge(pk_sb, 1)
            for v in range(2):
                for m in range(2):
                    dve.tensor_tensor(bdt[:, v, m, :, :],
                                      pks[:, v, m, :].unsqueeze(1).to_broadcast([HALF, 6, REL]),
                                      hmask.unsqueeze(2).to_broadcast([HALF, 6, REL]), ALU.mult).then_inc(bd_ready, 1)
            dve.wait_ge(tok_ps, NT)
            dve.memset(ann[:, :], 0.0).then_inc(ring_zero, 1)
            dve.wait_ge(ring_zero, 1)
            for i in range(GRID):
                for m in range(2):
                    dve.wait_ge(qk_ps, 4 * i + 3 + m)
                    for e in range(2):
                        dve.tensor_scalar(ke[:, m, e, GRID * i:GRID * i + GRID, :],
                                          bank[0:HALF, (4 * i + 2 + m) % 6, 0:CHUNK].rearrange("p (t b) -> p t b", b=B),
                                          colb[:, 2 + m:3 + m], emask[:, e:e + 1], ALU.add, ALU.mult).then_inc(k_ready, 1)

            def win(u, par, flip):
                w = bank[64 * par:64 * par + 64, u % 4, 0:H * WIN].rearrange("p (h w) -> p h w", w=WIN)
                return w[:, :, 1 - par:1 - par + T]

            for jp in range(T // 2):
                dve.wait_ge(p2c_ps, jp + 1)
                dve.tensor_copy(cmat[:, :, :, 2 * jp + 1].rearrange("p i h -> p h i"), win(jp, 1, 0)).then_inc(p2c_dve, 1)
            dve.wait_ge(p2c_dve, T // 2)
            dve.wait_ge(p2c_act, T // 2)
            for ip in range(T // 2):
                dve.wait_ge(c2p_ps, ip + 1)
                for par in range(2):
                    dst = cmat[:, 2 * ip + par, :, :]
                    dve.tensor_tensor(dst, win(ip + T // 2, par, 0), dst, ALU.add).then_inc(c_ready, 1)
            dve.wait_ge(c_ready, T)
            dve.memset(bank[:, 0:3, 0:4 * T], 0.0).then_inc(sbank_zero, 1)
            for n in range(NT):
                dve.wait_ge(v_ps, n + 1)
                if n >= 4:
                    dve.wait_ge(vz_out[n % 4], 16 * (n // 4))
                dst = bass.AP(tensor=vz.tensor, offset=vz[:, n % 4, :, :].offset,
                              ap=[list(vz.ap[0]), [2 * DH, 6], [D + DH, 2], [1, DH]])
                dve.tensor_tensor(dst, bank[:, 6 + n % 2, 0:D].rearrange("p (g e d) -> p g e d", g=6, e=2),
                                  brow_bc("bv1").rearrange("p (g e d) -> p g e d", g=6, e=2), ALU.add).then_inc(vz_ready, 1)
            for k in range(4):
                dve.wait_ge(vz_out[k], 16 * len(range(k, NT, 4)))

            def v3(t):
                return t.rearrange("p (h j) -> p h j", j=T)

            def total(n):
                dve.wait_ge(s_exp, n + 1)
                dve.tensor_reduce(rs[0:100, n % 3, :], v3(sring[0:100, n % 3, :]), AX.X, ALU.add).then_inc(s_tot, 1)
                dve.wait_ge(s_tot, n + 1)
                dve.reciprocal(rs[0:100, n % 3, :], rs[0:100, n % 3, :]).then_inc(s_inv, 1)

            for n in range(PAIRS):
                dve.wait_ge(s_ps, n + 1)
                dve.wait_ge(c_in[n // 2 % 2], 32 * (n // 4 + 1))
                if n >= 3:
                    dve.wait_ge(pt_ps, n - 2)
                dve.tensor_tensor(sring[0:100, n % 3, :].rearrange("p (g c) -> p g c", g=GQ), bank[0:100, 0:GQ, 0:4 * T],
                                  cring[0:100, n // 2 % 2, n % 2, :].rearrange("p (g c) -> p g c", g=GQ),
                                  ALU.add).then_inc(s_sum, 1)
                dve.wait_ge(s_sum, n + 1)
                dve.tensor_reduce(mx[0:100, n % 3, :], v3(sring[0:100, n % 3, :]), AX.X, ALU.max).then_inc(s_max, 1)
                if n:
                    total(n - 1)
            total(PAIRS - 1)

            steps = [0]

            def step(ins):
                steps[0] += 1
                ins.then_inc(dve_step, 1)

            def settle():
                dve.wait_ge(dve_step, steps[0])

            def moments(k, src, n, ready):
                step(dve.bn_stats(stats[:, :], src))
                settle()
                dve.bn_aggr(lnb[:, k, n, 0:2], stats[:, :]).then_inc(ready, 1)

            def add_eps(k, i, mv_ready, var_ready):
                dve.wait_ge(mv_ready, TPR * (i + 1))
                v = lnb[:, k, TPR * i:TPR * i + TPR, 1]
                dve.tensor_scalar(v, v, EPS, None, ALU.add).then_inc(var_ready, 1)

            def centre(k, dst, src, n):
                return dve.tensor_scalar(dst, src, lnb[:, k, n, 0:1], lnb[:, k, n, 2:3], ALU.subtract, ALU.mult)

            def resid(i):
                for n in range(TPR * i, TPR * i + TPR):
                    dve.wait_ge(wo_ps, n + 1)
                    dve.wait_ge(hb_ready, n + 1)
                    dve.tensor_tensor(nat[:, n, :], bank[:, n % 6, 0:D], nat[:, n, :], ALU.add).then_inc(r_ready, 1)
                    dve.wait_ge(r_ready, n + 1)
                    if n:
                        dve.wait_ge(ln_mv, n)
                    moments(0, nat[:, n, :], n, ln_mv)
                add_eps(0, i, ln_mv, ln_var)

            def h1_norm(i):
                dve.wait_ge(ln_rstd, i + 1)
                for n in range(TPR * i, TPR * i + TPR):
                    centre(0, nat[:, n, :], nat[:, n, :], n).then_inc(h1_ready, 1)
                for n in range(TPR * i, TPR * i + TPR):
                    dve.wait_ge(h1_ready, n + 1)
                    moments(1, nat[:, n, :], n, ln1_mv)
                    dve.wait_ge(ln1_mv, n + 1)
                add_eps(1, i, ln1_mv, ln1_var)

            def n_norm(i):
                dve.wait_ge(ln1_rstd, i + 1)
                for n in range(TPR * i, TPR * i + TPR):
                    centre(1, norm[:, n, :], nat[:, n, :], n).then_inc(n_cent, 1)

            dve.wait_ge(pt_ps, PAIRS)
            for i in range(GRID + 2):
                if i < GRID:
                    resid(i)
                if 1 <= i <= GRID:
                    dve.wait_ge(ln_mv, TPR * min(i + 1, GRID))
                    h1_norm(i - 1)
                if i >= 2:
                    n_norm(i - 2)
            dve.tensor_scalar(nbr[:, :], brs[:, :], -1.0, None, ALU.mult).then_inc(nbr_ready, 1)
            for n in range(NT):
                i = n // TPR
                dve.wait_ge(v2_ps, n + 1)
                if n % TPR == 0 and i >= 2:
                    dve.wait_ge(v2_out[i % 2], 16 * (i // 2))
                dve.tensor_copy(zt[:, n:n + 1], bank[:, 4 + n % 2, D:D + 1]).then_inc(z_ready, 1)
                dve.tensor_tensor(vring[:, i % 2, n % TPR, :], bank[:, 4 + n % 2, 0:D], brow_bc("bv2"), ALU.add).then_inc(v2_ready, 1)

            dve.wait_ge(z_ready, NT)
            step(dve.tensor_scalar(zz[:, 0, :], zt[:, :], sidem[:, 0:1], None, ALU.mult))
            dve.tensor_scalar(zz[:, 1, :], zt[:, :], sidem[:, 1:2], None, ALU.mult).then_inc(dve_step, 1)
            steps[0] += 1
            settle()
            dve.tensor_copy(zt[:, :], zt[:, :]).then_inc(zz_ready, 1)
            dve.wait_ge(z_exp, 1)
            step(dve.tensor_scalar(rt[:, :], rt[:, :], 1.0, None, ALU.add))
            settle()
            step(dve.reciprocal(sc[:, :].rearrange("p (n e) -> p e n", e=2), rt[:, :].rearrange("p (e n) -> p e n", e=2)))
            settle()
            inner = sc[:, :].unsqueeze(1).to_broadcast([P, T, T])
            outer = sc[:, :].unsqueeze(2).to_broadcast([P, T, T])
            step(dve.tensor_tensor(less, inner, outer, ALU.is_lt))
            step(dve.tensor_tensor(same, inner, outer, ALU.is_equal))
            step(dve.tensor_reduce(rsum[:, 0:1], sc[:, :], AX.X, ALU.add))
            settle()
            dve.wait_ge(s_low, 16)
            step(dve.tensor_tensor(same, same, lows, ALU.mult))
            step(dve.tensor_scalar(rsum[:, 1:2], rsum[:, 0:1], 1e-6, None, ALU.add))
            settle()
            step(dve.tensor_tensor(less, less, same, ALU.add))
            step(dve.reciprocal(rsum[:, 0:1], rsum[:, 1:2]))
            settle()
            step(dve.tensor_reduce(rt[:, :], less, AX.X, ALU.add))
            step(dve.tensor_scalar(oh[:, NSEL, :], sc[:, :], rsum[:, 0:1], None, ALU.mult))
            settle()
            for k in range(NSEL):
                step(dve.tensor_scalar(oh[:, k, :], rt[:, :], float(k), None, ALU.is_equal))
            settle()
            for e in range(2):
                lo, hi = 64 * e, 64 * e + 64
                step(dve.tensor_copy(own[lo:hi, 0, :], sc[lo:hi, e:T:2]))
                step(dve.tensor_scalar(own[lo:hi, 1, :], rt[lo:hi, e:T:2], float(NSEL), None, ALU.is_ge))
                step(dve.tensor_copy(gsl[lo:hi, :, :], oh[lo:hi, :, e:T:2]))
            step(dve.tensor_copy(ohs[0:64, :, :], oh[0:64, 0:NSEL:2, :]))
            step(dve.tensor_copy(ohs[64:128, 0:2, :], oh[64:128, 1:4:2, :]))
            step(dve.memset(ohs[64:128, 2, :], 0.0))
            settle()
            dve.memset(qe[:, :, :, 30:32], 0.0).then_inc(oh_ready, 1)

            dve.wait_ge(d_used, NT)
            step(dve.tensor_copy(gt[:, :, 0:SLOT, :], bank[0:HALF, 1:3, 0:SLOT * B].rearrange("p m (s b) -> p m s b", b=B)))
            dve.wait_ge(oh_ready, 1)
            settle()
            dve.tensor_copy(gt[:, :, SLOT, :], gt[:, :, NSEL, :]).then_inc(g_ready, 1)
            dve.wait_ge(q2_sb, 1)
            for k in range(6):
                dve.tensor_scalar(qe[:, :, :, NSEL * k:NSEL * k + NSEL].rearrange("p m b s -> p m s b"), qs[:, :, :, :],
                                  hmask[:, k:k + 1], None, ALU.mult).then_inc(qe_ready, 1)
            dve.wait_ge(pm_ps, 1)
            dve.tensor_copy(pm, bank[:, 5, 0:D]).then_inc(pm_ready, 1)

            for k in range(3):
                n0, n1 = 12 * k, min(12 * k + 12, PAIRS)
                raw = bank[:, k, 0:(n1 - n0) * T].rearrange("p (n j) -> p n j", j=T)
                dve.wait_ge(l2_ps, k + 1)
                step(dve.tensor_reduce(mx2[:, 0, n0:n1], raw, AX.X, ALU.max))
                settle()
                dve.tensor_tensor(s2[:, n0:n1, :], raw, mx2[:, 0, n0:n1].unsqueeze(2).to_broadcast([P, n1 - n0, T]),
                                  ALU.subtract).then_inc(l2_cent, 1)
            for k in range(3):
                n0, n1 = 12 * k, min(12 * k + 12, PAIRS)
                dve.wait_ge(l2_exp, k + 1)
                step(dve.tensor_reduce(mx2[:, 1, n0:n1], s2[:, n0:n1, :], AX.X, ALU.add))
                settle()
                step(dve.reciprocal(mx2[:, 1, n0:n1], mx2[:, 1, n0:n1]))
                settle()
                dve.tensor_tensor(s2[:, n0:n1, :], s2[:, n0:n1, :], mx2[:, 1, n0:n1].unsqueeze(2).to_broadcast([P, n1 - n0, T]),
                                  ALU.mult).then_inc(l2_ready, 1)
            for k in range(PAIRS // 4):
                dve.wait_ge(c2_ps, k + 1)
                if k >= 2:
                    dve.wait_ge(c2_ready, k - 1)
                dve.tensor_tensor(otmp[:, k % 2, :, :].rearrange("p n (h s) -> p n h s", s=NSEL),
                                  bank[0:HALF, 6 + k % 2, :].rearrange("p (n c) -> p n c", c=32)[:, :, 0:30].rearrange("p n (h s) -> p n h s", s=NSEL),
                                  hmask.unsqueeze(1).unsqueeze(3).to_broadcast([HALF, 16, 6, NSEL]), ALU.mult).then_inc(c2_tmp, 1)
                dve.wait_ge(c2_tmp, k + 1)
                for m in range(2):
                    ins = dve.tensor_reduce(o2t[:, m, :, 8 * k:8 * k + 8].rearrange("p s b -> p b s"),
                                            otmp[:, k % 2, 8 * m:8 * m + 8, :].rearrange("p n (h s) -> p n s h", s=NSEL),
                                            AX.X, ALU.add)
                    if m:
                        ins.then_inc(c2_ready, 1)
                    else:
                        step(ins)
            settle()
            dve.memset(asel[64:128, 2, :], 0.0).then_inc(as_ready, 1)
            for k in range(3):
                rows = P if k < 2 else B
                dve.wait_ge(as_ps, k + 1)
                dve.tensor_tensor(asel[0:rows, k, :], bank[0:rows, 3 + k, 0:D], brow_bc("bo2")[0:rows, :], ALU.add).then_inc(as_ready, 1)

            def merged(i):
                for n in range(TPR * i, TPR * i + TPR):
                    j = n % TPR
                    dve.wait_ge(mg_ps, n + 1)
                    step(dve.scalar_tensor_tensor(mrg[:, 0, j, :], pm, own[:, 0, n:n + 1], bank[:, n % 3, 0:D], ALU.mult, ALU.add))
                    dve.scalar_tensor_tensor(mrg[:, 1, j, :], brow_bc("bm"), own[:, 1, n:n + 1], nat[:, n, :],
                                             ALU.mult, ALU.add).then_inc(mg_bias, 1)
                    settle()
                    dve.scalar_tensor_tensor(mrg[:, 0, j, :], mrg[:, 0, j, :], own[:, 1, n:n + 1], bank[:, n % 3, D:2 * D],
                                             ALU.mult, ALU.add).then_inc(mg_c, 1)
                    dve.wait_ge(mg_c, n + 1)
                    dve.wait_ge(mg_bias, n + 1)
                    dve.tensor_tensor(norm[:, n, :], mrg[:, 0, j, :], mrg[:, 1, j, :], ALU.add).then_inc(h2_ready, 1)
                    dve.wait_ge(h2_ready, n + 1)
                    moments(2, norm[:, n, :], n, ln2_mv)
                    dve.wait_ge(ln2_mv, n + 1)
                add_eps(2, i, ln2_mv, ln2_var)
                dve.wait_ge(ln2_rstd, i + 1)
                for n in range(TPR * i, TPR * i + TPR):
                    if i >= 2:
                        dve.wait_ge(n2_ps, n - 2 * TPR + 1)
                    centre(2, mrg[:, 2 + i % 2, n % TPR, :], norm[:, n, :], n).then_inc(n2_cent, 1)

            def final(i):
                for n in range(TPR * i, TPR * i + TPR):
                    dve.wait_ge(f2_ps, n + 1)
                    dve.wait_ge(res_ready, n + 1)
                    dve.tensor_tensor(nat[:, n, :], bank[:, 7, 0:D], nat[:, n, :], ALU.add).then_inc(y_ready, 1)
                    dve.wait_ge(y_ready, n + 1)
                    moments(3, nat[:, n, :], n, ln3_mv)
                    dve.wait_ge(ln3_mv, n + 1)
                add_eps(3, i, ln3_mv, ln3_var)
                dve.wait_ge(ln3_rstd, i + 1)
                for n in range(TPR * i, TPR * i + TPR):
                    centre(3, nat[:, n, :], nat[:, n, :], n).then_inc(y_out, 1)

            for i in range(GRID + 2):
                if i < GRID:
                    merged(i)
                if i >= 2:
                    final(i - 2)

        @block.scalar
        def _(act):
            for k in range(2):
                load_x(act, k)
            act.dma_start(cs[:, :], cst).then_inc(s_cst, 16)
            act.wait_ge(pads_left, 1)
            act.wait_ge(pads_right, 1)

            def squares(r):
                act.wait_ge(s_x[(r + 1) // 2], 32)
                if r >= 2:
                    act.wait_ge(rsq_ready, r - 1)
                act.activation(sq[:, r % 2, :, :].rearrange("p c q -> p (c q)"),
                               xs[:, r, :, :, :].rearrange("p c q b -> p (c q b)"), ACT.Square).then_inc(sq_ready, 1)

            for r in range(3):
                squares(r)
            for i in range(GRID + 1):
                for r in (2 * i + 3, 2 * i + 4):
                    if r < NB:
                        squares(r)
                if i:
                    for n in range(TPR * (i - 1), TPR * i):
                        act.wait_ge(htr_ps, n + 1)
                        act.copy(ht[:, :, n * P:(n + 1) * P],
                                 bank[0:HALF, 6 + n % 2, 0:2 * P].rearrange("p (m c) -> p m c", m=2)).then_inc(ht_ready, 1)
            for i in range(GRID):
                for m in range(2):
                    act.wait_ge(qk_ps, 4 * i + 1 + m)
                    act.activation(qt[:, m, GRID * i:GRID * i + GRID, :],
                                   bank[0:HALF, (4 * i + m) % 6, 0:CHUNK].rearrange("p (t b) -> p t b", b=B),
                                   ACT.Identity, bias=colb[:, m:m + 1]).then_inc(q_ready, 1)
            for jp in range(T // 2):
                act.wait_ge(p2c_ps, jp + 1)
                w = bank[0:64, jp % 4, 0:H * WIN].rearrange("p (h w) -> p h w", w=WIN)
                act.copy(cmat[:, :, :, 2 * jp].rearrange("p i h -> p h i"), w[:, :, 1:1 + T]).then_inc(p2c_act, 1)
            for n in range(NT):
                act.wait_ge(vz_ready, n + 1)
                act.dma_start(vd[n * P:(n + 1) * P, :], vz[:, n % 4, :, :].rearrange("p e o -> p (e o)")).then_inc(vz_out[n % 4], 16)

            def pt_copy(n):
                act.wait_ge(pt_ps, n + 1)
                if n >= 2:
                    act.wait_ge(o_ps, n - 1)
                b0 = 3 + 2 * (n % 2)
                act.copy(ptr[:, n % 2, :, :].rearrange("p (a k) c -> p a (k c)", a=2),
                         bank[0:2 * T, b0:b0 + 2, 0:300]).then_inc(pt_sb, 1)

            def o_copy(n):
                act.wait_ge(o_ps, n + 1)
                act.copy(ot[:, :, :, 2 * n:2 * n + 2].rearrange("p m t b -> p m b t"),
                         bank[0:HALF, 7, 0:4 * T].rearrange("p (m b t) -> p m b t", m=2, b=2)).then_inc(o_sb, 1)

            act.wait_ge(v_ps, NT)
            act.wait_ge(bd_ready, 4)
            for n in range(PAIRS + 3):
                if n < PAIRS:
                    act.wait_ge(s_sub, n + 1)
                    act.activation(sring[0:100, n % 3, :], sring[0:100, n % 3, :], ACT.Exp,
                                   scale=float((3 * DH) ** -0.5)).then_inc(s_exp, 1)
                if 0 <= n - 2 < PAIRS:
                    pt_copy(n - 2)
                if n >= 3:
                    o_copy(n - 3)

            def turned(n, ps_ready, sb_ready, b):
                act.wait_ge(ps_ready, n + 1)
                act.copy(nt_[:, :, n * P:(n + 1) * P],
                         bank[0:HALF, b, 0:2 * P].rearrange("p (m c) -> p m c", m=2)).then_inc(sb_ready, 1)

            act.wait_ge(wo_ps, NT)
            for i in range(GRID):
                for n in range(TPR * i, TPR * i + TPR):
                    turned(n, n_ps, nt_ready, 6 + n % 2)
                for m in range(2):
                    u = 2 * i + m
                    act.wait_ge(k2_ps, u + 1)
                    act.activation(ktf[:, m, i * CHUNK:(i + 1) * CHUNK], bank[0:HALF, u % 4, 0:CHUNK], ACT.Identity,
                                   bias=colb[:, 10 + m:11 + m]).then_inc(k2_ready, 1)
            act.wait_ge(z_ps, 1)
            act.wait_ge(nbr_ready, 1)
            act.activation(rt[:, :], bank[:, 0, 0:T], ACT.Exp, scale=-1.0, bias=nbr[:, :]).then_inc(z_exp, 1)
            act.wait_ge(q2_ps, 1)
            act.activation(qs[:, 0, :, :].rearrange("p s b -> p (s b)"), bank[0:HALF, 3, 0:NSEL * B], ACT.Identity,
                           bias=colb[:, 8:9]).then_inc(q2_part, 1)
            act.wait_ge(q2_part, 1)
            act.activation(qs[:, 1, :, :].rearrange("p s b -> p (s b)"), bank[0:HALF, 6, 0:NSEL * B], ACT.Identity,
                           bias=colb[:, 9:10]).then_inc(q2_sb, 1)
            for k in range(3):
                n0, n1 = 12 * k, min(12 * k + 12, PAIRS)
                act.wait_ge(l2_cent, k + 1)
                act.activation(s2[:, n0:n1, :], s2[:, n0:n1, :], ACT.Exp, scale=float(DH ** -0.5)).then_inc(l2_exp, 1)
            for k in range(PAIRS // 4):
                act.wait_ge(t2_ps, k + 1)
                if k >= 2:
                    act.wait_ge(c2_ps, k - 1)
                act.copy(pt2[:, k % 2, :, :].rearrange("p n c -> p (n c)"), bank[0:T, 3 + k % 2, :]).then_inc(t2_ready, 1)
            for i in range(GRID):
                for n in range(TPR * i, TPR * i + TPR):
                    turned(n, n2_ps, n2t_ready, 6)
                for k in range(FF // P):
                    u = 6 * i + k
                    act.wait_ge(f1_ps, u + 1)
                    act.activation(hid[:, k, i * CHUNK:(i + 1) * CHUNK], bank[:, 3 + u % 3, 0:CHUNK], ACT.Gelu,
                                   bias=bf1s[:, k:k + 1]).then_inc(f1_ready, 1)

        @block.gpsimd
        def _(pool):
            def rstd_tok(i):
                pool.wait_ge(tvar, i + 1)
                pool.tensor_tensor(rst[:, :], st[:, 3 * TPR:4 * TPR], nhalf[:, :], ALU.pow).then_inc(trstd, 1)

            pool.memset(ones[:, :], 1.0).then_inc(ones_set, 1)
            pool.memset(nhalf[:, :], -0.5).then_inc(nhalf_set, 1)
            pool.wait_ge(ones_set, 1)
            pool.wait_ge(nhalf_set, 1)
            pool.memset(xs[64:128, :, :, NQ - 1, :].rearrange("p r c b -> p (r c) b"), 0.0).then_inc(pads_right, 1)
            pool.wait_ge(pads_right, 1)

            def beta_w():
                pool.wait_ge(wg_ready, 8)
                pool.wait_ge(wc_ready, 4)
                pool.wait_ge(s_gb, 32)
                pool.tensor_tensor(wraw, wraw, bets[:, :].unsqueeze(2).to_broadcast([P, WRAW, D]), ALU.mult).then_inc(wb_ready, 1)
            for i in range(GRID):
                pool.wait_ge(rsq_ready, min(2 * i + 3, NB))
                if i >= 2:
                    pool.wait_ge(ss_ready, i - 1)
                pool.tensor_tensor(esum[i % 2], rsq[:, 2 * i % 6, :], rsq[:, (2 * i + 1) % 6, :], ALU.add).then_inc(esum_set, 1)
                outer = [r for r in (2 * i - 1, 2 * i + 2) if 0 <= r < NB]
                if len(outer) == 2:
                    pool.tensor_tensor(usum[i % 2], rsq[:, outer[0] % 6, :], rsq[:, outer[1] % 6, :], ALU.add).then_inc(esum_set, 1)
                    pool.wait_ge(esum_set, 2 * i + 1)
                    pool.tensor_tensor(usum[i % 2], usum[i % 2], esum[i % 2], ALU.add).then_inc(eu_ready, 1)
                else:
                    pool.wait_ge(esum_set, max(2 * i, 1))
                    pool.tensor_tensor(usum[i % 2], rsq[:, outer[0] % 6, :], esum[i % 2], ALU.add).then_inc(eu_ready, 1)
                if i == 0:
                    beta_w()
                else:
                    rstd_tok(i - 1)
            rstd_tok(GRID - 1)

            for n in range(PAIRS + 1):
                if n < PAIRS:
                    pool.wait_ge(s_max, n + 1)
                    sv = sring[0:100, n % 3, :].rearrange("p (h j) -> p h j", j=T)
                    pool.tensor_tensor(sv, sv, mx[0:100, n % 3, :].unsqueeze(2).to_broadcast([100, H, T]),
                                       ALU.subtract).then_inc(s_sub, 1)
                if n:
                    k = n - 1
                    pool.wait_ge(s_inv, k + 1)
                    sv = sring[0:100, k % 3, :].rearrange("p (h j) -> p h j", j=T)
                    pool.tensor_tensor(sv, sv, rs[0:100, k % 3, :].unsqueeze(2).to_broadcast([100, H, T]),
                                       ALU.mult).then_inc(s_nrm, 1)
                if n < NT:
                    pool.tensor_tensor(nat[:, n, :], nat[:, n, :], brow_bc("bo1"), ALU.add).then_inc(hb_ready, 1)

            def rstd(k, i, var_ready, rstd_ready):
                pool.wait_ge(var_ready, i + 1)
                pool.tensor_tensor(lnb[:, k, TPR * i:TPR * i + TPR, 2], lnb[:, k, TPR * i:TPR * i + TPR, 1], nhalf[:, :],
                                   ALU.pow).then_inc(rstd_ready, 1)

            def gain(t, n, name_g, name_b, cent, gained, ready):
                pool.wait_ge(cent, n + 1)
                pool.tensor_tensor(t, t, brow_bc(name_g), ALU.mult).then_inc(gained, 1)
                pool.wait_ge(gained, n + 1)
                pool.tensor_tensor(t, t, brow_bc(name_b), ALU.add).then_inc(ready, 1)

            for i in range(GRID + 2):
                if i < GRID:
                    rstd(0, i, ln_var, ln_rstd)
                if 1 <= i <= GRID:
                    rstd(1, i - 1, ln1_var, ln1_rstd)
                if i >= 2:
                    for n in range(TPR * (i - 2), TPR * (i - 1)):
                        gain(norm[:, n, :], n, "g1", "b1", n_cent, n_gain, n_ready)
            pool.wait_ge(oh_ready, 1)
            for n in range(NT):
                if n >= 3:
                    pool.wait_ge(d_used, n - 2)
                pool.tensor_tensor(dring[:, n % 3, :, :], gsl[:, :, n:n + 1].to_broadcast([P, SLOT, B]),
                                   ident2[:, 0:B].unsqueeze(1).to_broadcast([P, SLOT, B]), ALU.mult).then_inc(d_ready, 1)
            pool.wait_ge(l2_ps, 3)

            def spread(n):
                if n >= 3:
                    pool.wait_ge(mg_ps, n - 2)
                pool.tensor_tensor(dtr[:, n % 3, :, :].rearrange("p k (e b) -> p k e b", e=2),
                                   ident2.rearrange("p (e b) -> p e b", e=2).unsqueeze(1).to_broadcast([P, 3, 2, B]),
                                   ohs[:, :, 2 * n:2 * n + 2].unsqueeze(3).to_broadcast([P, 3, 2, B]), ALU.mult).then_inc(dt_ready, 1)

            def residual(n):
                pool.wait_ge(h2_ready, n + 1)
                pool.tensor_tensor(nat[:, n, :], nat[:, n, :], norm[:, n, :], ALU.add).then_inc(res_part, 1)
                pool.wait_ge(res_part, n + 1)
                pool.tensor_tensor(nat[:, n, :], nat[:, n, :], brow_bc("bf2"), ALU.add).then_inc(res_ready, 1)

            for n in range(TPR):
                spread(n)
            for i in range(GRID + 2):
                if i < GRID:
                    for n in range(TPR * (i + 1), min(TPR * (i + 2), NT)):
                        spread(n)
                    rstd(2, i, ln2_var, ln2_rstd)
                    for n in range(TPR * i, TPR * i + TPR):
                        gain(mrg[:, 2 + i % 2, n % TPR, :], n, "g2", "b2", n2_cent, n2_gain, n2_ready)
                    for n in range(TPR * i, TPR * i + TPR):
                        residual(n)
                if i >= 2:
                    rstd(3, i - 2, ln3_var, ln3_rstd)


def kernel(**a):
    import numpy as np
    import concourse.bacc as bacc
    from concourse.bass_utils import run_bass_kernel_spmd

    x = a["x"].reshape(B, CH, NB, 8, NQ - 1, 2, 8)
    xh = np.stack([x[:, :, :, :, :, 1, :], x[:, :, :, :, :, 0, :]]).transpose(0, 4, 6, 3, 2, 5, 1)
    xh = xh.reshape(P, NB, CH, NQ - 1, B)

    def pack(w):
        o = w.shape[0]
        w = w.reshape(o, 2, 8, 2, 8, 5, CH)
        quad = {(0, 0): 1, (0, 1): 3, (1, 0): 4, (1, 1): 2}
        chunks = []
        for r in range(4):
            for s in range(2):
                q = w[:, r % 2, :, :, :, quad[(r // 2, s)], :]
                chunks.append(q.transpose(2, 1, 3, 4, 0).reshape(P, CH, o))
        for r in range(2):
            q = w[:, r, :, ::-1, :, 0, :]
            chunks.append(q.transpose(2, 1, 3, 4, 0).reshape(P, CH, o))
        return np.concatenate(chunks, axis=1)

    def split(w):
        return w.reshape(2, HALF, -1).transpose(1, 0, 2)

    A, F = "L0_attn_", "L0_ffn_"
    rel = a[A + "rel_table"][127 - (T - 1):127 + T]
    consts = np.zeros((P, 2 * P + 10), np.float32)
    p = np.arange(P)
    consts[:, 0:P] = np.eye(P)
    consts[:, P:2 * P] = p[:, None] % 64 == p[None, :] % 64
    consts[:, 2 * P:2 * P + 6] = (p[:, None] // DH) % 8 == np.arange(6)[None, :]
    consts[:, 2 * P + 6:2 * P + 8] = (p[:, None] // DH) % 2 == np.arange(2)[None, :]
    consts[:, 2 * P + 8] = p < 64
    consts[:, 2 * P + 9] = p >= 64
    t = np.arange(T)
    rows = {"tok_b": "L0_tok_b", "bv1": A + "bv", "bo1": A + "bo", "g1": F + "g1", "b1": F + "b1", "bv2": F + "bv",
            "bm": F + "bm", "bo2": F + "bo", "g2": F + "g2", "b2": F + "b2", "bf2": F + "bf2"}
    arrays = {
        "x": xh,
        "wtok": pack(a["L0_tok_W"]),
        "gam": pack(a["L0_tok_ln_gamma"].reshape(1, PDIM))[:, :, 0],
        "bet": pack(a["L0_tok_ln_beta"].reshape(1, PDIM))[:, :, 0],
        "watt": np.stack([split(a[A + n]) for n in ("Wq", "Wk", "Wv", "Wo", "Wpk", "Wpq")], axis=1),
        "relt": np.stack([split(rel[::-1].T), split(rel.T)], axis=1),
        "wffn": np.concatenate([split(a[F + n]) for n in ("Wq", "Wk", "Wv", "Wo", "Wm", "W1")], axis=2),
        "w2": a[F + "W2"].reshape(FF // P, P, D).transpose(1, 0, 2),
        "brow": np.stack([a[rows[n]] for n in BIAS_ROWS]),
        "col": np.concatenate([a[n].reshape(2, HALF).T for n in
                               (A + "bq", A + "bk", A + "bpk", A + "bpq", F + "bq", F + "bk")], axis=1),
        "bf1": a[F + "bf1"].reshape(FF // P, P).T,
        "wr": a[F + "Wr"].reshape(2, HALF).T,
        "br": a[F + "br"].reshape(1, 1),
        "cst": consts,
        "lower": (t[None, :] < t[:, None]).astype(np.float32).reshape(1, T, T),
    }
    nc = bacc.Bacc("TRN2", target_bir_lowering=False, num_devices=1)
    args, feed = [], {}
    for name, v in arrays.items():
        feed[f"in_{name}"] = np.ascontiguousarray(v)
        args.append(nc.dram_tensor(f"in_{name}", feed[f"in_{name}"].shape, F32, kind="ExternalInput").ap())
    args.append(nc.dram_tensor("out_0", (B, T, D), F32, kind="ExternalOutput").ap())
    build(nc, *args)
    r = run_bass_kernel_spmd(nc, [feed], core_ids=[0])
    return r.results[0]["out_0"]
```

```python
from contextlib import ExitStack

import concourse.bass as bass
from concourse import mybir

F32 = mybir.dt.float32
ALU = mybir.AluOpType
ACT = mybir.ActivationFunctionType
AX = mybir.AxisListType

P = 128
B = 64
GRID = 6
T = GRID * GRID
D = 192
HALF = D // 2
H = 12
DH = D // H
FF = 4 * D
CH = 3
PATCH = 16
PDIM = PATCH * PATCH * 5 * CH
EPS = 1e-5
NT = B * T // P
TPR = NT // GRID
TOK = B * T
CHUNK = TPR * P
REL = 2 * T - 1
WIN = T + 1
NB = 12
NQ = NB // 2 + 1
ROW = CH * NQ * B
QW = NQ * B
GQ = 3
HT_COLS = H * T
PAIRS = B // 2
NSEL = 5
SLOT = NSEL + 1
BIAS_ROWS = ["tok_b", "bv1", "bo1", "b1", "bm", "bo2", "bf2"]
COLS = ["bq1", "bk1", "bpk", "bpq", "bq2", "bk2", "g1", "b1", "g2", "b2", "bv2"]
WCH = 24
WRAW = WCH + 6


def build(nc, x, wtok, gam, bet, watt, relt, wffn, w2, brow, col, bf1, br, cst, lower, out):
    with ExitStack() as ctx:
        def sb(name, shape):
            return ctx.enter_context(nc.sbuf_tensor(name, shape, F32))

        def sem(name):
            return ctx.enter_context(nc.semaphore(name))

        ax = sb("arena_x", [P, NB * ROW])
        aqk = sb("arena_qk", [P, 6 * TOK + 2])
        aht = sb("arena_ht", [HALF, 2 * TOK])
        nat = sb("nat", [P, NT, D])
        ann = sb("arena_nn", [P, NT * D])
        arg = sb("arena_ring", [P, 2 * ROW + 48])
        wat = sb("wat", [HALF, 6, 2, D])
        bdt = sb("bdt", [HALF, 2, 2, 6, REL])
        bias = sb("bias", [P, len(BIAS_ROWS), D])
        cs = sb("cs", [P, 2 * P + 6 + 2 + 2])
        colb = sb("colb", [HALF, 2 * len(COLS)])
        bf1s = sb("bf1s", [P, FF // P])
        brs = sb("brs", [P, 1])
        st = sb("st", [P, 128])

        ident = cs[:, 0:P]
        ident2 = cs[:, P:2 * P]
        hmask = cs[0:HALF, 2 * P:2 * P + 6]
        emask = cs[0:HALF, 2 * P + 6:2 * P + 8]
        sidem = cs[:, 2 * P + 8:2 * P + 10]

        def brow_bc(name):
            return bias[:, BIAS_ROWS.index(name), :]

        def fcol(name, m):
            k = 2 * COLS.index(name) + m
            return colb[:, k:k + 1]

        xs = ax[:, :].rearrange("p (r c q b) -> p r c q b", r=NB, c=CH, q=NQ)
        wraw = aqk[:, 0:WRAW * D].rearrange("p (k o) -> p k o", o=D)
        o0 = WRAW * D
        wg = aqk[:, o0:o0 + WCH * (D + 1)].rearrange("p (a s c o) -> p a s c o", a=4, s=2, c=CH)
        wgf = aqk[:, o0:o0 + WCH * (D + 1)].rearrange("p (k o) -> p k o", o=D + 1)
        o0 += WCH * (D + 1)
        wgc = aqk[:, o0:o0 + 6 * D].rearrange("p (a c o) -> p a c o", a=2, c=CH)
        o0 += 6 * D
        esum = [aqk[:, o0 + 2 * k * QW:o0 + (2 * k + 1) * QW] for k in range(2)]
        usum = [aqk[:, o0 + (2 * k + 1) * QW:o0 + (2 * k + 2) * QW] for k in range(2)]
        side1 = aqk[:, o0 + 4 * QW:o0 + 5 * QW]
        assert o0 + 5 * QW <= 6 * TOK
        gams = sb("gams", [P, WRAW])
        bets = sb("bets", [P, WRAW])
        rsq = ann[:, 0:6 * QW].rearrange("p (s q) -> p s q", s=6)
        ssum = ann[:, 6 * QW:6 * QW + 2 * CHUNK].rearrange("p (s c) -> p s c", s=2)
        sq = arg[:, 0:2 * ROW].rearrange("p (s c q) -> p s c q", s=2, c=CH)
        swb = sb("swb", [P, D])
        cb = sb("cb", [P, D])
        red = sb("red", [P, 2, D])
        ones = sb("ones", [P, P])

        ht = aht[:, :].rearrange("p (m t) -> p m t", m=2)
        qt = aqk[0:HALF, 0:2 * TOK].rearrange("p (m t b) -> p m t b", m=2, t=T)
        ke = aqk[0:HALF, 2 * TOK:6 * TOK].rearrange("p (m e t b) -> p m e t b", m=2, e=2, t=T)
        cmat = ax[0:B, 0:T * HT_COLS].rearrange("p (i h j) -> p i h j", i=T, j=T)
        vz = ann[:, 4 * HT_COLS:4 * HT_COLS + 8 * D].rearrange("p (s e o) -> p s e o", s=4, e=2)
        cring = ann[:, 0:4 * HT_COLS].rearrange("p (s n c) -> p s n c", s=2, n=2)
        sring = ann[:, 4 * HT_COLS:7 * HT_COLS].rearrange("p (s c) -> p s c", s=3)
        ptr = arg[0:2 * T, 0:1200].rearrange("p (s k c) -> p s k c", s=2, k=6)
        vbd = arg[0:2 * T, 1200:1200 + 8 * D].rearrange("p (s n o) -> p s n o", s=2, n=4)
        ot = aht[:, :].rearrange("p (m t b) -> p m t b", m=2, t=T)
        relts = arg[0:HALF, 0:4 * REL].rearrange("p (v m r) -> p v m r", v=2, m=2)
        pks = arg[0:HALF, 4 * REL:8 * REL].rearrange("p (v m r) -> p v m r", v=2, m=2)
        mx = st[:, 64:100].rearrange("p (s h) -> p s h", s=3)
        rs = sb("rs", [P, 3, H])
        stats = sb("stats", [P, TPR, 6])
        mv = sb("mv", [P, TPR, 2])
        nhalf = sb("nhalf", [P, 2 * TPR])
        rst = sb("rst", [P, TPR])

        norm = ann[:, :].rearrange("p (n o) -> p n o", o=D)
        nt_ = ht
        kt = aqk[0:HALF, 2 * TOK:4 * TOK].rearrange("p (m t b) -> p m t b", m=2, t=T)
        ktf = aqk[0:HALF, 2 * TOK:4 * TOK].rearrange("p (m t) -> p m t", m=2)
        FFC = 5 * D + 1 + FF
        wf = aqk[0:HALF, 4 * TOK:4 * TOK + 2 * FFC].rearrange("p (m o) -> p m o", m=2)
        w2s = aqk[:, 4 * TOK + 2 * FFC:6 * TOK + 2].rearrange("p (k o) -> p k o", o=D)
        WQ, WK, WV, WO, WM, W1 = 0, D, 2 * D, 3 * D + 1, 4 * D + 1, 5 * D + 1
        less = aqk[:, 0:T * T].rearrange("p (t u) -> p t u", u=T)
        same = aqk[:, T * T:2 * T * T].rearrange("p (t u) -> p t u", u=T)
        lows = aqk[:, 2 * T * T:3 * T * T].rearrange("p (t u) -> p t u", u=T)
        qe = aqk[0:HALF, 0:2 * B * 32].rearrange("p (m b c) -> p m b c", m=2, c=32)
        dring = arg[:, 0:3 * SLOT * B].rearrange("p (s k b) -> p s k b", s=3, k=SLOT)
        o1 = 3 * SLOT * B
        s2 = arg[:, 0:PAIRS * T].rearrange("p (n j) -> p n j", j=T)
        assert PAIRS * T <= o1
        o2t = arg[0:HALF, o1:o1 + 2 * NSEL * B].rearrange("p (m s b) -> p m s b", m=2, b=B)
        o1 += 2 * NSEL * B
        asel = arg[:, o1:o1 + 3 * D].rearrange("p (s o) -> p s o", o=D)
        o1 += 3 * D
        pm = arg[:, o1:o1 + D]
        o1 += D
        wdiag = arg[:, o1:o1 + B]
        assert o1 + B <= 2 * ROW + 48
        mixed = ax[:, 0:NT * D].rearrange("p (n o) -> p n o", o=D)
        o2 = NT * D
        hid = ax[:, o2:o2 + 3 * FF // P * CHUNK].rearrange("p (s k t) -> p s k t", s=3, t=CHUNK)
        v2s = ax[:, o2:o2 + NT * (D + 1)].rearrange("p (n o) -> p n o", o=D + 1)
        W2X = 64 + T
        s2x = ax[:, o2:o2 + PAIRS * W2X].rearrange("p (n j) -> p n j", j=W2X)
        o2 += NT * (D + 1)
        vj = ax[0:W2X, o2:o2 + PAIRS * D].rearrange("p (b o) -> p b o", o=D)
        o2 += PAIRS * D
        gt = ax[0:HALF, o2:o2 + 2 * (SLOT + 1) * B].rearrange("p (m s b) -> p m s b", m=2, b=B)
        o2 += 2 * (SLOT + 1) * B
        qs = ax[0:HALF, o2:o2 + 2 * NSEL * B].rearrange("p (m s b) -> p m s b", m=2, b=B)
        o2 += 2 * NSEL * B
        pt2 = ax[0:W2X, o2:o2 + 2 * 4 * P].rearrange("p (s n c) -> p s n c", s=2, n=4)
        assert o2 + 8 * P <= NB * ROW
        otmp = aqk[0:HALF, 18 * P:18 * P + 960].rearrange("p (s n c) -> p s n c", s=2, n=16)
        dtr = aqk[:, 0:6 * 3 * P].rearrange("p (s k c) -> p s k c", s=6, k=3)
        mrg = aqk[:, 18 * P:18 * P + 4 * TPR * D].rearrange("p (v n o) -> p v n o", v=4, n=TPR)
        lnb = sb("lnb", [P, 3, NT, 4])
        nb1 = sb("nb1", [P, NT])
        wsum = sb("wsum", [P, 1])
        zz = sb("zz", [P, 2, NT])
        sc = sb("sc", [P, T])
        rt = sb("rt", [P, T])
        oh = sb("oh", [P, SLOT, T])
        gsl = sb("gsl", [P, SLOT, NT])
        ohs = sb("ohs", [P, 3, T])
        own = sb("own", [P, 2, NT])
        nbr = sb("nbr", [P, 1])
        mx2 = sb("mx2", [P, 2, PAIRS])
        rsum = sb("rsum", [P, 2])

        bank = ctx.enter_context(nc.psum_tensor("bank", [P, 8, 512], F32))

        vd = nc.dram_tensor("v_scratch", [TOK, 2 * D], F32, kind="Internal").ap()
        v2d = nc.dram_tensor("v2_scratch", [TOK, D], F32, kind="Internal").ap()
        cd = nc.dram_tensor("c_scratch", [B, T, HT_COLS], F32, kind="Internal").ap()

        s_cst = sem("consts_in")
        s_w = [sem(f"wtok_in{k}") for k in range(5)]
        s_gb = sem("gamma_beta_in")
        s_x = [sem(f"x_in{k}") for k in range(7)]
        s_wat = sem("watt_in")
        s_rel = sem("rel_in")
        s_bias = sem("bias_in")
        pads_left = sem("pads_left")
        pads_right = sem("pads_right")
        ones_set = sem("ones_set")
        nhalf_set = sem("nhalf_set")
        wg_ready = sem("wg_ready")
        wc_ready = sem("wc_ready")
        wb_ready = sem("wb_ready")
        red_ready = sem("red_ready")
        swcb_ps = sem("swcb_ps")
        swb_ready = sem("swb_ready")
        sq_ready = sem("sq_ready")
        rsq_ready = sem("rsq_ready")
        eu_ready = sem("eu_ready")
        esum_set = sem("esum_set")
        ss_part = sem("window_squares_part")
        ss_ready = sem("window_squares_ready")
        tok_ps = sem("tok_ps")
        tstat = sem("tstat")
        tvar = sem("tvar")
        trstd = sem("trstd")
        tcent = sem("tcent")
        h_ready = sem("h_ready")
        htr_ps = sem("htr_ps")
        ht_ready = sem("ht_ready")
        pk_ps = sem("pk_ps")
        pk_sb = sem("pk_sb")
        bd_ready = sem("bd_ready")
        qk_ps = sem("qk_ps")
        q_ready = sem("q_ready")
        k_ready = sem("k_ready")
        v_ps = sem("v_ps")
        vz_ready = sem("vz_ready")
        vz_out = [sem(f"vz_out{k}") for k in range(4)]
        p2c_ps = sem("p2c_ps")
        p2c_act = sem("p2c_act")
        p2c_dve = sem("p2c_dve")
        c2p_ps = sem("c2p_ps")
        c_ready = sem("c_ready")
        c_out = sem("c_out")
        ring_zero = sem("ring_zero")
        sbank_zero = sem("sbank_zero")
        c_in = [sem("c_in0"), sem("c_in1")]
        v_in = [sem("v_in0"), sem("v_in1")]
        s_ps = sem("scores_ps")
        s_sum = sem("scores_summed")
        s_max = sem("scores_max")
        s_sub = sem("scores_centred")
        s_exp = sem("probs_exp")
        s_tot = sem("probs_total")
        s_inv = sem("probs_inv")
        s_nrm = sem("probs_ready")
        pt_ps = sem("probsT_ps")
        pt_sb = sem("probsT_ready")
        o_ps = sem("attn_ps")
        o_sb = sem("attn_ready")
        hb_ready = sem("hb_ready")
        wo_ps = sem("wo_ps")
        r_ready = sem("resid_ready")
        ln_var = sem("ln_var")
        ln_rstd = sem("ln_rstd")
        h1_ready = sem("h1_ready")
        nb_ready = sem("h1_shift_ready")
        n_ready = sem("normed_ready")
        n_ps = sem("normedT_ps")
        nt_ready = sem("normedT_ready")
        s_wf = sem("wffn_in")
        s_low = sem("lower_in")
        x2_ps = sem("mix_ps")
        x2_ready = sem("mix_ready")
        mb_ready = sem("mix_shifted")
        sx_zero = sem("probs2_zero")
        vj_zero = sem("values2_zero")
        pg_ready = sem("pooled_in_ready")
        k2_ps = sem("k2_ps")
        k2_ready = sem("k2_ready")
        v2_ps = sem("v2_ps")
        v2_ready = sem("v2_ready")
        v2_out = sem("v2_out")
        vj_in = sem("vj_in")
        zz_ready = sem("zz_ready")
        z_ps = sem("z_ps")
        nbr_ready = sem("nbr_ready")
        z_exp = sem("z_exp")
        dve_step = sem("dve_step")
        oh_ready = sem("onehot_ready")
        d_ready = sem("gather_diag_ready")
        d_used = sem("gather_diag_used")
        g_ready = sem("gathered_ready")
        q2_ps = sem("q2_ps")
        q2_sb = sem("q2_sb")
        qe_ready = sem("qe_ready")
        pm_ps = sem("pooled_ps")
        pm_ready = sem("pooled_ready")
        l2_ps = sem("logits_ps")
        l2_cent = sem("logits_centred")
        l2_exp = sem("logits_exp")
        l2_ready = sem("probs2_ready")
        t2_ps = sem("probs2T_ps")
        t2_ready = sem("probs2T_ready")
        c2_ps = sem("context_ps")
        c2_ready = sem("context_ready")
        ctx_ready = sem("context_with_bias")
        as_ps = sem("chosen_ps")
        as_ready = sem("chosen_ready")
        dt_ready = sem("scatter_diag_ready")
        mg_ps = sem("merge_ps")
        h2_ready = sem("h2_ready")
        ln2_var = sem("ln2_var")
        ln2_rstd = sem("ln2_rstd")
        n2_ready = sem("n2_ready")
        n2_ps = sem("n2T_ps")
        n2t_ready = sem("n2T_ready")
        res_part = sem("res_part")
        res_ready = sem("res_ready")
        f1_ps = sem("ffn1_ps")
        f1_ready = sem("ffn1_ready")
        f2_ps = sem("ffn2_ps")
        y_ready = sem("y_ready")
        ln3_var = sem("ln3_var")
        ln3_rstd = sem("ln3_rstd")
        y_out = sem("y_ready_out")
        s_out = sem("s_out")

        block = ctx.enter_context(nc.Block())
        XCH = [(0, 1), (1, 3), (3, 5), (5, 7), (7, 9), (9, 11), (11, 12)]
        xv = xs

        def window(i):
            return [(a, 2 * i - 1 + a) for a in range(4) if 0 <= 2 * i - 1 + a < NB]

        def load_x(eng, k):
            r0, r1 = XCH[k]
            for h in range(2):
                eng.dma_start(xs[64 * h:64 * h + 64, r0:r1, :, 1 - h:NQ - h, :],
                              x[64 * h:64 * h + 64, r0:r1, :, :, :]).then_inc(s_x[k], 16)

        @block.sync
        def _(sp):
            sp.dma_start(gams[:, :], gam).then_inc(s_gb, 16)
            sp.dma_start(bets[:, :], bet).then_inc(s_gb, 16)

            def load_w(k):
                sp.dma_start(wraw[:, 6 * k:6 * k + 6, :], wtok[:, 6 * k:6 * k + 6, :]).then_inc(s_w[k], 16)

            for k in (1, 4, 2, 3, 0):
                load_w(k)
            for k in range(2, len(XCH)):
                load_x(sp, k)
            sp.dma_start(bias[:, :, :], brow.partition_broadcast(P)).then_inc(s_bias, 16)
            sp.dma_start(colb[:, :], col).then_inc(s_bias, 16)
            sp.dma_start(bf1s[:, :], bf1).then_inc(s_bias, 16)
            sp.dma_start(brs[:, :], br.to_broadcast([P, 1])).then_inc(s_bias, 16)
            sp.dma_start(wat[:, :, :, :], watt).then_inc(s_wat, 16)
            sp.wait_ge(rsq_ready, NB)
            sp.dma_start(relts, relt).then_inc(s_rel, 16)
            for ip in range(T // 2):
                sp.wait_ge(c_ready, 2 * ip + 2)
                sp.dma_start(cd[:, 2 * ip:2 * ip + 2, :],
                             ax[0:B, 2 * ip * HT_COLS:(2 * ip + 2) * HT_COLS].rearrange("p (i c) -> p i c", i=2)
                             ).then_inc(c_out, 16)
            sp.wait_ge(c_out, 16 * (T // 2))
            sp.wait_ge(ring_zero, 1)

            def load_c(g):
                if g >= 2:
                    sp.wait_ge(s_sum, 2 * g - 2)
                for ib in range(2):
                    sp.dma_start(cring[64 * ib:64 * ib + T, g % 2, :, :],
                                 cd[4 * g + ib:4 * g + ib + 3:2, :, :].rearrange("n i c -> i n c")
                                 ).then_inc(c_in[g % 2], 16)

            def load_v(g):
                if g >= 2:
                    sp.wait_ge(o_ps, 2 * g - 2)
                for e in range(2):
                    sp.dma_start(vbd[T * e:T * e + T, g % 2, :, :],
                                 vd.rearrange("(t b) o -> t b o", b=B)[:, 4 * g:4 * g + 4, e * D:(e + 1) * D]
                                 ).then_inc(v_in[g % 2], 16)

            load_c(0)
            for g in range(PAIRS // 2):
                if g + 1 < PAIRS // 2:
                    load_c(g + 1)
                if g == 0:
                    for k in range(4):
                        sp.wait_ge(vz_out[k], 16 * len(range(k, NT, 4)))
                load_v(g)
            sp.wait_ge(s_ps, PAIRS)
            sp.dma_start(wf, wffn).then_inc(s_wf, 16)
            sp.dma_start(w2s, w2).then_inc(s_wf, 16)
            sp.dma_start(lows, lower.partition_broadcast(P)).then_inc(s_low, 16)
            for i in range(GRID):
                sp.wait_ge(v2_ready, TPR * (i + 1))
                sp.dma_start(v2d[i * CHUNK:(i + 1) * CHUNK, :].rearrange("(n p) o -> p n o", p=P),
                             v2s[:, TPR * i:TPR * i + TPR, 0:D]).then_inc(v2_out, 16)
            sp.wait_ge(v2_out, 16 * GRID)
            sp.wait_ge(vj_zero, 1)
            for ib in range(2):
                sp.dma_start(vj[64 * ib:64 * ib + T, :, :],
                             v2d.rearrange("(t n e) o -> e t n o", t=T, e=2)[ib]).then_inc(vj_in, 16)
            for n in range(NT):
                sp.wait_ge(y_out, n + 1)
                sp.dma_start(out[:, 2 * n:2 * n + 2, :].rearrange("b t o -> t b o"), nat[:, n, :]).then_inc(s_out, 16)
            sp.wait_ge(s_out, 16 * NT)

        @block.tensor
        def _(pe):
            def tok_product(n, a, r, first, last):
                k = 0
                for s in range(2):
                    for c in range(CH):
                        q0 = 2 * (n % TPR) + s
                        pe.matmul(bank[:, n % (2 * TPR), 0:D + 1], xs[:, r, c, q0:q0 + 2, :], wg[:, a, s, c, :],
                                  start=(first and k == 0), stop=(last and k == 2 * CH - 1))
                        k += 1

            def tok_squares(i):
                pe.wait_ge(ss_ready, i + 1)
                for n in range(TPR * i, TPR * i + TPR):
                    pe.matmul(bank[:, n % (2 * TPR), D + 8:D + 9], ssum[:, i % 2, n % TPR * P:n % TPR * P + P], ones[:, 0:1],
                              start=True, stop=True).then_inc(tok_ps, 1)

            def tok_row(i):
                rows = window(i)
                for k in range(7):
                    if XCH[k][0] <= rows[-1][1] < XCH[k][1]:
                        pe.wait_ge(s_x[k], 32)
                if i == 0:
                    for a, r in rows:
                        pe.wait_ge(s_x[(r + 1) // 2], 32)
                        pe.wait_ge(wg_ready, {1: 4, 2: 6, 3: 7}[a])
                        for n in range(TPR):
                            tok_product(n, a, r, a == 1, a == 3)
                else:
                    pe.wait_ge(wg_ready, 8)
                    for n in range(TPR * i, TPR * i + TPR):
                        if n >= 2 * TPR:
                            pe.wait_ge(h_ready, n - 2 * TPR + 1)
                        for a, r in rows:
                            tok_product(n, a, r, (a, r) == rows[0], (a, r) == rows[-1])
                        if n == TPR + 1:
                            pe.wait_ge(red_ready, 2)
                            for k in range(2):
                                mm = pe.matmul(bank[:, 6, k * D:(k + 1) * D], ones[:, :], red[:, k, :], start=True, stop=True)
                            mm.then_inc(swcb_ps, 1)
                tok_squares(i)

            def h_turn(n):
                pe.wait_ge(h_ready, n + 1)
                if n >= 2:
                    pe.wait_ge(ht_ready, n - 1)
                for m in range(2):
                    mm = pe.transpose(bank[0:HALF, 6 + n % 2, m * P:(m + 1) * P],
                                      nat[:, n, m * HALF:(m + 1) * HALF], ident)
                mm.then_inc(htr_ps, 1)

            pe.wait_ge(ones_set, 1)
            pe.wait_ge(pads_left, 1)
            pe.wait_ge(pads_right, 1)
            for i in range(GRID):
                tok_row(i)
                if i == 1:
                    pe.wait_ge(s_cst, 16)
                    pe.wait_ge(swb_ready, 2)
                if i:
                    for n in range(TPR * (i - 1), TPR * i):
                        h_turn(n)
            for jj in range(TPR):
                h_turn(TPR * (GRID - 1) + jj)

            pe.wait_ge(s_wat, 16)
            pe.wait_ge(s_rel, 16)
            pe.wait_ge(h_ready, NT)
            for v in range(2):
                for m in range(2):
                    for kk in range(2):
                        mm = pe.matmul(bank[0:HALF, 0, (2 * v + m) * REL:(2 * v + m + 1) * REL],
                                       wat[:, 4 + v, kk, m * HALF:(m + 1) * HALF], relts[:, v, kk, :],
                                       start=(kk == 0), stop=(kk == 1))
            mm.then_inc(pk_ps, 1)

            pe.wait_ge(pk_sb, 1)
            for i in range(GRID):
                pe.wait_ge(ht_ready, TPR * (i + 1))
                for which in range(2):
                    for m in range(2):
                        u = 4 * i + 2 * which + m
                        if u >= 6:
                            o = u - 6
                            if o % 4 < 2:
                                pe.wait_ge(q_ready, 2 * (o // 4) + o % 4 + 1)
                            else:
                                pe.wait_ge(k_ready, 2 * (2 * (o // 4) + o % 4 - 2) + 2)
                        for kk in range(2):
                            mm = pe.matmul(bank[0:HALF, u % 6, 0:CHUNK], wat[:, which, kk, m * HALF:(m + 1) * HALF],
                                           ht[:, kk, i * CHUNK:(i + 1) * CHUNK], start=(kk == 0), stop=(kk == 1))
                        mm.then_inc(qk_ps, 1)

            pe.wait_ge(q_ready, 2 * GRID)
            pe.wait_ge(k_ready, 4 * GRID)
            pe.wait_ge(bd_ready, 4)
            for jp in range(T // 2):
                if jp >= 4:
                    pe.wait_ge(p2c_act, jp - 3)
                    pe.wait_ge(p2c_dve, jp - 3)
                dst = bank[:, jp % 4, 0:H * WIN].rearrange("p (g m e w) -> p g m e w", g=GQ, m=2, e=2)
                for m in range(2):
                    for e in range(2):
                        mm = pe.matmul(dst[:, :, m, e, :],
                                       ke[:, m, e, 2 * jp:2 * jp + 2, :].rearrange("p t b -> p (t b)"),
                                       bdt[:, 1, m, e:6:2, T - 2 - 2 * jp:T - 2 - 2 * jp + WIN],
                                       start=True, stop=True)
                mm.then_inc(p2c_ps, 1)
            for ip in range(T // 2):
                u = ip + T // 2
                if ip < 4:
                    pe.wait_ge(p2c_act, u - 3)
                    pe.wait_ge(p2c_dve, u - 3)
                else:
                    pe.wait_ge(c_ready, 2 * (ip - 3))
                dst = bank[:, u % 4, 0:H * WIN].rearrange("p (g m e w) -> p g m e w", g=GQ, m=2, e=2)
                for m in range(2):
                    mm = pe.matmul(dst[:, :, m, :, :],
                                   qt[:, m, 2 * ip:2 * ip + 2, :].rearrange("p t b -> p (t b)"),
                                   bdt[:, 0, m, :, T - 2 - 2 * ip:T - 2 - 2 * ip + WIN].rearrange("p (g e) w -> p g e w", e=2),
                                   start=True, stop=True)
                mm.then_inc(c2p_ps, 1)

            for n in range(NT):
                if n >= 2:
                    pe.wait_ge(vz_ready, n - 1)
                for kk in range(2):
                    mm = pe.matmul(bank[:, 6 + n % 2, 0:D], ht[:, kk, n * P:(n + 1) * P], wat[:, 2, kk, :],
                                   start=(kk == 0), stop=(kk == 1))
                mm.then_inc(v_ps, 1)

            def scores(n):
                if n:
                    pe.wait_ge(s_sum, n)
                for m in range(2):
                    for ib in range(2):
                        for g in range(GQ):
                            mm = pe.matmul(bank[64 * ib:64 * ib + T, g, m * 2 * T:(m + 1) * 2 * T],
                                           qt[32 * g:32 * g + 32, m, :, 2 * n + ib],
                                           ke[32 * g:32 * g + 32, m, :, :, 2 * n + ib], start=True, stop=True)
                mm.then_inc(s_ps, 1)

            def turn(n):
                pe.wait_ge(s_nrm, n + 1)
                if n >= 2:
                    pe.wait_ge(pt_sb, n - 1)
                for k in range(6):
                    mm = pe.transpose(bank[0:2 * T, 3 + 2 * (n % 2) + k // 3, (k % 3) * 100:(k % 3) * 100 + 100],
                                      sring[0:100, n % 3, k * 2 * T:(k + 1) * 2 * T], ident[0:100, 0:100])
                mm.then_inc(pt_ps, 1)

            def mix(n):
                pe.wait_ge(pt_sb, n + 1)
                pe.wait_ge(v_in[n // 2 % 2], 32 * (n // 4 + 1))
                if n:
                    pe.wait_ge(o_sb, n)
                for ib in range(2):
                    for m in range(2):
                        for g in range(GQ):
                            mm = pe.matmul(bank[32 * g:32 * g + 32, 7, (2 * m + ib) * T:(2 * m + ib + 1) * T],
                                           vbd[:, n // 2 % 2, 2 * (n % 2) + ib, m * HALF + 32 * g:m * HALF + 32 * g + 32],
                                           ptr[:, n % 2, 2 * g + m, 64 * ib:64 * ib + T], start=True, stop=True)
                mm.then_inc(o_ps, 1)

            pe.wait_ge(sbank_zero, 1)
            pe.wait_ge(c_ready, T)
            for n in range(PAIRS + 3):
                if n < PAIRS:
                    scores(n)
                if 0 <= n - 2 < PAIRS:
                    turn(n - 2)
                if n >= 3:
                    mix(n - 3)

            def wo(i):
                for n in range(TPR * i, TPR * i + TPR):
                    if n >= 2:
                        pe.wait_ge(r_ready, n - 1)
                    for m in range(2):
                        mm = pe.matmul(bank[:, n % 2, 0:D], ot[:, m, 2 * n:2 * n + 2, :].rearrange("p t b -> p (t b)"),
                                       wat[:, 3, m, :], start=(m == 0), stop=(m == 1))
                    mm.then_inc(wo_ps, 1)

            def n_turn(i):
                if i >= 2:
                    pe.wait_ge(nt_ready, 2 * (i - 1))
                for n in range(TPR * i, TPR * i + TPR):
                    pe.wait_ge(n_ready, n + 1)
                    for m in range(2):
                        mm = pe.transpose(bank[0:HALF, 4 + 2 * (i % 2) + m, n % TPR * P:n % TPR * P + P],
                                          norm[:, n, m * HALF:(m + 1) * HALF], ident)
                mm.then_inc(n_ps, 1)

            def v2_row(i):
                pe.wait_ge(nt_ready, 2 * (i + 1))
                for n in range(TPR * i, TPR * i + TPR):
                    if n >= 2:
                        pe.wait_ge(v2_ready, n - 1)
                    for kk in range(2):
                        mm = pe.matmul(bank[:, 2 + n % 2, 0:D + 1], nt_[:, kk, n * P:(n + 1) * P], wf[:, kk, WV:WV + D + 1],
                                       start=(kk == 0), stop=(kk == 1))
                    mm.then_inc(v2_ps, 1)

            pe.wait_ge(o_sb, PAIRS)
            for i in range(GRID + 3):
                if i < GRID:
                    wo(i)
                if 2 <= i < GRID + 2:
                    n_turn(i - 2)
                if i >= 3:
                    if i == 3:
                        pe.wait_ge(s_wf, 32)
                    v2_row(i - 3)

            for i in range(GRID):
                if i == 1:
                    pe.wait_ge(zz_ready, 1)
                    pe.matmul(bank[:, 6, 0:T], ident2, zz[:, :, :].rearrange("p e n -> p (e n)"),
                              start=True, stop=True).then_inc(z_ps, 1)
                for m in range(2):
                    u = 2 * i + m
                    if u >= 2:
                        pe.wait_ge(k2_ready, u - 1)
                    else:
                        pe.wait_ge(r_ready, NT)
                    for kk in range(2):
                        mm = pe.matmul(bank[0:HALF, u % 2, 0:CHUNK], wf[:, kk, WK + m * HALF:WK + (m + 1) * HALF],
                                       nt_[:, kk, i * CHUNK:(i + 1) * CHUNK], start=(kk == 0), stop=(kk == 1))
                    mm.then_inc(k2_ps, 1)
            for n in range(NT):
                if n >= 2:
                    pe.wait_ge(x2_ready, n - 1)
                else:
                    pe.wait_ge(v2_ready, NT)
                for kk in range(2):
                    mm = pe.matmul(bank[:, 2 + n % 2, 0:D], nt_[:, kk, n * P:(n + 1) * P], wf[:, kk, WM:WM + D],
                                   start=(kk == 0), stop=(kk == 1))
                mm.then_inc(x2_ps, 1)

            pe.wait_ge(oh_ready, 1)
            for m in range(2):
                pe.matmul(bank[0:HALF, 4 + m, SLOT * B:(SLOT + 1) * B], brow_bc("b1")[:, m * HALF:(m + 1) * HALF], wdiag,
                          start=True, stop=True)
            for n in range(NT):
                pe.wait_ge(d_ready, n + 1)
                for m in range(2):
                    mm = pe.matmul(bank[0:HALF, 4 + m, 0:SLOT * B], norm[:, n, m * HALF:(m + 1) * HALF],
                                   dring[:, n % 3, :, :].rearrange("p k b -> p (k b)"), start=(n == 0), stop=(n == NT - 1))
                mm.then_inc(d_used, 1)
            pe.wait_ge(z_exp, 1)
            pe.wait_ge(g_ready, 2)
            for m in range(2):
                for kk in range(2):
                    mm = pe.matmul(bank[0:HALF, 6 + m, 0:NSEL * B], wf[:, kk, WQ + m * HALF:WQ + (m + 1) * HALF],
                                   gt[:, kk, 0:NSEL, :].rearrange("p s b -> p (s b)"), start=(kk == 0), stop=(kk == 1))
                mm.then_inc(q2_ps, 1)
            pe.wait_ge(x2_ready, NT)
            pe.wait_ge(pg_ready, 1)
            for kk in range(2):
                mm = pe.matmul(bank[:, 3, 0:D], gt[:, kk, NSEL:NSEL + 2, :].rearrange("p s b -> p (s b)"),
                               wf[:, kk, WM:WM + D], start=(kk == 0), stop=(kk == 1))
            mm.then_inc(pm_ps, 1)

            pe.wait_ge(qe_ready, 7)
            pe.wait_ge(k2_ready, 2 * GRID)
            for n in range(PAIRS):
                for ib in range(2):
                    for m in range(2):
                        q0 = 32 * (2 * ib + m)
                        mm = pe.matmul(bank[q0:q0 + 32, n // 12, n % 12 * T:n % 12 * T + T], qe[:, m, 2 * n + ib, :],
                                       kt[:, m, :, 2 * n + ib], start=True, stop=True)
                if n % 12 == 11 or n == PAIRS - 1:
                    mm.then_inc(l2_ps, 1)

            def turn2(k):
                pe.wait_ge(l2_ready, 2 * (k // 3 + 1))
                if k >= 2:
                    pe.wait_ge(t2_ready, k - 1)
                for n in range(4):
                    mm = pe.transpose(bank[0:W2X, 4 + k % 2, n * P:(n + 1) * P], s2x[:, 4 * k + n, :], ident)
                mm.then_inc(t2_ps, 1)

            def context(k):
                pe.wait_ge(t2_ready, k + 1)
                if k >= 2:
                    pe.wait_ge(c2_ready, 2 * (k - 1))
                for n in range(4):
                    for m in range(2):
                        c0 = (8 * m + 2 * n) * 32
                        mm = pe.matmul(bank[0:HALF, 6 + k % 2, c0:c0 + 64].rearrange("p (e c) -> p e c", e=2),
                                       vj[:, 4 * k + n, m * HALF:(m + 1) * HALF],
                                       pt2[:, k % 2, n, :].rearrange("p (e m c) -> p e m c", e=2, m=2)[:, :, m, :],
                                       start=True, stop=True)
                mm.then_inc(c2_ps, 1)

            pe.wait_ge(vj_in, 32)
            pe.wait_ge(q2_sb, 2)
            for k in range(PAIRS // 4 + 1):
                if k < PAIRS // 4:
                    turn2(k)
                if k:
                    context(k - 1)
            pe.wait_ge(ctx_ready, 2)
            pe.wait_ge(pm_ready, 1)
            for k in range(3):
                rows = P if k < 2 else B
                for m in range(2):
                    mm = pe.matmul(bank[0:rows, 3 + k, 0:D], o2t[:, m, :, :].rearrange("p s b -> p (s b)")[:, k * P:k * P + rows],
                                   wf[:, m, WO:WO + D], start=(m == 0), stop=(m == 1))
                mm.then_inc(as_ps, 1)

            def scatter(n):
                pe.wait_ge(dt_ready, n + 1)
                if n >= 2:
                    pe.wait_ge(h2_ready, n - 1)
                for k in range(3):
                    mm = pe.matmul(bank[:, n % 2, 0:D], dtr[:, n % 6, k, :], asel[:, k, :], start=(k == 0), stop=(k == 2))
                mm.then_inc(mg_ps, 1)

            def n2_turn(i):
                if i:
                    pe.wait_ge(n2t_ready, 2 * i)
                for n in range(TPR * i, TPR * i + TPR):
                    pe.wait_ge(n2_ready, n + 1)
                    for m in range(2):
                        mm = pe.transpose(bank[0:HALF, 2 + m, n % TPR * P:n % TPR * P + P],
                                          mrg[:, 2 + i % 2, n % TPR, m * HALF:(m + 1) * HALF], ident)
                mm.then_inc(n2_ps, 1)

            def ffn1(i):
                pe.wait_ge(n2t_ready, 2 * (i + 1))
                for k in range(FF // P):
                    u = 6 * i + k
                    if u >= 2:
                        pe.wait_ge(f1_ready, u - 1)
                    for kk in range(2):
                        mm = pe.matmul(bank[:, 4 + u % 2, 0:CHUNK], wf[:, kk, W1 + k * P:W1 + (k + 1) * P],
                                       nt_[:, kk, i * CHUNK:(i + 1) * CHUNK], start=(kk == 0), stop=(kk == 1))
                    mm.then_inc(f1_ps, 1)

            def ffn2(n):
                i, j = n // TPR, n % TPR
                pe.wait_ge(f1_ready, 6 * (i + 1))
                if n >= 2:
                    pe.wait_ge(y_ready, n - 1)
                for k in range(FF // P):
                    mm = pe.matmul(bank[:, 6 + n % 2, 0:D], hid[:, i % 3, k, j * P:(j + 1) * P], w2s[:, k, :],
                                   start=(k == 0), stop=(k == FF // P - 1))
                mm.then_inc(f2_ps, 1)

            pe.wait_ge(as_ready, 4)
            for i in range(GRID + 2):
                if i < GRID:
                    for n in range(TPR * i, TPR * i + TPR):
                        scatter(n)
                if 1 <= i <= GRID:
                    n2_turn(i - 1)
                if i >= 2:
                    for n in range(TPR * (i - 2), TPR * (i - 1)):
                        ffn2(n)
                if 1 <= i <= GRID:
                    ffn1(i - 1)

        @block.vector
        def _(dve):
            dve.memset(xs[0:64, :, :, 0, :].rearrange("p r c b -> p (r c) b"), 0.0).then_inc(pads_left, 1)
            dve.memset(wgf[:, :, D:D + 1], 1.0).then_inc(wc_ready, 1)
            dve.wait_ge(wc_ready, 1)
            dve.memset(wg[0:64, 1:3, 1, :, D:D + 1], 2.0).then_inc(wg_ready, 1)
            dve.memset(wg[64:128, 1:3, 0, :, D:D + 1], 2.0).then_inc(wg_ready, 1)
            dve.wait_ge(s_gb, 32)

            def gained(k):
                dve.wait_ge(s_w[k], 16)
                scale = gams[:, 6 * k:6 * k + 6].unsqueeze(2).to_broadcast([P, 6, D])
                dst = wgf[:, 6 * k:6 * k + 6, 0:D] if k < 4 else wgc.rearrange("p a c o -> p (a c) o")
                return dve.tensor_tensor(dst, wraw[:, 6 * k:6 * k + 6, :], scale, ALU.mult)

            def centre_in(a):
                s0, s1 = wg[64:128, 1 + a, 0, :, 0:D], wg[0:64, 1 + a, 1, :, 0:D]
                dve.tensor_tensor(s0, s0, wgc[64:128, a, :, :], ALU.add).then_inc(wg_ready, 1)
                dve.tensor_tensor(s1, s1, wgc[0:64, a, :, :], ALU.add).then_inc(wg_ready, 1)

            gained(1).then_inc(wc_ready, 1)
            gained(4).then_inc(wc_ready, 1)
            dve.wait_ge(wc_ready, 3)
            centre_in(0)
            gained(2).then_inc(wc_ready, 1)
            dve.wait_ge(wc_ready, 4)
            centre_in(1)
            gained(3).then_inc(wg_ready, 1)
            gained(0).then_inc(wg_ready, 1)

            def channel_sum(r):
                dve.wait_ge(sq_ready, r + 1)
                dve.tensor_reduce(rsq[:, r % 6, :], sq[:, r % 2, :, :].rearrange("p c q -> p q c"), AX.X,
                                  ALU.add).then_inc(rsq_ready, 1)

            def window_squares(i):
                dve.wait_ge(eu_ready, i + 1)
                if i >= 2:
                    dve.wait_ge(tok_ps, TPR * (i - 1))
                dve.scalar_tensor_tensor(side1, esum[i % 2], sidem[:, 1:2], usum[i % 2], ALU.mult, ALU.add).then_inc(ss_part, 1)
                dve.scalar_tensor_tensor(esum[i % 2], esum[i % 2], sidem[:, 0:1], usum[i % 2], ALU.mult,
                                         ALU.add).then_inc(ss_part, 1)
                dve.wait_ge(ss_part, 2 * i + 2)
                dve.tensor_tensor(ssum[:, i % 2, :], side1[:, 0:CHUNK], esum[i % 2][:, B:B + CHUNK], ALU.add).then_inc(ss_ready, 1)

            def tok_out(i):
                b0 = TPR * (i % 2)
                raw = bank[:, b0:b0 + TPR, :]
                dve.wait_ge(tok_ps, TPR * (i + 1))
                neg, e2, msq, var = (st[:, TPR * k:TPR * k + TPR] for k in range(4))
                dve.tensor_scalar(neg, raw[:, :, D], -1.0 / PDIM, None, ALU.mult).then_inc(tstat, 1)
                dve.tensor_scalar(e2, raw[:, :, D + 8], 1.0 / PDIM, EPS, ALU.mult, ALU.add).then_inc(tstat, 1)
                dve.wait_ge(tstat, 3 * i + 2)
                dve.tensor_tensor(msq, neg, neg, ALU.mult).then_inc(tstat, 1)
                dve.wait_ge(tstat, 3 * i + 3)
                dve.tensor_tensor(var, e2, msq, ALU.subtract).then_inc(tvar, 1)
                for jj in range(TPR):
                    n = TPR * i + jj
                    dve.scalar_tensor_tensor(nat[:, n, :], swb[:, :], st[:, jj:jj + 1], raw[:, jj, 0:D],
                                             ALU.mult, ALU.add).then_inc(tcent, 1)
                dve.wait_ge(trstd, i + 1)
                for jj in range(TPR):
                    n = TPR * i + jj
                    dve.wait_ge(tcent, n + 1)
                    dve.scalar_tensor_tensor(nat[:, n, :], nat[:, n, :], rst[:, jj:jj + 1], cb[:, :],
                                             ALU.mult, ALU.add).then_inc(h_ready, 1)

            for r in range(3):
                channel_sum(r)
            dve.wait_ge(s_cst, 16)
            window_squares(0)
            dve.wait_ge(wg_ready, 8)
            dve.tensor_reduce(red[:, 0, :], wgf[:, :, 0:D].rearrange("p k o -> p o k"), AX.X, ALU.add).then_inc(red_ready, 1)
            for r in range(3, 5):
                channel_sum(r)
            dve.wait_ge(wb_ready, 1)
            dve.tensor_reduce(red[:, 1, :], wraw.rearrange("p k o -> p o k"), AX.X, ALU.add).then_inc(red_ready, 1)
            window_squares(1)
            dve.wait_ge(swcb_ps, 1)
            dve.wait_ge(s_bias, 64)
            dve.tensor_copy(swb[:, :], bank[:, 6, 0:D]).then_inc(swb_ready, 1)
            dve.tensor_tensor(cb[:, :], bank[:, 6, D:2 * D], brow_bc("tok_b"), ALU.add).then_inc(swb_ready, 1)
            dve.wait_ge(swb_ready, 2)
            for i in range(GRID):
                if i:
                    for r in (2 * i + 3, 2 * i + 4):
                        if r < NB:
                            if r >= 6:
                                dve.wait_ge(eu_ready, (r - 6) // 2 + 1 + (r % 2))
                            channel_sum(r)
                    if i + 1 < GRID:
                        window_squares(i + 1)
                tok_out(i)

            dve.wait_ge(pk_ps, 1)
            for v in range(2):
                for m in range(2):
                    ins = dve.tensor_scalar(pks[:, v, m, :], bank[0:HALF, 0, (2 * v + m) * REL:(2 * v + m + 1) * REL],
                                            colb[:, 4 + 2 * v + m:5 + 2 * v + m], None, ALU.add)
            ins.then_inc(pk_sb, 1)
            dve.wait_ge(pk_sb, 1)
            for v in range(2):
                for m in range(2):
                    dve.tensor_tensor(bdt[:, v, m, :, :],
                                      pks[:, v, m, :].unsqueeze(1).to_broadcast([HALF, 6, REL]),
                                      hmask.unsqueeze(2).to_broadcast([HALF, 6, REL]), ALU.mult).then_inc(bd_ready, 1)
            dve.wait_ge(tok_ps, NT)
            dve.memset(ann[:, :], 0.0).then_inc(ring_zero, 1)
            dve.wait_ge(ring_zero, 1)
            for i in range(GRID):
                for m in range(2):
                    dve.wait_ge(qk_ps, 4 * i + 3 + m)
                    for e in range(2):
                        dve.tensor_scalar(ke[:, m, e, GRID * i:GRID * i + GRID, :],
                                          bank[0:HALF, (4 * i + 2 + m) % 6, 0:CHUNK].rearrange("p (t b) -> p t b", b=B),
                                          colb[:, 2 + m:3 + m], emask[:, e:e + 1], ALU.add, ALU.mult).then_inc(k_ready, 1)

            def win(u, par, flip):
                w = bank[64 * par:64 * par + 64, u % 4, 0:H * WIN].rearrange("p (h w) -> p h w", w=WIN)
                return w[:, :, 1 - par:1 - par + T]

            for jp in range(T // 2):
                dve.wait_ge(p2c_ps, jp + 1)
                dve.tensor_copy(cmat[:, :, :, 2 * jp + 1].rearrange("p i h -> p h i"), win(jp, 1, 0)).then_inc(p2c_dve, 1)
            dve.wait_ge(p2c_dve, T // 2)
            dve.wait_ge(p2c_act, T // 2)
            for ip in range(T // 2):
                dve.wait_ge(c2p_ps, ip + 1)
                for par in range(2):
                    dst = cmat[:, 2 * ip + par, :, :]
                    dve.tensor_tensor(dst, win(ip + T // 2, par, 0), dst, ALU.add).then_inc(c_ready, 1)
            dve.wait_ge(c_ready, T)
            dve.memset(bank[:, 0:3, 0:4 * T], 0.0).then_inc(sbank_zero, 1)
            for n in range(NT):
                dve.wait_ge(v_ps, n + 1)
                if n >= 4:
                    dve.wait_ge(vz_out[n % 4], 16 * (n // 4))
                dst = bass.AP(tensor=vz.tensor, offset=vz[:, n % 4, :, :].offset,
                              ap=[list(vz.ap[0]), [2 * DH, 6], [D + DH, 2], [1, DH]])
                dve.tensor_tensor(dst, bank[:, 6 + n % 2, 0:D].rearrange("p (g e d) -> p g e d", g=6, e=2),
                                  brow_bc("bv1").rearrange("p (g e d) -> p g e d", g=6, e=2), ALU.add).then_inc(vz_ready, 1)
            for k in range(4):
                dve.wait_ge(vz_out[k], 16 * len(range(k, NT, 4)))

            def v3(t):
                return t.rearrange("p (h j) -> p h j", j=T)

            def total(n):
                dve.wait_ge(s_exp, n + 1)
                dve.tensor_reduce(rs[0:100, n % 3, :], v3(sring[0:100, n % 3, :]), AX.X, ALU.add).then_inc(s_tot, 1)
                dve.wait_ge(s_tot, n + 1)
                dve.reciprocal(rs[0:100, n % 3, :], rs[0:100, n % 3, :]).then_inc(s_inv, 1)

            for n in range(PAIRS):
                dve.wait_ge(s_ps, n + 1)
                dve.wait_ge(c_in[n // 2 % 2], 32 * (n // 4 + 1))
                if n >= 3:
                    dve.wait_ge(pt_ps, n - 2)
                dve.tensor_tensor(sring[0:100, n % 3, :].rearrange("p (g c) -> p g c", g=GQ), bank[0:100, 0:GQ, 0:4 * T],
                                  cring[0:100, n // 2 % 2, n % 2, :].rearrange("p (g c) -> p g c", g=GQ),
                                  ALU.add).then_inc(s_sum, 1)
                dve.wait_ge(s_sum, n + 1)
                dve.tensor_reduce(mx[0:100, n % 3, :], v3(sring[0:100, n % 3, :]), AX.X, ALU.max).then_inc(s_max, 1)
                if n:
                    total(n - 1)
            total(PAIRS - 1)

            steps = [0]

            def step(ins):
                steps[0] += 1
                ins.then_inc(dve_step, 1)

            def settle():
                dve.wait_ge(dve_step, steps[0])

            def moments(k, i, src):
                for j in range(TPR):
                    step(dve.bn_stats(stats[:, j, :], src[:, TPR * i + j, :]))
                settle()
                for j in range(TPR):
                    step(dve.bn_aggr(lnb[:, k, TPR * i + j, 0:2], stats[:, j, :]))
                settle()

            def lnv(k, i, c):
                return lnb[:, k, TPR * i:TPR * i + TPR, c]

            def centre(k, dst, src, n, c=2):
                return dve.tensor_scalar(dst, src, lnb[:, k, n, 0:1], lnb[:, k, n, c:c + 1], ALU.subtract, ALU.mult)

            def resid(i):
                for n in range(TPR * i, TPR * i + TPR):
                    dve.wait_ge(wo_ps, n + 1)
                    dve.wait_ge(hb_ready, n + 1)
                    dve.tensor_tensor(nat[:, n, :], bank[:, n % 2, 0:D], nat[:, n, :], ALU.add).then_inc(r_ready, 1)
                dve.wait_ge(r_ready, TPR * (i + 1))
                moments(0, i, nat)
                dve.tensor_scalar(lnv(0, i, 2), lnv(0, i, 1), EPS, None, ALU.add).then_inc(ln_var, 1)
                dve.tensor_scalar(lnv(0, i, 3), lnv(0, i, 1), 1.0 + EPS, EPS * EPS, ALU.mult, ALU.add).then_inc(ln_var, 1)

            def n_norm(i):
                dve.wait_ge(ln_rstd, i + 1)
                for n in range(TPR * i, TPR * i + TPR):
                    centre(0, norm[:, n, :], nat[:, n, :], n, 3).then_inc(n_ready, 1)
                dve.scalar_tensor_tensor(nb1[:, TPR * i:TPR * i + TPR], lnv(0, i, 0), -1.0, lnv(0, i, 2), ALU.mult,
                                         ALU.mult).then_inc(nb_ready, 1)

            dve.wait_ge(pt_ps, PAIRS)
            for i in range(GRID + 1):
                if i < GRID:
                    resid(i)
                if i:
                    n_norm(i - 1)
            dve.tensor_scalar(nbr[:, :], brs[:, :], -1.0, None, ALU.mult).then_inc(nbr_ready, 1)

            dve.wait_ge(v2_ready, NT)
            for e in range(2):
                ins = dve.tensor_scalar(zz[:, e, :], v2s[:, :, D], sidem[:, e:e + 1], None, ALU.mult)
            ins.then_inc(zz_ready, 1)
            dve.wait_ge(z_exp, 1)
            step(dve.tensor_scalar(rt[:, :], rt[:, :], 1.0, None, ALU.add))
            settle()
            step(dve.reciprocal(sc[:, :].rearrange("p (n e) -> p e n", e=2), rt[:, :].rearrange("p (e n) -> p e n", e=2)))
            settle()
            inner = sc[:, :].unsqueeze(1).to_broadcast([P, T, T])
            outer = sc[:, :].unsqueeze(2).to_broadcast([P, T, T])
            step(dve.tensor_tensor(less, inner, outer, ALU.is_lt))
            step(dve.tensor_tensor(same, inner, outer, ALU.is_equal))
            step(dve.tensor_reduce(rsum[:, 0:1], sc[:, :], AX.X, ALU.add))
            settle()
            dve.wait_ge(s_low, 16)
            step(dve.tensor_tensor(same, same, lows, ALU.mult))
            step(dve.tensor_scalar(rsum[:, 1:2], rsum[:, 0:1], 1e-6, None, ALU.add))
            settle()
            step(dve.tensor_tensor(less, less, same, ALU.add))
            step(dve.reciprocal(rsum[:, 0:1], rsum[:, 1:2]))
            settle()
            step(dve.tensor_reduce(rt[:, :], less, AX.X, ALU.add))
            step(dve.tensor_scalar(oh[:, NSEL, :], sc[:, :], rsum[:, 0:1], None, ALU.mult))
            settle()
            for k in range(NSEL):
                step(dve.tensor_scalar(oh[:, k, :], rt[:, :], float(k), None, ALU.is_equal))
            settle()
            for e in range(2):
                lo, hi = 64 * e, 64 * e + 64
                step(dve.tensor_copy(own[lo:hi, 0, :], sc[lo:hi, e:T:2]))
                step(dve.tensor_scalar(own[lo:hi, 1, :], rt[lo:hi, e:T:2], float(NSEL), None, ALU.is_ge))
                step(dve.tensor_copy(gsl[lo:hi, :, :], oh[lo:hi, :, e:T:2]))
            step(dve.tensor_copy(ohs[0:64, :, :], oh[0:64, 0:NSEL:2, :]))
            step(dve.tensor_copy(ohs[64:128, 0:2, :], oh[64:128, 1:4:2, :]))
            step(dve.memset(ohs[64:128, 2, :], 0.0))
            settle()
            step(dve.tensor_reduce(wsum[:, :], gsl[:, NSEL, :], AX.X, ALU.add))
            settle()
            dve.tensor_scalar(wdiag, ident2[:, 0:B], wsum[:, 0:1], None, ALU.mult).then_inc(oh_ready, 1)
            dve.memset(qe[:, :, :, 30:32], 0.0).then_inc(qe_ready, 1)

            dve.wait_ge(d_used, NT)
            for m in range(2):
                dve.tensor_scalar(gt[:, m, 0:NSEL, :], bank[0:HALF, 4 + m, 0:NSEL * B].rearrange("p (s b) -> p s b", b=B),
                                  fcol("g1", m), fcol("b1", m), ALU.mult, ALU.add).then_inc(g_ready, 1)
            step(dve.tensor_copy(gt[:, :, SLOT, :], bank[0:HALF, 4:6, SLOT * B:(SLOT + 1) * B]))
            settle()
            for m in range(2):
                step(dve.scalar_tensor_tensor(gt[:, m, NSEL, :], bank[0:HALF, 4 + m, NSEL * B:SLOT * B], fcol("g1", m),
                                              gt[:, m, SLOT, :], ALU.mult, ALU.add))
            settle()
            dve.tensor_copy(gt[:, :, SLOT, :], gt[:, :, NSEL, :]).then_inc(pg_ready, 1)
            dve.wait_ge(q2_sb, 2)
            for k in range(6):
                dve.tensor_scalar(qe[:, :, :, NSEL * k:NSEL * k + NSEL].rearrange("p m b s -> p m s b"), qs[:, :, :, :],
                                  hmask[:, k:k + 1], None, ALU.mult).then_inc(qe_ready, 1)
            dve.wait_ge(pm_ps, 1)
            dve.tensor_copy(pm, bank[:, 3, 0:D]).then_inc(pm_ready, 1)

            for k in range(3):
                n0, n1 = 12 * k, min(12 * k + 12, PAIRS)
                raw = bank[:, k, 0:(n1 - n0) * T].rearrange("p (n j) -> p n j", j=T)
                dve.wait_ge(l2_ps, k + 1)
                step(dve.tensor_reduce(mx2[:, 0, n0:n1], raw, AX.X, ALU.max))
                settle()
                dve.tensor_tensor(s2[:, n0:n1, :], raw, mx2[:, 0, n0:n1].unsqueeze(2).to_broadcast([P, n1 - n0, T]),
                                  ALU.subtract).then_inc(l2_cent, 1)
            for k in range(3):
                n0, n1 = 12 * k, min(12 * k + 12, PAIRS)
                dve.wait_ge(l2_exp, k + 1)
                step(dve.tensor_reduce(mx2[:, 1, n0:n1], s2[:, n0:n1, :], AX.X, ALU.add))
                settle()
                step(dve.reciprocal(mx2[:, 1, n0:n1], mx2[:, 1, n0:n1]))
                settle()
                if k == 0:
                    dve.wait_ge(sx_zero, 1)
                for ib in range(2):
                    p0, p1 = 64 * ib, 64 * ib + 64
                    dve.tensor_tensor(s2x[p0:p1, n0:n1, p0:p0 + T], s2[p0:p1, n0:n1, :],
                                      mx2[p0:p1, 1, n0:n1].unsqueeze(2).to_broadcast([64, n1 - n0, T]),
                                      ALU.mult).then_inc(l2_ready, 1)
            for k in range(PAIRS // 4):
                dve.wait_ge(c2_ps, k + 1)
                step(dve.tensor_tensor(otmp[:, k % 2, :, :].rearrange("p n (h s) -> p n h s", s=NSEL),
                                       bank[0:HALF, 6 + k % 2, :].rearrange("p (n c) -> p n c", c=32)[:, :, 0:30].rearrange("p n (h s) -> p n h s", s=NSEL),
                                       hmask.unsqueeze(1).unsqueeze(3).to_broadcast([HALF, 16, 6, NSEL]), ALU.mult))
                settle()
                for m in range(2):
                    ins = dve.tensor_reduce(o2t[:, m, :, 8 * k:8 * k + 8].rearrange("p s b -> p b s"),
                                            otmp[:, k % 2, 8 * m:8 * m + 8, :].rearrange("p n (h s) -> p n s h", s=NSEL),
                                            AX.X, ALU.add)
                    ins.then_inc(c2_ready, 1)
            dve.wait_ge(c2_ready, PAIRS // 2)
            for m in range(2):
                o = o2t[:, m, :, :].rearrange("p s b -> p (s b)")
                dve.tensor_scalar(o, o, fcol("bv2", m), None, ALU.add).then_inc(ctx_ready, 1)
            dve.memset(asel[64:128, 2, :], 0.0).then_inc(as_ready, 1)
            for k in range(3):
                rows = P if k < 2 else B
                dve.wait_ge(as_ps, k + 1)
                dve.tensor_tensor(asel[0:rows, k, :], bank[0:rows, 3 + k, 0:D], brow_bc("bo2")[0:rows, :], ALU.add).then_inc(as_ready, 1)

            def merged(i):
                tiles = range(TPR * i, TPR * i + TPR)
                dve.wait_ge(mb_ready, TPR * (i + 1))
                dve.wait_ge(h1_ready, TPR * (i + 1))
                for n in tiles:
                    step(dve.scalar_tensor_tensor(mrg[:, 0, n % TPR, :], pm, own[:, 0, n:n + 1], mixed[:, n, :], ALU.mult, ALU.add))
                settle()
                for n in tiles:
                    step(dve.scalar_tensor_tensor(mrg[:, 1, n % TPR, :], mrg[:, 0, n % TPR, :], own[:, 1, n:n + 1], nat[:, n, :],
                                                  ALU.mult, ALU.add))
                settle()
                for n in tiles:
                    dve.wait_ge(mg_ps, n + 1)
                    dve.tensor_tensor(norm[:, n, :], bank[:, n % 2, 0:D], mrg[:, 1, n % TPR, :], ALU.add).then_inc(h2_ready, 1)
                dve.wait_ge(h2_ready, TPR * (i + 1))
                moments(1, i, norm)
                dve.tensor_scalar(lnv(1, i, 2), lnv(1, i, 1), EPS, None, ALU.add).then_inc(ln2_var, 1)

            def n2_norm(i):
                dve.wait_ge(ln2_rstd, i + 1)
                if i >= 2:
                    dve.wait_ge(n2_ps, i - 1)
                for n in range(TPR * i, TPR * i + TPR):
                    centre(1, mrg[:, 2 + i % 2, n % TPR, :], norm[:, n, :], n).then_inc(n2_ready, 1)

            def final(i):
                for n in range(TPR * i, TPR * i + TPR):
                    dve.wait_ge(f2_ps, n + 1)
                    dve.wait_ge(res_ready, n + 1)
                    dve.tensor_tensor(nat[:, n, :], bank[:, 6 + n % 2, 0:D], nat[:, n, :], ALU.add).then_inc(y_ready, 1)
                dve.wait_ge(y_ready, TPR * (i + 1))
                moments(2, i, nat)
                dve.tensor_scalar(lnv(2, i, 2), lnv(2, i, 1), EPS, None, ALU.add).then_inc(ln3_var, 1)

            def out_norm(i):
                dve.wait_ge(ln3_rstd, i + 1)
                for n in range(TPR * i, TPR * i + TPR):
                    centre(2, nat[:, n, :], nat[:, n, :], n).then_inc(y_out, 1)

            for i in range(GRID + 2):
                if i < GRID:
                    merged(i)
                    n2_norm(i)
                if i >= 2:
                    final(i - 2)
                    out_norm(i - 2)

        @block.scalar
        def _(act):
            for k in range(2):
                load_x(act, k)
            act.dma_start(cs[:, :], cst).then_inc(s_cst, 16)
            act.wait_ge(pads_left, 1)
            act.wait_ge(pads_right, 1)

            def squares(r):
                act.wait_ge(s_x[(r + 1) // 2], 32)
                if r >= 2:
                    act.wait_ge(rsq_ready, r - 1)
                act.activation(sq[:, r % 2, :, :].rearrange("p c q -> p (c q)"),
                               xs[:, r, :, :, :].rearrange("p c q b -> p (c q b)"), ACT.Square).then_inc(sq_ready, 1)

            for r in range(3):
                squares(r)
            for i in range(GRID + 1):
                for r in (2 * i + 3, 2 * i + 4):
                    if r < NB:
                        squares(r)
                if i:
                    for n in range(TPR * (i - 1), TPR * i):
                        act.wait_ge(htr_ps, n + 1)
                        act.copy(ht[:, :, n * P:(n + 1) * P],
                                 bank[0:HALF, 6 + n % 2, 0:2 * P].rearrange("p (m c) -> p m c", m=2)).then_inc(ht_ready, 1)
            for i in range(GRID):
                for m in range(2):
                    act.wait_ge(qk_ps, 4 * i + 1 + m)
                    act.activation(qt[:, m, GRID * i:GRID * i + GRID, :],
                                   bank[0:HALF, (4 * i + m) % 6, 0:CHUNK].rearrange("p (t b) -> p t b", b=B),
                                   ACT.Identity, bias=colb[:, m:m + 1]).then_inc(q_ready, 1)
            for jp in range(T // 2):
                act.wait_ge(p2c_ps, jp + 1)
                w = bank[0:64, jp % 4, 0:H * WIN].rearrange("p (h w) -> p h w", w=WIN)
                act.copy(cmat[:, :, :, 2 * jp].rearrange("p i h -> p h i"), w[:, :, 1:1 + T]).then_inc(p2c_act, 1)
            for n in range(NT):
                act.wait_ge(vz_ready, n + 1)
                act.dma_start(vd[n * P:(n + 1) * P, :], vz[:, n % 4, :, :].rearrange("p e o -> p (e o)")).then_inc(vz_out[n % 4], 16)

            def pt_copy(n):
                act.wait_ge(pt_ps, n + 1)
                if n >= 2:
                    act.wait_ge(o_ps, n - 1)
                b0 = 3 + 2 * (n % 2)
                act.copy(ptr[:, n % 2, :, :].rearrange("p (a k) c -> p a (k c)", a=2),
                         bank[0:2 * T, b0:b0 + 2, 0:300]).then_inc(pt_sb, 1)

            def o_copy(n):
                act.wait_ge(o_ps, n + 1)
                act.copy(ot[:, :, :, 2 * n:2 * n + 2].rearrange("p m t b -> p m b t"),
                         bank[0:HALF, 7, 0:4 * T].rearrange("p (m b t) -> p m b t", m=2, b=2)).then_inc(o_sb, 1)

            act.wait_ge(v_ps, NT)
            act.wait_ge(bd_ready, 4)
            for n in range(PAIRS + 3):
                if n < PAIRS:
                    act.wait_ge(s_sub, n + 1)
                    act.activation(sring[0:100, n % 3, :], sring[0:100, n % 3, :], ACT.Exp,
                                   scale=float((3 * DH) ** -0.5)).then_inc(s_exp, 1)
                if 0 <= n - 2 < PAIRS:
                    pt_copy(n - 2)
                if n >= 3:
                    o_copy(n - 3)

            def router_exp():
                act.wait_ge(z_ps, 1)
                act.wait_ge(nbr_ready, 1)
                act.activation(rt[:, :], bank[:, 6, 0:T], ACT.Exp, scale=-1.0, bias=nbr[:, :]).then_inc(z_exp, 1)

            def turned(i, ps_ready, sb_ready, b, gain, shift):
                act.wait_ge(ps_ready, i + 1)
                for m in range(2):
                    act.activation(nt_[:, m, i * CHUNK:(i + 1) * CHUNK], bank[0:HALF, b + m, 0:CHUNK], ACT.Identity,
                                   scale=fcol(gain, m), bias=fcol(shift, m)).then_inc(sb_ready, 1)

            for i in range(GRID):
                turned(i, n_ps, nt_ready, 4 + 2 * (i % 2), "g1", "b1")
                act.wait_ge(nb_ready, i + 1)
                for n in range(TPR * i, TPR * i + TPR):
                    act.activation(nat[:, n, :], nat[:, n, :], ACT.Identity, scale=lnb[:, 0, n, 2:3],
                                   bias=nb1[:, n:n + 1]).then_inc(h1_ready, 1)
                for n in range(TPR * i, TPR * i + TPR):
                    act.wait_ge(v2_ps, n + 1)
                    act.copy(v2s[:, n, :], bank[:, 2 + n % 2, 0:D + 1]).then_inc(v2_ready, 1)
            for u in range(2 * GRID):
                i, m = u // 2, u % 2
                act.wait_ge(k2_ps, u + 1)
                act.activation(ktf[:, m, i * CHUNK:(i + 1) * CHUNK], bank[0:HALF, u % 2, 0:CHUNK], ACT.Identity,
                               bias=fcol("bk2", m)).then_inc(k2_ready, 1)
                if u == 3:
                    router_exp()
            for n in range(NT):
                act.wait_ge(x2_ps, n + 1)
                act.copy(mixed[:, n, :], bank[:, 2 + n % 2, 0:D]).then_inc(x2_ready, 1)
            for m in range(2):
                act.wait_ge(q2_ps, m + 1)
                act.activation(qs[:, m, :, :].rearrange("p s b -> p (s b)"), bank[0:HALF, 6 + m, 0:NSEL * B], ACT.Identity,
                               bias=fcol("bq2", m)).then_inc(q2_sb, 1)
            for k in range(3):
                n0, n1 = 12 * k, min(12 * k + 12, PAIRS)
                act.wait_ge(l2_cent, k + 1)
                act.activation(s2[:, n0:n1, :], s2[:, n0:n1, :], ACT.Exp, scale=float(DH ** -0.5)).then_inc(l2_exp, 1)
            for k in range(PAIRS // 4):
                act.wait_ge(t2_ps, k + 1)
                if k >= 2:
                    act.wait_ge(c2_ps, k - 1)
                act.copy(pt2[:, k % 2, :, :].rearrange("p n c -> p (n c)"), bank[0:W2X, 4 + k % 2, :]).then_inc(t2_ready, 1)
            for i in range(GRID):
                turned(i, n2_ps, n2t_ready, 2, "g2", "b2")
                for k in range(FF // P):
                    u = 6 * i + k
                    act.wait_ge(f1_ps, u + 1)
                    act.activation(hid[:, i % 3, k, :], bank[:, 4 + u % 2, 0:CHUNK], ACT.Gelu,
                                   bias=bf1s[:, k:k + 1]).then_inc(f1_ready, 1)

        @block.gpsimd
        def _(pool):
            def rstd_tok(i):
                pool.wait_ge(tvar, i + 1)
                pool.tensor_tensor(rst[:, :], st[:, 3 * TPR:4 * TPR], nhalf[:, 0:TPR], ALU.pow).then_inc(trstd, 1)

            pool.memset(ones[:, :], 1.0).then_inc(ones_set, 1)
            pool.memset(nhalf[:, :], -0.5).then_inc(nhalf_set, 1)
            pool.wait_ge(ones_set, 1)
            pool.wait_ge(nhalf_set, 1)
            pool.memset(xs[64:128, :, :, NQ - 1, :].rearrange("p r c b -> p (r c) b"), 0.0).then_inc(pads_right, 1)
            pool.wait_ge(pads_right, 1)

            def beta_w():
                pool.wait_ge(wg_ready, 8)
                pool.wait_ge(wc_ready, 4)
                pool.wait_ge(s_gb, 32)
                pool.tensor_tensor(wraw, wraw, bets[:, :].unsqueeze(2).to_broadcast([P, WRAW, D]), ALU.mult).then_inc(wb_ready, 1)
            for i in range(GRID):
                pool.wait_ge(rsq_ready, min(2 * i + 3, NB))
                if i >= 2:
                    pool.wait_ge(ss_ready, i - 1)
                pool.tensor_tensor(esum[i % 2], rsq[:, 2 * i % 6, :], rsq[:, (2 * i + 1) % 6, :], ALU.add).then_inc(esum_set, 1)
                outer = [r for r in (2 * i - 1, 2 * i + 2) if 0 <= r < NB]
                if len(outer) == 2:
                    pool.tensor_tensor(usum[i % 2], rsq[:, outer[0] % 6, :], rsq[:, outer[1] % 6, :], ALU.add).then_inc(esum_set, 1)
                    pool.wait_ge(esum_set, 2 * i + 1)
                    pool.tensor_tensor(usum[i % 2], usum[i % 2], esum[i % 2], ALU.add).then_inc(eu_ready, 1)
                else:
                    pool.wait_ge(esum_set, max(2 * i, 1))
                    pool.tensor_tensor(usum[i % 2], rsq[:, outer[0] % 6, :], esum[i % 2], ALU.add).then_inc(eu_ready, 1)
                if i == 0:
                    beta_w()
                else:
                    rstd_tok(i - 1)
            rstd_tok(GRID - 1)

            for n in range(PAIRS + 1):
                if n < PAIRS:
                    pool.wait_ge(s_max, n + 1)
                    sv = sring[0:100, n % 3, :].rearrange("p (h j) -> p h j", j=T)
                    pool.tensor_tensor(sv, sv, mx[0:100, n % 3, :].unsqueeze(2).to_broadcast([100, H, T]),
                                       ALU.subtract).then_inc(s_sub, 1)
                if n:
                    k = n - 1
                    pool.wait_ge(s_inv, k + 1)
                    sv = sring[0:100, k % 3, :].rearrange("p (h j) -> p h j", j=T)
                    pool.tensor_tensor(sv, sv, rs[0:100, k % 3, :].unsqueeze(2).to_broadcast([100, H, T]),
                                       ALU.mult).then_inc(s_nrm, 1)
                if n < NT:
                    pool.tensor_tensor(nat[:, n, :], nat[:, n, :], brow_bc("bo1"), ALU.add).then_inc(hb_ready, 1)

            def rstd(k, i, var_ready, rstd_ready):
                pool.wait_ge(var_ready, i + 1)
                pool.tensor_tensor(lnb[:, k, TPR * i:TPR * i + TPR, 2], lnb[:, k, TPR * i:TPR * i + TPR, 2], nhalf[:, 0:TPR],
                                   ALU.pow).then_inc(rstd_ready, 1)

            for i in range(GRID):
                pool.wait_ge(ln_var, 2 * (i + 1))
                v = lnb[:, 0, TPR * i:TPR * i + TPR, 2:4]
                pool.tensor_tensor(v, v, nhalf[:, :].rearrange("p (n c) -> p n c", c=2), ALU.pow).then_inc(ln_rstd, 1)
            pool.wait_ge(ln_rstd, GRID)
            pool.memset(vj[32:64, :, :], 0.0).then_inc(vj_zero, 1)
            pool.wait_ge(v2_out, 16 * GRID)
            pool.wait_ge(zz_ready, 1)
            pool.wait_ge(vj_zero, 1)
            pool.memset(s2x, 0.0).then_inc(sx_zero, 1)
            pool.wait_ge(oh_ready, 1)
            for n in range(NT):
                if n >= 3:
                    pool.wait_ge(d_used, n - 2)
                pool.tensor_tensor(dring[:, n % 3, :, :], gsl[:, :, n:n + 1].to_broadcast([P, SLOT, B]),
                                   ident2[:, 0:B].unsqueeze(1).to_broadcast([P, SLOT, B]), ALU.mult).then_inc(d_ready, 1)
            for n in range(NT):
                pool.wait_ge(x2_ready, n + 1)
                pool.tensor_tensor(mixed[:, n, :], mixed[:, n, :], brow_bc("bm"), ALU.add).then_inc(mb_ready, 1)
            pool.wait_ge(l2_ps, 3)

            def spread(n):
                if n >= 6:
                    pool.wait_ge(mg_ps, n - 5)
                pool.tensor_tensor(dtr[:, n % 6, :, :].rearrange("p k (e b) -> p k e b", e=2),
                                   ident2.rearrange("p (e b) -> p e b", e=2).unsqueeze(1).to_broadcast([P, 3, 2, B]),
                                   ohs[:, :, 2 * n:2 * n + 2].unsqueeze(3).to_broadcast([P, 3, 2, B]), ALU.mult).then_inc(dt_ready, 1)

            def residual(n):
                pool.wait_ge(h2_ready, n + 1)
                pool.tensor_tensor(nat[:, n, :], nat[:, n, :], norm[:, n, :], ALU.add).then_inc(res_part, 1)
                pool.wait_ge(res_part, n + 1)
                pool.tensor_tensor(nat[:, n, :], nat[:, n, :], brow_bc("bf2"), ALU.add).then_inc(res_ready, 1)

            for n in range(2 * TPR):
                spread(n)
            for i in range(GRID + 2):
                if i < GRID:
                    rstd(1, i, ln2_var, ln2_rstd)
                if i >= 2:
                    rstd(2, i - 2, ln3_var, ln3_rstd)
                if i < GRID:
                    for n in range(TPR * i, TPR * i + TPR):
                        residual(n)
                    for n in range(TPR * (i + 2), min(TPR * (i + 3), NT)):
                        spread(n)


def kernel(**a):
    import numpy as np
    import concourse.bacc as bacc
    from concourse.bass_utils import run_bass_kernel_spmd

    x = a["x"].reshape(B, CH, NB, 8, NQ - 1, 2, 8)
    xh = np.stack([x[:, :, :, :, :, 1, :], x[:, :, :, :, :, 0, :]]).transpose(0, 4, 6, 3, 2, 5, 1)
    xh = xh.reshape(P, NB, CH, NQ - 1, B)

    def pack(w):
        o = w.shape[0]
        w = w.reshape(o, 2, 8, 2, 8, 5, CH)
        quad = {(0, 0): 1, (0, 1): 3, (1, 0): 4, (1, 1): 2}
        chunks = []
        for r in range(4):
            for s in range(2):
                q = w[:, r % 2, :, :, :, quad[(r // 2, s)], :]
                chunks.append(q.transpose(2, 1, 3, 4, 0).reshape(P, CH, o))
        for r in range(2):
            q = w[:, r, :, ::-1, :, 0, :]
            chunks.append(q.transpose(2, 1, 3, 4, 0).reshape(P, CH, o))
        return np.concatenate(chunks, axis=1)

    def split(w):
        return w.reshape(2, HALF, -1).transpose(1, 0, 2)

    A, F = "L0_attn_", "L0_ffn_"
    rel = a[A + "rel_table"][127 - (T - 1):127 + T]
    consts = np.zeros((P, 2 * P + 10), np.float32)
    p = np.arange(P)
    consts[:, 0:P] = np.eye(P)
    consts[:, P:2 * P] = p[:, None] % 64 == p[None, :] % 64
    consts[:, 2 * P:2 * P + 6] = (p[:, None] // DH) % 8 == np.arange(6)[None, :]
    consts[:, 2 * P + 6:2 * P + 8] = (p[:, None] // DH) % 2 == np.arange(2)[None, :]
    consts[:, 2 * P + 8] = p < 64
    consts[:, 2 * P + 9] = p >= 64
    t = np.arange(T)
    rows = {"tok_b": "L0_tok_b", "bv1": A + "bv", "bo1": A + "bo", "b1": F + "b1",
            "bm": F + "bm", "bo2": F + "bo", "bf2": F + "bf2"}
    by_feature = {"bq1": A + "bq", "bk1": A + "bk", "bpk": A + "bpk", "bpq": A + "bpq", "bq2": F + "bq", "bk2": F + "bk",
                  "g1": F + "g1", "b1": F + "b1", "g2": F + "g2", "b2": F + "b2", "bv2": F + "bv"}
    arrays = {
        "x": xh,
        "wtok": pack(a["L0_tok_W"]),
        "gam": pack(a["L0_tok_ln_gamma"].reshape(1, PDIM))[:, :, 0],
        "bet": pack(a["L0_tok_ln_beta"].reshape(1, PDIM))[:, :, 0],
        "watt": np.stack([split(a[A + n]) for n in ("Wq", "Wk", "Wv", "Wo", "Wpk", "Wpq")], axis=1),
        "relt": np.stack([split(rel[::-1].T), split(rel.T)], axis=1),
        "wffn": np.concatenate([split(a[F + n]) for n in ("Wq", "Wk", "Wv", "Wr", "Wo", "Wm", "W1")], axis=2),
        "w2": a[F + "W2"].reshape(FF // P, P, D).transpose(1, 0, 2),
        "brow": np.stack([a[rows[n]] for n in BIAS_ROWS]),
        "col": np.concatenate([a[by_feature[n]].reshape(2, HALF).T for n in COLS], axis=1),
        "bf1": a[F + "bf1"].reshape(FF // P, P).T,
        "br": a[F + "br"].reshape(1, 1),
        "cst": consts,
        "lower": (t[None, :] < t[:, None]).astype(np.float32).reshape(1, T, T),
    }
    nc = bacc.Bacc("TRN2", target_bir_lowering=False, num_devices=1)
    args, feed = [], {}
    for name, v in arrays.items():
        feed[f"in_{name}"] = np.ascontiguousarray(v)
        args.append(nc.dram_tensor(f"in_{name}", feed[f"in_{name}"].shape, F32, kind="ExternalInput").ap())
    args.append(nc.dram_tensor("out_0", (B, T, D), F32, kind="ExternalOutput").ap())
    build(nc, *args)
    r = run_bass_kernel_spmd(nc, [feed], core_ids=[0])
    return r.results[0]["out_0"]
```

```python
from contextlib import ExitStack

import concourse.bass as bass
from concourse import mybir

F32 = mybir.dt.float32
ALU = mybir.AluOpType
ACT = mybir.ActivationFunctionType
AX = mybir.AxisListType

P = 128
B = 64
GRID = 6
T = GRID * GRID
D = 192
HALF = D // 2
H = 12
DH = D // H
FF = 4 * D
CH = 3
PATCH = 16
PDIM = PATCH * PATCH * 5 * CH
EPS = 1e-5
NT = B * T // P
TPR = NT // GRID
TOK = B * T
CHUNK = TPR * P
REL = 2 * T - 1
WIN = T + 1
NB = 12
NQ = NB // 2 + 1
ROW = CH * NQ * B
QW = NQ * B
GQ = 3
NR = 4
H3 = 3
GW = H3 * DH
OROWS = 64 + GW
HT_COLS = H * T
PAIRS = B // 2
NSEL = 5
SLOT = NSEL + 1
BIAS_ROWS = ["tok_b", "bv1", "bo1", "b1", "bm", "bo2", "bf2"]
COLS = ["bq1", "bk1", "bpk", "bpq", "bq2", "bk2", "g1", "b1", "g2", "b2", "bv2"]
NMIX, NMIX2 = 9, 14
WCH = 24
WRAW = WCH + 6


def build(nc, x, wtok, gam, bet, watt, wout, relt, wffn, w2, brow, col, bf1, br, cst, lower, out):
    with ExitStack() as ctx:
        def sb(name, shape):
            return ctx.enter_context(nc.sbuf_tensor(name, shape, F32))

        def sem(name):
            return ctx.enter_context(nc.semaphore(name))

        ax = sb("arena_x", [P, NB * ROW])
        aqk = sb("arena_qk", [P, 6 * TOK + 2])
        aht = sb("arena_ht", [OROWS, 2 * TOK])
        nat = sb("nat", [P, NT, D])
        ann = sb("arena_nn", [P, NT * D])
        arg = sb("arena_ring", [P, 2 * ROW + 48])
        wat = sb("wat", [HALF, 5, 2, D])
        wos = sb("wos", [OROWS, 2, D])
        bdt = sb("bdt", [HALF, 2, 2, 6, REL])
        bias = sb("bias", [P, len(BIAS_ROWS), D])
        cs = sb("cs", [P, 2 * P + 6 + 2 + 2 + 1 + T])
        colb = sb("colb", [HALF, 2 * len(COLS)])
        bf1s = sb("bf1s", [P, FF // P])
        brs = sb("brs", [P, 1])
        st = sb("st", [P, 128])

        ident = cs[:, 0:P]
        ident2 = cs[:, P:2 * P]
        hmask = cs[0:HALF, 2 * P:2 * P + 6]
        emask = cs[0:HALF, 2 * P + 6:2 * P + 8]
        sidem = cs[:, 2 * P + 8:2 * P + 10]

        imgc = cs[:, 2 * P + 10:2 * P + 11]
        rowc = cs[:, 2 * P + 11:2 * P + 11 + T]

        def brow_bc(name):
            return bias[:, BIAS_ROWS.index(name), :]

        def fcol(name, m):
            k = 2 * COLS.index(name) + m
            return colb[:, k:k + 1]

        xs = ax[:, :].rearrange("p (r c q b) -> p r c q b", r=NB, c=CH, q=NQ)
        wraw = aqk[:, 0:WRAW * D].rearrange("p (k o) -> p k o", o=D)
        o0 = WRAW * D
        wg = aqk[:, o0:o0 + WCH * (D + 1)].rearrange("p (a s c o) -> p a s c o", a=4, s=2, c=CH)
        wgf = aqk[:, o0:o0 + WCH * (D + 1)].rearrange("p (k o) -> p k o", o=D + 1)
        o0 += WCH * (D + 1)
        wgc = aqk[:, o0:o0 + 6 * D].rearrange("p (a c o) -> p a c o", a=2, c=CH)
        o0 += 6 * D
        esum = [aqk[:, o0 + 2 * k * QW:o0 + (2 * k + 1) * QW] for k in range(2)]
        usum = [aqk[:, o0 + (2 * k + 1) * QW:o0 + (2 * k + 2) * QW] for k in range(2)]
        side1 = aqk[:, o0 + 4 * QW:o0 + 5 * QW]
        assert o0 + 5 * QW <= 6 * TOK
        gams = sb("gams", [P, WRAW])
        bets = sb("bets", [P, WRAW])
        rsq = ann[:, 0:6 * QW].rearrange("p (s q) -> p s q", s=6)
        ssum = ann[:, 6 * QW:6 * QW + 2 * CHUNK].rearrange("p (s c) -> p s c", s=2)
        sq = arg[:, 0:2 * ROW].rearrange("p (s c q) -> p s c q", s=2, c=CH)
        swb = sb("swb", [P, D])
        cb = sb("cb", [P, D])
        red = sb("red", [P, 2, D])
        ones = sb("ones", [P, P])

        ht = aht[0:HALF, :].rearrange("p (m t) -> p m t", m=2)
        qt = aqk[0:HALF, 0:2 * TOK].rearrange("p (m t b) -> p m t b", m=2, t=T)
        ke = aqk[0:HALF, 2 * TOK:6 * TOK].rearrange("p (m e t b) -> p m e t b", m=2, e=2, t=T)
        cmat = ax[0:B, 0:T * HT_COLS].rearrange("p (i h j) -> p i h j", i=T, j=T)
        vn = ann[:, 4 * HT_COLS:4 * HT_COLS + 9 * D].rearrange("p (n o) -> p n o", o=D)
        cring = ann[:, 0:4 * HT_COLS].rearrange("p (s n c) -> p s n c", s=2, n=2)
        sring = ann[:, 4 * HT_COLS:8 * HT_COLS].rearrange("p (s c) -> p s c", s=NR)
        ptr = arg[:, 0:800].rearrange("p (s k c) -> p s k c", s=2, k=4)
        vbd = arg[:, 1200:1200 + 8 * D].rearrange("p (s n o) -> p s n o", s=2, n=4)
        ot = aht[:, :].rearrange("p (m t b) -> p m t b", m=2, t=T)
        relts = arg[0:HALF, 0:4 * REL].rearrange("p (v m r) -> p v m r", v=2, m=2)
        pks = arg[0:HALF, 4 * REL:8 * REL].rearrange("p (v m r) -> p v m r", v=2, m=2)
        mx = st[:, 64:64 + NR * H].rearrange("p (s h) -> p s h", s=NR)
        rs = sb("rs", [P, NR, H])
        stats = sb("stats", [P, TPR, 6])
        mv = sb("mv", [P, TPR, 2])
        nhalf = sb("nhalf", [P, 2 * TPR])
        rst = sb("rst", [P, TPR])

        norm = ann[:, :].rearrange("p (n o) -> p n o", o=D)
        nt_ = ht
        kt = aqk[0:HALF, 2 * TOK:4 * TOK].rearrange("p (m t b) -> p m t b", m=2, t=T)
        ktf = aqk[0:HALF, 2 * TOK:4 * TOK].rearrange("p (m t) -> p m t", m=2)
        FFC = 5 * D + 1 + FF
        wf = aqk[0:HALF, 4 * TOK:4 * TOK + 2 * FFC].rearrange("p (m o) -> p m o", m=2)
        w2s = aqk[:, 4 * TOK + 2 * FFC:6 * TOK + 2].rearrange("p (k o) -> p k o", o=D)
        WQ, WK, WV, WO, WM, W1 = 0, D, 2 * D, 3 * D + 1, 4 * D + 1, 5 * D + 1
        less = aqk[:, 0:T * T].rearrange("p (t u) -> p t u", u=T)
        same = aqk[:, T * T:2 * T * T].rearrange("p (t u) -> p t u", u=T)
        lows = aqk[:, 2 * T * T:3 * T * T].rearrange("p (t u) -> p t u", u=T)
        qe = aqk[0:HALF, 0:2 * B * 32].rearrange("p (m b c) -> p m b c", m=2, c=32)
        pwd = arg[:, 0:NT * B].rearrange("p (n b) -> p n b", b=B)
        o1 = NT * B
        s2 = arg[:, 0:PAIRS * T].rearrange("p (n j) -> p n j", j=T)
        assert PAIRS * T <= o1
        o2t = arg[0:HALF, o1:o1 + 2 * NSEL * B].rearrange("p (m s b) -> p m s b", m=2, b=B)
        o1 += 2 * NSEL * B
        asel = arg[:, o1:o1 + 3 * D].rearrange("p (s o) -> p s o", o=D)
        gsb = asel
        o1 += 3 * D
        pm = arg[:, o1:o1 + D]
        o1 += D
        wdiag = arg[:, o1:o1 + B]
        o1 += B
        assert o1 <= 2 * ROW + 48
        mixed = ax[:, 0:NT * D].rearrange("p (n o) -> p n o", o=D)
        o2 = NT * D
        hid = ax[:, o2:o2 + 3 * FF // P * CHUNK].rearrange("p (s k t) -> p s k t", s=3, t=CHUNK)
        v2s = ax[:, o2:o2 + NT * (D + 1)].rearrange("p (n o) -> p n o", o=D + 1)
        W2X = 64 + T
        s2x = ax[:, o2:o2 + PAIRS * W2X].rearrange("p (n j) -> p n j", j=W2X)
        o2 += NT * (D + 1)
        vj = ax[0:W2X, o2:o2 + PAIRS * D].rearrange("p (b o) -> p b o", o=D)
        o2 += PAIRS * D
        gt = ax[0:HALF, o2:o2 + 2 * (SLOT + 1) * B].rearrange("p (m s b) -> p m s b", m=2, b=B)
        o2 += 2 * (SLOT + 1) * B
        qs = ax[0:HALF, o2:o2 + 2 * NSEL * B].rearrange("p (m s b) -> p m s b", m=2, b=B)
        o2 += 2 * NSEL * B
        pt2 = ax[0:W2X, o2:o2 + 2 * 4 * P].rearrange("p (s n c) -> p s n c", s=2, n=4)
        assert o2 + 8 * P <= NB * ROW
        otmp = aqk[0:HALF, 12 * D:12 * D + 960].rearrange("p (s n c) -> p s n c", s=2, n=16)
        scr = aqk[:, 0:12 * D].rearrange("p (n o) -> p n o", o=D)
        mrg = aqk[:, 12 * D:12 * D + 4 * TPR * D].rearrange("p (v n o) -> p v n o", v=4, n=TPR)
        lnb = sb("lnb", [P, 3, NT, 4])
        nb1 = sb("nb1", [P, NT])
        wsum = sb("wsum", [P, 1])
        zz = sb("zz", [P, 2, NT])
        sc = sb("sc", [P, T])
        rt = sb("rt", [P, T])
        pw = sb("pw", [P, NT])
        rt2 = sb("rt2", [P, T])
        ohs = sb("ohs", [P, 3, T])
        idxf = sb("idxf", [P, 4])
        idx = ctx.enter_context(nc.sbuf_tensor("idx", [P, 4], mybir.dt.uint32))
        own = sb("own", [P, 2, NT])
        nbr = sb("nbr", [P, 1])
        mx2 = sb("mx2", [P, 2, PAIRS])
        rsum = sb("rsum", [P, 2])

        bank = ctx.enter_context(nc.psum_tensor("bank", [P, 8, 512], F32))

        vd = nc.dram_tensor("v_scratch", [TOK, D], F32, kind="Internal").ap()
        v2d = nc.dram_tensor("v2_scratch", [TOK, D], F32, kind="Internal").ap()
        nd = nc.dram_tensor("normed_scratch", [TOK, D], F32, kind="Internal").ap()
        sd = nc.dram_tensor("chosen_scratch", [TOK, D], F32, kind="Internal").ap()
        cd = nc.dram_tensor("c_scratch", [B, T, HT_COLS], F32, kind="Internal").ap()

        s_cst = sem("consts_in")
        s_w = [sem(f"wtok_in{k}") for k in range(5)]
        s_gb = sem("gamma_beta_in")
        s_x = [sem(f"x_in{k}") for k in range(7)]
        s_wat = sem("watt_in")
        s_rel = sem("rel_in")
        s_bias = sem("bias_in")
        pads_left = sem("pads_left")
        pads_right = sem("pads_right")
        ones_set = sem("ones_set")
        nhalf_set = sem("nhalf_set")
        wg_ready = sem("wg_ready")
        wc_ready = sem("wc_ready")
        wb_ready = sem("wb_ready")
        red_ready = sem("red_ready")
        swcb_ps = sem("swcb_ps")
        swb_ready = sem("swb_ready")
        sq_ready = sem("sq_ready")
        rsq_ready = sem("rsq_ready")
        eu_ready = sem("eu_ready")
        esum_set = sem("esum_set")
        ss_part = sem("window_squares_part")
        ss_ready = sem("window_squares_ready")
        tok_ps = sem("tok_ps")
        tstat = sem("tstat")
        tvar = sem("tvar")
        trstd = sem("trstd")
        tcent = sem("tcent")
        h_ready = sem("h_ready")
        htr_ps = sem("htr_ps")
        ht_ready = sem("ht_ready")
        pk_ps = sem("pk_ps")
        pk_sb = sem("pk_sb")
        bd_ready = sem("bd_ready")
        qk_ps = sem("qk_ps")
        q_ready = sem("q_ready")
        k_ready = sem("k_ready")
        v_ps = sem("v_ps")
        vz_ready = sem("vz_ready")
        vz_out = [sem(f"vz_out{k}") for k in range(3)]
        p2c_ps = sem("p2c_ps")
        p2c_act = sem("p2c_act")
        p2c_dve = sem("p2c_dve")
        c2p_ps = sem("c2p_ps")
        c_ready = sem("c_ready")
        c_out = sem("c_out")
        ring_zero = sem("ring_zero")
        pad_zero = sem("pad_rows_zero")
        sbank_zero = sem("sbank_zero")
        c_in = [sem("c_in0"), sem("c_in1")]
        v_in = [sem("v_in0"), sem("v_in1")]
        s_ps = sem("scores_ps")
        s_sum = sem("scores_summed")
        s_max = sem("scores_max")
        s_sub = sem("scores_centred")
        s_exp = sem("probs_exp")
        s_tot = sem("probs_total")
        s_inv = sem("probs_inv")
        s_nrm = sem("probs_ready")
        pt_ps = sem("probsT_ps")
        pt_sb = sem("probsT_ready")
        o_ps = sem("attn_ps")
        o_sb = sem("attn_ready")
        hb_ready = sem("hb_ready")
        wo_ps = sem("wo_ps")
        r_ready = sem("resid_ready")
        ln_var = sem("ln_var")
        ln_rstd = sem("ln_rstd")
        h1_ready = sem("h1_ready")
        nb_ready = sem("h1_shift_ready")
        n_ready = sem("normed_ready")
        n_ps = sem("normedT_ps")
        nt_ready = sem("normedT_ready")
        s_wf = sem("wffn_in")
        s_low = sem("lower_in")
        x2_ps = sem("mix_ps")
        x2_ready = sem("mix_ready")
        mb_ready = sem("mix_shifted")
        sx_zero = sem("probs2_zero")
        vj_zero = sem("values2_zero")
        pg_ready = sem("pooled_in_ready")
        k2_ps = sem("k2_ps")
        k2_ready = sem("k2_ready")
        v2_ps = sem("v2_ps")
        v2_ready = sem("v2_ready")
        v2_out = sem("v2_out")
        vj_in = sem("vj_in")
        zz_ready = sem("zz_ready")
        z_ps = sem("z_ps")
        nbr_ready = sem("nbr_ready")
        z_exp = sem("z_exp")
        dve_step = sem("dve_step")
        oh_ready = sem("pool_diag_ready")
        nd_out = sem("normed_out")
        idx_ready = sem("indices_ready")
        g_in = sem("chosen_in")
        gt_ps = sem("chosenT_ps")
        zero_out = sem("chosen_scratch_zero")
        sc_out = sem("chosen_out")
        sc_in = [sem(f"chosen_tiles_in{k}") for k in range(4)]
        g_ready = sem("gathered_ready")
        q2_ps = sem("q2_ps")
        q2_sb = sem("q2_sb")
        qe_ready = sem("qe_ready")
        pm_ps = sem("pooled_ps")
        pm_ready = sem("pooled_ready")
        l2_ps = sem("logits_ps")
        l2_cent = sem("logits_centred")
        l2_exp = sem("logits_exp")
        l2_ready = sem("probs2_ready")
        t2_ps = sem("probs2T_ps")
        t2_ready = sem("probs2T_ready")
        c2_ps = sem("context_ps")
        c2_ready = sem("context_ready")
        ctx_ready = sem("context_with_bias")
        as_ps = sem("chosen_ps")
        as_ready = sem("chosen_ready")
        h2_ready = sem("h2_ready")
        ln2_var = sem("ln2_var")
        ln2_rstd = sem("ln2_rstd")
        n2_ready = sem("n2_ready")
        n2_ps = sem("n2T_ps")
        n2t_ready = sem("n2T_ready")
        res_part = sem("res_part")
        res_ready = sem("res_ready")
        f1_ps = sem("ffn1_ps")
        f1_ready = sem("ffn1_ready")
        f2_ps = sem("ffn2_ps")
        y_ready = sem("y_ready")
        ln3_var = sem("ln3_var")
        ln3_rstd = sem("ln3_rstd")
        y_out = sem("y_ready_out")
        s_out = sem("s_out")

        block = ctx.enter_context(nc.Block())
        XCH = [(0, 1), (1, 3), (3, 5), (5, 7), (7, 9), (9, 11), (11, 12)]

        def window(i):
            return [(a, 2 * i - 1 + a) for a in range(4) if 0 <= 2 * i - 1 + a < NB]

        def load_x(eng, k):
            r0, r1 = XCH[k]
            for h in range(2):
                eng.dma_start(xs[64 * h:64 * h + 64, r0:r1, :, 1 - h:NQ - h, :],
                              x[64 * h:64 * h + 64, r0:r1, :, :, :]).then_inc(s_x[k], 16)

        @block.sync
        def _(sp):
            sp.dma_start(gams[:, :], gam).then_inc(s_gb, 16)
            sp.dma_start(bets[:, :], bet).then_inc(s_gb, 16)

            def load_w(k):
                sp.dma_start(wraw[:, 6 * k:6 * k + 6, :], wtok[:, 6 * k:6 * k + 6, :]).then_inc(s_w[k], 16)

            for k in (3, 1, 4, 2, 0):
                load_w(k)
            for k in range(2, len(XCH)):
                load_x(sp, k)
            sp.dma_start(bias[:, :, :], brow.partition_broadcast(P)).then_inc(s_bias, 16)
            sp.dma_start(colb[:, :], col).then_inc(s_bias, 16)
            sp.dma_start(bf1s[:, :], bf1).then_inc(s_bias, 16)
            sp.dma_start(brs[:, :], br.to_broadcast([P, 1])).then_inc(s_bias, 16)
            sp.dma_start(wat[:, :, :, :], watt).then_inc(s_wat, 16)
            sp.dma_start(wos[:, :, :], wout).then_inc(s_wat, 16)
            sp.wait_ge(rsq_ready, NB)
            sp.dma_start(relts, relt).then_inc(s_rel, 16)
            for ip in range(T // 2):
                sp.wait_ge(c_ready, 2 * ip + 2)
                sp.dma_start(cd[:, 2 * ip:2 * ip + 2, :],
                             ax[0:B, 2 * ip * HT_COLS:(2 * ip + 2) * HT_COLS].rearrange("p (i c) -> p i c", i=2)
                             ).then_inc(c_out, 16)
            sp.wait_ge(c_out, 16 * (T // 2))
            sp.wait_ge(ring_zero, 1)

            for k in range(2):
                sp.dma_start(sd.rearrange("(k n p) o -> k p n o", k=2, p=P)[k],
                             ann[:, 0:9 * D].rearrange("p (n o) -> p n o", o=D)).then_inc(zero_out, 16)
            sp.wait_ge(zero_out, 32)

            def load_c(g):
                if g >= 2:
                    sp.wait_ge(s_sum, 2 * g - 2)
                for ib in range(2):
                    sp.dma_start(cring[64 * ib:64 * ib + T, g % 2, :, :],
                                 cd[4 * g + ib:4 * g + ib + 3:2, :, :].rearrange("n i c -> i n c")
                                 ).then_inc(c_in[g % 2], 16)

            def load_v(g):
                if g >= 2:
                    sp.wait_ge(o_ps, 2 * g - 2)
                if g == 0:
                    sp.wait_ge(pad_zero, 1)
                for r in range(H3):
                    sp.dma_start(vbd[T * r:T * r + T, g % 2, :, :].rearrange("p n (k c) -> p (n k) c", c=GW)[:, :, r * DH:(r + 1) * DH],
                                 vd.rearrange("(t b) (k c) -> t (b k) c", b=B, c=GW)[:, 16 * g:16 * g + 16, r * DH:(r + 1) * DH]
                                 ).then_inc(v_in[g % 2], 16)

            load_c(0)
            for g in range(PAIRS // 2):
                if g + 1 < PAIRS // 2:
                    load_c(g + 1)
                if g == 0:
                    for k in range(3):
                        sp.wait_ge(vz_out[k], 32)
                load_v(g)
            sp.wait_ge(s_ps, PAIRS)
            sp.dma_start(wf, wffn).then_inc(s_wf, 16)
            sp.dma_start(w2s, w2).then_inc(s_wf, 16)
            sp.dma_start(lows, lower.partition_broadcast(P)).then_inc(s_low, 16)
            for i in range(GRID):
                sp.wait_ge(n_ready, TPR * (i + 1))
                sp.dma_start(nd[i * CHUNK:(i + 1) * CHUNK, :].rearrange("(n p) o -> p n o", p=P),
                             norm[:, TPR * i:TPR * i + TPR, :]).then_inc(nd_out, 16)
                sp.wait_ge(v2_ready, TPR * (i + 1))
                sp.dma_start(v2d[i * CHUNK:(i + 1) * CHUNK, :].rearrange("(n p) o -> p n o", p=P),
                             v2s[:, TPR * i:TPR * i + TPR, 0:D]).then_inc(v2_out, 16)
            sp.wait_ge(v2_out, 16 * GRID)
            sp.wait_ge(vj_zero, 1)
            for ib in range(2):
                sp.dma_start(vj[64 * ib:64 * ib + T, :, :],
                             v2d.rearrange("(t n e) o -> e t n o", t=T, e=2)[ib]).then_inc(vj_in, 16)

            def load_chosen(i):
                if i >= 4:
                    sp.wait_ge(h2_ready, TPR * (i - 3))
                sp.dma_start(scr[:, TPR * (i % 4):TPR * (i % 4) + TPR, :],
                             sd[i * CHUNK:(i + 1) * CHUNK, :].rearrange("(n p) o -> p n o", p=P)).then_inc(sc_in[i % 4], 16)

            sp.wait_ge(sc_out, 48)
            for i in range(4):
                load_chosen(i)
            for n in range(NT):
                if n in (0, TPR):
                    load_chosen(4 + n // TPR)
                sp.wait_ge(y_out, n + 1)
                sp.dma_start(out[:, 2 * n:2 * n + 2, :].rearrange("b t o -> t b o"), nat[:, n, :]).then_inc(s_out, 16)
            sp.wait_ge(s_out, 16 * NT)

        @block.tensor
        def _(pe):
            def keep_clock(products, b):
                for _ in range(products):
                    pe.matmul(bank[:, b, 0:P], ident, ident, start=True, stop=True)

            def tok_product(n, a, r, first, last):
                k = 0
                for s in range(2):
                    for c in range(CH):
                        q0 = 2 * (n % TPR) + s
                        pe.matmul(bank[:, n % (2 * TPR), 0:D + 1], xs[:, r, c, q0:q0 + 2, :], wg[:, a, s, c, :],
                                  start=(first and k == 0), stop=(last and k == 2 * CH - 1))
                        k += 1

            def tok_squares(i):
                pe.wait_ge(ss_ready, i + 1)
                for n in range(TPR * i, TPR * i + TPR):
                    pe.matmul(bank[:, n % (2 * TPR), D + 8:D + 9], ssum[:, i % 2, n % TPR * P:n % TPR * P + P], ones[:, 0:1],
                              start=True, stop=True).then_inc(tok_ps, 1)

            def tok_row(i):
                rows = window(i)
                for k in range(7):
                    if XCH[k][0] <= rows[-1][1] < XCH[k][1]:
                        pe.wait_ge(s_x[k], 32)
                if i == 0:
                    for a, r in (rows[2], rows[0], rows[1]):
                        pe.wait_ge(s_x[(r + 1) // 2], 32)
                        pe.wait_ge(wg_ready, {3: 3, 1: 5, 2: 7}[a])
                        for n in range(TPR):
                            tok_product(n, a, r, a == 3, a == 2)
                else:
                    pe.wait_ge(wg_ready, 8)
                    for n in range(TPR * i, TPR * i + TPR):
                        if n >= 2 * TPR:
                            pe.wait_ge(h_ready, n - 2 * TPR + 1)
                        for a, r in rows:
                            tok_product(n, a, r, (a, r) == rows[0], (a, r) == rows[-1])
                        if n == TPR + 1:
                            pe.wait_ge(red_ready, 2)
                            for k in range(2):
                                mm = pe.matmul(bank[:, 6, k * D:(k + 1) * D], ones[:, :], red[:, k, :], start=True, stop=True)
                            mm.then_inc(swcb_ps, 1)
                tok_squares(i)

            def h_turn(n):
                pe.wait_ge(h_ready, n + 1)
                if n >= 2:
                    pe.wait_ge(ht_ready, n - 1)
                for m in range(2):
                    mm = pe.transpose(bank[0:HALF, 6 + n % 2, m * P:(m + 1) * P],
                                      nat[:, n, m * HALF:(m + 1) * HALF], ident)
                mm.then_inc(htr_ps, 1)

            pe.wait_ge(ones_set, 1)
            pe.wait_ge(pads_left, 1)
            pe.wait_ge(pads_right, 1)
            for i in range(GRID):
                tok_row(i)
                if i == 1:
                    pe.wait_ge(s_cst, 16)
                    pe.wait_ge(swb_ready, 2)
                if i:
                    for n in range(TPR * (i - 1), TPR * i):
                        h_turn(n)
            for jj in range(TPR):
                h_turn(TPR * (GRID - 1) + jj)

            pe.wait_ge(s_wat, 32)
            pe.wait_ge(s_rel, 16)
            pe.wait_ge(h_ready, NT)
            for v in range(2):
                for m in range(2):
                    for kk in range(2):
                        mm = pe.matmul(bank[0:HALF, 0, (2 * v + m) * REL:(2 * v + m + 1) * REL],
                                       wat[:, 3 + v, kk, m * HALF:(m + 1) * HALF], relts[:, v, kk, :],
                                       start=(kk == 0), stop=(kk == 1))
            mm.then_inc(pk_ps, 1)

            pe.wait_ge(pk_sb, 1)
            for i in range(GRID):
                pe.wait_ge(ht_ready, TPR * (i + 1))
                for which in range(2):
                    for m in range(2):
                        u = 4 * i + 2 * which + m
                        if u >= 6:
                            o = u - 6
                            if o % 4 < 2:
                                pe.wait_ge(q_ready, 2 * (o // 4) + o % 4 + 1)
                            else:
                                pe.wait_ge(k_ready, 2 * (2 * (o // 4) + o % 4 - 2) + 2)
                        for kk in range(2):
                            mm = pe.matmul(bank[0:HALF, u % 6, 0:CHUNK], wat[:, which, kk, m * HALF:(m + 1) * HALF],
                                           ht[:, kk, i * CHUNK:(i + 1) * CHUNK], start=(kk == 0), stop=(kk == 1))
                        mm.then_inc(qk_ps, 1)

            pe.wait_ge(q_ready, 2 * GRID)
            pe.wait_ge(k_ready, 4 * GRID)
            pe.wait_ge(bd_ready, 4)
            for jp in range(T // 2):
                if jp >= 4:
                    pe.wait_ge(p2c_act, jp - 3)
                    pe.wait_ge(p2c_dve, jp - 3)
                dst = bank[:, jp % 4, 0:H * WIN].rearrange("p (g m e w) -> p g m e w", g=GQ, m=2, e=2)
                for m in range(2):
                    for e in range(2):
                        mm = pe.matmul(dst[:, :, m, e, :],
                                       ke[:, m, e, 2 * jp:2 * jp + 2, :].rearrange("p t b -> p (t b)"),
                                       bdt[:, 1, m, e:6:2, T - 2 - 2 * jp:T - 2 - 2 * jp + WIN],
                                       start=True, stop=True)
                mm.then_inc(p2c_ps, 1)
            for ip in range(T // 2):
                u = ip + T // 2
                if ip < 4:
                    pe.wait_ge(p2c_act, u - 3)
                    pe.wait_ge(p2c_dve, u - 3)
                else:
                    pe.wait_ge(c_ready, 2 * (ip - 3))
                dst = bank[:, u % 4, 0:H * WIN].rearrange("p (g m e w) -> p g m e w", g=GQ, m=2, e=2)
                for m in range(2):
                    mm = pe.matmul(dst[:, :, m, :, :],
                                   qt[:, m, 2 * ip:2 * ip + 2, :].rearrange("p t b -> p (t b)"),
                                   bdt[:, 0, m, :, T - 2 - 2 * ip:T - 2 - 2 * ip + WIN].rearrange("p (g e) w -> p g e w", e=2),
                                   start=True, stop=True)
                mm.then_inc(c2p_ps, 1)

            for n in range(NT):
                if n >= 2:
                    pe.wait_ge(vz_ready, n - 1)
                for kk in range(2):
                    mm = pe.matmul(bank[:, 6 + n % 2, 0:D], ht[:, kk, n * P:(n + 1) * P], wat[:, 2, kk, :],
                                   start=(kk == 0), stop=(kk == 1))
                mm.then_inc(v_ps, 1)

            def scores(n):
                if n >= 2:
                    pe.wait_ge(s_sum, n - 1)
                for m in range(2):
                    for ib in range(2):
                        for g in range(GQ):
                            mm = pe.matmul(bank[64 * ib:64 * ib + T, GQ * (n % 2) + g, m * 2 * T:(m + 1) * 2 * T],
                                           qt[32 * g:32 * g + 32, m, :, 2 * n + ib],
                                           ke[32 * g:32 * g + 32, m, :, :, 2 * n + ib], start=True, stop=True)
                mm.then_inc(s_ps, 1)

            def turn(n):
                if n:
                    pe.wait_ge(pt_sb, n)
                keep_clock(1, 6)
                pe.wait_ge(s_nrm, n + 1)
                for k in range(4):
                    mm = pe.transpose(bank[0:H3 * T, 6, k * P:(k + 1) * P],
                                      sring[:, n % NR, k * H3 * T:(k + 1) * H3 * T], ident)
                mm.then_inc(pt_ps, 1)

            def blend(n):
                pe.wait_ge(pt_sb, n + 1)
                pe.wait_ge(v_in[n // 2 % 2], 48 * (n // 4 + 1))
                if n:
                    pe.wait_ge(o_sb, n)
                for ib in range(2):
                    for k in range(4):
                        r0, m = 64 * (k % 2), k // 2
                        mm = pe.matmul(bank[r0:r0 + GW, 7, (2 * m + ib) * T:(2 * m + ib + 1) * T],
                                       vbd[:, n // 2 % 2, 2 * (n % 2) + ib, k * GW:(k + 1) * GW],
                                       ptr[:, n % 2, k, 64 * ib:64 * ib + T], start=True, stop=True)
                mm.then_inc(o_ps, 1)

            pe.wait_ge(vz_ready, NT)
            keep_clock(16, 6)
            pe.wait_ge(sbank_zero, 2)
            pe.wait_ge(c_ready, T)
            for n in range(PAIRS + 4):
                if n < PAIRS:
                    scores(n)
                if n < 3:
                    keep_clock((2, 8, 8)[n], 6)
                if n == 3:
                    pe.wait_ge(pad_zero, 2)
                if 0 <= n - 3 < PAIRS:
                    turn(n - 3)
                if n >= 4:
                    blend(n - 4)

            def wo(i):
                for n in range(TPR * i, TPR * i + TPR):
                    if n >= 2:
                        pe.wait_ge(r_ready, n - 1)
                    for m in range(2):
                        mm = pe.matmul(bank[:, n % 2, 0:D], ot[:, m, 2 * n:2 * n + 2, :].rearrange("p t b -> p (t b)"),
                                       wos[:, m, :], start=(m == 0), stop=(m == 1))
                    mm.then_inc(wo_ps, 1)

            def n_turn(i):
                if i >= 2:
                    pe.wait_ge(nt_ready, 2 * (i - 1))
                for n in range(TPR * i, TPR * i + TPR):
                    pe.wait_ge(n_ready, n + 1)
                    for m in range(2):
                        mm = pe.transpose(bank[0:HALF, 4 + 2 * (i % 2) + m, n % TPR * P:n % TPR * P + P],
                                          norm[:, n, m * HALF:(m + 1) * HALF], ident)
                mm.then_inc(n_ps, 1)

            def v2_row(i):
                pe.wait_ge(nt_ready, 2 * (i + 1))
                for n in range(TPR * i, TPR * i + TPR):
                    if n >= 2:
                        pe.wait_ge(v2_ready, n - 1)
                    for kk in range(2):
                        mm = pe.matmul(bank[:, 2 + n % 2, 0:D + 1], nt_[:, kk, n * P:(n + 1) * P], wf[:, kk, WV:WV + D + 1],
                                       start=(kk == 0), stop=(kk == 1))
                    mm.then_inc(v2_ps, 1)

            pe.wait_ge(o_sb, PAIRS)
            for i in range(GRID + 3):
                if i < GRID:
                    wo(i)
                if 2 <= i < GRID + 2:
                    n_turn(i - 2)
                if i >= 3:
                    if i == 3:
                        pe.wait_ge(s_wf, 32)
                    v2_row(i - 3)

            for i in range(GRID):
                if i == 1:
                    pe.wait_ge(zz_ready, 1)
                    pe.matmul(bank[:, 6, 0:T], ident2, zz[:, :, :].rearrange("p e n -> p (e n)"),
                              start=True, stop=True).then_inc(z_ps, 1)
                for m in range(2):
                    u = 2 * i + m
                    if u >= 2:
                        pe.wait_ge(k2_ready, u - 1)
                    else:
                        pe.wait_ge(r_ready, NT)
                    for kk in range(2):
                        mm = pe.matmul(bank[0:HALF, u % 2, 0:CHUNK], wf[:, kk, WK + m * HALF:WK + (m + 1) * HALF],
                                       nt_[:, kk, i * CHUNK:(i + 1) * CHUNK], start=(kk == 0), stop=(kk == 1))
                    mm.then_inc(k2_ps, 1)

            def mix(n):
                b = 2 + n % 2 if n < NMIX else 4 + n % 2
                if n >= 2:
                    pe.wait_ge(x2_ready, n - 1)
                else:
                    pe.wait_ge(v2_ready, NT)
                for kk in range(2):
                    mm = pe.matmul(bank[:, b, 0:D], nt_[:, kk, n * P:(n + 1) * P], wf[:, kk, WM:WM + D],
                                   start=(kk == 0), stop=(kk == 1))
                mm.then_inc(x2_ps, 1)

            for n in range(NMIX):
                mix(n)

            pe.wait_ge(oh_ready, 2)
            for m in range(2):
                pe.matmul(bank[0:HALF, 4 + m, SLOT * B:(SLOT + 1) * B], brow_bc("b1")[:, m * HALF:(m + 1) * HALF], wdiag,
                          start=True, stop=True)
            for m in range(2):
                for n in range(NT):
                    mm = pe.matmul(bank[0:HALF, 4 + m, NSEL * B:SLOT * B], norm[:, n, m * HALF:(m + 1) * HALF], pwd[:, n, :],
                                   start=(n == 0), stop=(n == NT - 1))
            pe.wait_ge(g_in, 48)
            for k in range(3):
                rows = P if k < 2 else B
                for m in range(2):
                    mm = pe.transpose(bank[0:HALF, 4 + m, k * P:k * P + rows], gsb[0:rows, k, m * HALF:(m + 1) * HALF],
                                      ident[0:rows, 0:rows])
            mm.then_inc(gt_ps, 1)
            pe.wait_ge(z_exp, 1)
            pe.wait_ge(g_ready, 2)
            for m in range(2):
                for kk in range(2):
                    mm = pe.matmul(bank[0:HALF, 6 + m, 0:NSEL * B], wf[:, kk, WQ + m * HALF:WQ + (m + 1) * HALF],
                                   gt[:, kk, 0:NSEL, :].rearrange("p s b -> p (s b)"), start=(kk == 0), stop=(kk == 1))
                mm.then_inc(q2_ps, 1)
            pe.wait_ge(x2_ready, NMIX)
            pe.wait_ge(pg_ready, 1)
            for kk in range(2):
                mm = pe.matmul(bank[:, 3, 0:D], gt[:, kk, NSEL:NSEL + 2, :].rearrange("p s b -> p (s b)"),
                               wf[:, kk, WM:WM + D], start=(kk == 0), stop=(kk == 1))
            mm.then_inc(pm_ps, 1)
            for n in range(NMIX, NMIX2):
                mix(n)

            pe.wait_ge(qe_ready, 7)
            pe.wait_ge(k2_ready, 2 * GRID)
            for n in range(PAIRS):
                for ib in range(2):
                    for m in range(2):
                        q0 = 32 * (2 * ib + m)
                        mm = pe.matmul(bank[q0:q0 + 32, n // 12, n % 12 * T:n % 12 * T + T], qe[:, m, 2 * n + ib, :],
                                       kt[:, m, :, 2 * n + ib], start=True, stop=True)
                if n % 12 == 11 or n == PAIRS - 1:
                    mm.then_inc(l2_ps, 1)

            def turn2(k):
                if k >= 2:
                    pe.wait_ge(t2_ready, k - 1)
                else:
                    pe.wait_ge(x2_ready, NMIX2)
                keep_clock(14 if k == 0 else 1, 4 + k % 2)
                pe.wait_ge(l2_ready, 2 * (k // 3 + 1))
                for n in range(4):
                    mm = pe.transpose(bank[0:W2X, 4 + k % 2, n * P:(n + 1) * P], s2x[:, 4 * k + n, :], ident)
                mm.then_inc(t2_ps, 1)

            def context(k):
                pe.wait_ge(t2_ready, k + 1)
                if k >= 2:
                    pe.wait_ge(c2_ready, 2 * (k - 1))
                for n in range(4):
                    for m in range(2):
                        c0 = (8 * m + 2 * n) * 32
                        mm = pe.matmul(bank[0:HALF, 6 + k % 2, c0:c0 + 64].rearrange("p (e c) -> p e c", e=2),
                                       vj[:, 4 * k + n, m * HALF:(m + 1) * HALF],
                                       pt2[:, k % 2, n, :].rearrange("p (e m c) -> p e m c", e=2, m=2)[:, :, m, :],
                                       start=True, stop=True)
                mm.then_inc(c2_ps, 1)

            pe.wait_ge(vj_in, 32)
            pe.wait_ge(q2_sb, 2)
            for k in range(PAIRS // 4 + 1):
                if k < PAIRS // 4:
                    turn2(k)
                if k:
                    context(k - 1)
            pe.wait_ge(ctx_ready, 2)
            pe.wait_ge(pm_ready, 1)
            for k in range(3):
                rows = P if k < 2 else B
                for m in range(2):
                    mm = pe.matmul(bank[0:rows, 3 + k, 0:D], o2t[:, m, :, :].rearrange("p s b -> p (s b)")[:, k * P:k * P + rows],
                                   wf[:, m, WO:WO + D], start=(m == 0), stop=(m == 1))
                mm.then_inc(as_ps, 1)

            pe.wait_ge(as_ready, 3)
            for n in range(NMIX2, NT):
                mix(n)

            def n2_turn(i):
                if i:
                    pe.wait_ge(n2t_ready, 2 * i)
                for n in range(TPR * i, TPR * i + TPR):
                    pe.wait_ge(n2_ready, n + 1)
                    for m in range(2):
                        mm = pe.transpose(bank[0:HALF, 2 + m, n % TPR * P:n % TPR * P + P],
                                          mrg[:, 2 + i % 2, n % TPR, m * HALF:(m + 1) * HALF], ident)
                mm.then_inc(n2_ps, 1)

            def ffn1(i):
                pe.wait_ge(n2t_ready, 2 * (i + 1))
                for k in range(FF // P):
                    u = 6 * i + k
                    if u >= 2:
                        pe.wait_ge(f1_ready, u - 1)
                    for kk in range(2):
                        mm = pe.matmul(bank[:, 4 + u % 2, 0:CHUNK], wf[:, kk, W1 + k * P:W1 + (k + 1) * P],
                                       nt_[:, kk, i * CHUNK:(i + 1) * CHUNK], start=(kk == 0), stop=(kk == 1))
                    mm.then_inc(f1_ps, 1)

            def ffn2(n):
                i, j = n // TPR, n % TPR
                pe.wait_ge(f1_ready, 6 * (i + 1))
                if n >= 2:
                    pe.wait_ge(y_ready, n - 1)
                for k in range(FF // P):
                    mm = pe.matmul(bank[:, 6 + n % 2, 0:D], hid[:, i % 3, k, j * P:(j + 1) * P], w2s[:, k, :],
                                   start=(k == 0), stop=(k == FF // P - 1))
                mm.then_inc(f2_ps, 1)

            for i in range(1, GRID + 2):
                if 1 <= i <= GRID:
                    n2_turn(i - 1)
                if i >= 2:
                    for n in range(TPR * (i - 2), TPR * (i - 1)):
                        ffn2(n)
                if 1 <= i <= GRID:
                    ffn1(i - 1)

        @block.vector
        def _(dve):
            dve.memset(xs[0:64, :, :, 0, :].rearrange("p r c b -> p (r c) b"), 0.0).then_inc(pads_left, 1)
            dve.memset(wgf[:, :, D:D + 1], 1.0).then_inc(wc_ready, 1)
            dve.wait_ge(wc_ready, 1)
            dve.memset(wg[0:64, 1:3, 1, :, D:D + 1], 2.0).then_inc(wg_ready, 1)
            dve.memset(wg[64:128, 1:3, 0, :, D:D + 1], 2.0).then_inc(wg_ready, 1)
            dve.wait_ge(s_gb, 32)

            def gained(k):
                dve.wait_ge(s_w[k], 16)
                scale = gams[:, 6 * k:6 * k + 6].unsqueeze(2).to_broadcast([P, 6, D])
                dst = wgf[:, 6 * k:6 * k + 6, 0:D] if k < 4 else wgc.rearrange("p a c o -> p (a c) o")
                return dve.tensor_tensor(dst, wraw[:, 6 * k:6 * k + 6, :], scale, ALU.mult)

            def centre_in(a):
                s0, s1 = wg[64:128, 1 + a, 0, :, 0:D], wg[0:64, 1 + a, 1, :, 0:D]
                dve.tensor_tensor(s0, s0, wgc[64:128, a, :, :], ALU.add).then_inc(wg_ready, 1)
                dve.tensor_tensor(s1, s1, wgc[0:64, a, :, :], ALU.add).then_inc(wg_ready, 1)

            gained(3).then_inc(wg_ready, 1)
            gained(1).then_inc(wc_ready, 1)
            gained(4).then_inc(wc_ready, 1)
            dve.wait_ge(wc_ready, 3)
            centre_in(0)
            gained(2).then_inc(wc_ready, 1)
            dve.wait_ge(wc_ready, 4)
            centre_in(1)
            gained(0).then_inc(wg_ready, 1)

            def channel_sum(r):
                dve.wait_ge(sq_ready, r + 1)
                dve.tensor_reduce(rsq[:, r % 6, :], sq[:, r % 2, :, :].rearrange("p c q -> p q c"), AX.X,
                                  ALU.add).then_inc(rsq_ready, 1)

            def window_squares(i):
                dve.wait_ge(eu_ready, i + 1)
                if i >= 2:
                    dve.wait_ge(tok_ps, TPR * (i - 1))
                dve.scalar_tensor_tensor(side1, esum[i % 2], sidem[:, 1:2], usum[i % 2], ALU.mult, ALU.add).then_inc(ss_part, 1)
                dve.scalar_tensor_tensor(esum[i % 2], esum[i % 2], sidem[:, 0:1], usum[i % 2], ALU.mult,
                                         ALU.add).then_inc(ss_part, 1)
                dve.wait_ge(ss_part, 2 * i + 2)
                dve.tensor_tensor(ssum[:, i % 2, :], side1[:, 0:CHUNK], esum[i % 2][:, B:B + CHUNK], ALU.add).then_inc(ss_ready, 1)

            def tok_out(i):
                b0 = TPR * (i % 2)
                raw = bank[:, b0:b0 + TPR, :]
                dve.wait_ge(tok_ps, TPR * (i + 1))
                neg, e2, msq, var = (st[:, TPR * k:TPR * k + TPR] for k in range(4))
                dve.tensor_scalar(neg, raw[:, :, D], -1.0 / PDIM, None, ALU.mult).then_inc(tstat, 1)
                dve.tensor_scalar(e2, raw[:, :, D + 8], 1.0 / PDIM, EPS, ALU.mult, ALU.add).then_inc(tstat, 1)
                dve.wait_ge(tstat, 3 * i + 2)
                dve.tensor_tensor(msq, neg, neg, ALU.mult).then_inc(tstat, 1)
                dve.wait_ge(tstat, 3 * i + 3)
                dve.tensor_tensor(var, e2, msq, ALU.subtract).then_inc(tvar, 1)
                for jj in range(TPR):
                    n = TPR * i + jj
                    dve.scalar_tensor_tensor(nat[:, n, :], swb[:, :], st[:, jj:jj + 1], raw[:, jj, 0:D],
                                             ALU.mult, ALU.add).then_inc(tcent, 1)
                dve.wait_ge(trstd, i + 1)
                for jj in range(TPR):
                    n = TPR * i + jj
                    dve.wait_ge(tcent, n + 1)
                    dve.scalar_tensor_tensor(nat[:, n, :], nat[:, n, :], rst[:, jj:jj + 1], cb[:, :],
                                             ALU.mult, ALU.add).then_inc(h_ready, 1)

            for r in range(3):
                channel_sum(r)
            dve.wait_ge(s_cst, 16)
            window_squares(0)
            dve.wait_ge(wg_ready, 8)
            dve.tensor_reduce(red[:, 0, :], wgf[:, :, 0:D].rearrange("p k o -> p o k"), AX.X, ALU.add).then_inc(red_ready, 1)
            for r in range(3, 5):
                channel_sum(r)
            dve.wait_ge(wb_ready, 1)
            dve.tensor_reduce(red[:, 1, :], wraw.rearrange("p k o -> p o k"), AX.X, ALU.add).then_inc(red_ready, 1)
            window_squares(1)
            dve.wait_ge(swcb_ps, 1)
            dve.wait_ge(s_bias, 64)
            dve.tensor_copy(swb[:, :], bank[:, 6, 0:D]).then_inc(swb_ready, 1)
            dve.tensor_tensor(cb[:, :], bank[:, 6, D:2 * D], brow_bc("tok_b"), ALU.add).then_inc(swb_ready, 1)
            dve.wait_ge(swb_ready, 2)
            for i in range(GRID):
                if i:
                    for r in (2 * i + 3, 2 * i + 4):
                        if r < NB:
                            if r >= 6:
                                dve.wait_ge(eu_ready, (r - 6) // 2 + 1 + (r % 2))
                            channel_sum(r)
                    if i + 1 < GRID:
                        window_squares(i + 1)
                tok_out(i)

            dve.wait_ge(pk_ps, 1)
            for v in range(2):
                for m in range(2):
                    ins = dve.tensor_scalar(pks[:, v, m, :], bank[0:HALF, 0, (2 * v + m) * REL:(2 * v + m + 1) * REL],
                                            colb[:, 4 + 2 * v + m:5 + 2 * v + m], None, ALU.add)
            ins.then_inc(pk_sb, 1)
            dve.wait_ge(pk_sb, 1)
            for v in range(2):
                for m in range(2):
                    dve.tensor_tensor(bdt[:, v, m, :, :],
                                      pks[:, v, m, :].unsqueeze(1).to_broadcast([HALF, 6, REL]),
                                      hmask.unsqueeze(2).to_broadcast([HALF, 6, REL]), ALU.mult).then_inc(bd_ready, 1)
            dve.wait_ge(bd_ready, 4)
            dve.memset(arg[:, :], 0.0).then_inc(pad_zero, 1)
            dve.wait_ge(tok_ps, NT)
            dve.memset(ann[:, :], 0.0).then_inc(ring_zero, 1)
            dve.wait_ge(ring_zero, 1)
            for i in range(GRID):
                for m in range(2):
                    dve.wait_ge(qk_ps, 4 * i + 3 + m)
                    for e in range(2):
                        dve.tensor_scalar(ke[:, m, e, GRID * i:GRID * i + GRID, :],
                                          bank[0:HALF, (4 * i + 2 + m) % 6, 0:CHUNK].rearrange("p (t b) -> p t b", b=B),
                                          colb[:, 2 + m:3 + m], emask[:, e:e + 1], ALU.add, ALU.mult).then_inc(k_ready, 1)

            def win(u, par, flip):
                w = bank[64 * par:64 * par + 64, u % 4, 0:H * WIN].rearrange("p (h w) -> p h w", w=WIN)
                return w[:, :, 1 - par:1 - par + T]

            for jp in range(T // 2):
                dve.wait_ge(p2c_ps, jp + 1)
                dve.tensor_copy(cmat[:, :, :, 2 * jp + 1].rearrange("p i h -> p h i"), win(jp, 1, 0)).then_inc(p2c_dve, 1)
            dve.wait_ge(p2c_dve, T // 2)
            dve.wait_ge(p2c_act, T // 2)
            for ip in range(T // 2):
                dve.wait_ge(c2p_ps, ip + 1)
                for par in range(2):
                    dst = cmat[:, 2 * ip + par, :, :]
                    dve.tensor_tensor(dst, win(ip + T // 2, par, 0), dst, ALU.add).then_inc(c_ready, 1)
            dve.wait_ge(c_ready, T)
            dve.memset(bank[:, 0:2 * GQ, 0:4 * T], 0.0).then_inc(sbank_zero, 1)
            for n in range(NT):
                dve.wait_ge(v_ps, n + 1)
                if n >= 9 and n % TPR == 0:
                    dve.wait_ge(vz_out[n // TPR % 3], 16)
                dve.tensor_tensor(vn[:, n % 9, :], bank[:, 6 + n % 2, 0:D], brow_bc("bv1"), ALU.add).then_inc(vz_ready, 1)
            dve.wait_ge(vz_ready, NT)
            dve.memset(bank[0:OROWS, 7, 0:4 * T], 0.0).then_inc(sbank_zero, 1)
            for k in range(3):
                dve.wait_ge(vz_out[k], 32)
            dve.memset(sring[96:128, :, :], 0.0).then_inc(pad_zero, 1)
            dve.wait_ge(pad_zero, 2)

            def v3(t):
                return t.rearrange("p (h j) -> p h j", j=T)

            def total(n):
                dve.wait_ge(s_exp, n + 1)
                dve.tensor_reduce(rs[0:100, n % NR, :], v3(sring[0:100, n % NR, :]), AX.X, ALU.add).then_inc(s_tot, 1)
                dve.wait_ge(s_tot, n + 1)
                dve.reciprocal(rs[0:100, n % NR, :], rs[0:100, n % NR, :]).then_inc(s_inv, 1)

            for n in range(PAIRS):
                dve.wait_ge(s_ps, n + 1)
                dve.wait_ge(c_in[n // 2 % 2], 32 * (n // 4 + 1))
                if n >= NR:
                    dve.wait_ge(pt_ps, n - NR + 1)
                def by_group(t):
                    return t.rearrange("p g (m c) -> p g m c", m=2)

                dve.tensor_tensor(sring[0:100, n % NR, :].rearrange("p (m g c) -> p g m c", m=2, g=GQ),
                                  by_group(bank[0:100, GQ * (n % 2):GQ * (n % 2) + GQ, 0:4 * T]),
                                  by_group(cring[0:100, n // 2 % 2, n % 2, :].rearrange("p (g c) -> p g c", g=GQ)),
                                  ALU.add).then_inc(s_sum, 1)
                dve.wait_ge(s_sum, n + 1)
                dve.tensor_reduce(mx[0:100, n % NR, :], v3(sring[0:100, n % NR, :]), AX.X, ALU.max).then_inc(s_max, 1)
                if n:
                    total(n - 1)
            total(PAIRS - 1)

            steps = [0]

            def step(ins):
                steps[0] += 1
                ins.then_inc(dve_step, 1)

            def settle():
                dve.wait_ge(dve_step, steps[0])

            def moments(k, i, src):
                for j in range(TPR):
                    step(dve.bn_stats(stats[:, j, :], src[:, TPR * i + j, :]))
                settle()
                for j in range(TPR):
                    step(dve.bn_aggr(lnb[:, k, TPR * i + j, 0:2], stats[:, j, :]))
                settle()

            def lnv(k, i, c):
                return lnb[:, k, TPR * i:TPR * i + TPR, c]

            def centre(k, dst, src, n, c=2):
                return dve.tensor_scalar(dst, src, lnb[:, k, n, 0:1], lnb[:, k, n, c:c + 1], ALU.subtract, ALU.mult)

            def resid(i):
                for n in range(TPR * i, TPR * i + TPR):
                    dve.wait_ge(wo_ps, n + 1)
                    dve.wait_ge(hb_ready, n + 1)
                    dve.tensor_tensor(nat[:, n, :], bank[:, n % 2, 0:D], nat[:, n, :], ALU.add).then_inc(r_ready, 1)
                dve.wait_ge(r_ready, TPR * (i + 1))
                moments(0, i, nat)
                dve.tensor_scalar(lnv(0, i, 2), lnv(0, i, 1), EPS, None, ALU.add).then_inc(ln_var, 1)
                dve.tensor_scalar(lnv(0, i, 3), lnv(0, i, 1), 1.0 + EPS, EPS * EPS, ALU.mult, ALU.add).then_inc(ln_var, 1)

            def n_norm(i):
                dve.wait_ge(ln_rstd, i + 1)
                for n in range(TPR * i, TPR * i + TPR):
                    centre(0, norm[:, n, :], nat[:, n, :], n, 3).then_inc(n_ready, 1)
                dve.scalar_tensor_tensor(nb1[:, TPR * i:TPR * i + TPR], lnv(0, i, 0), -1.0, lnv(0, i, 2), ALU.mult,
                                         ALU.mult).then_inc(nb_ready, 1)

            dve.wait_ge(pt_ps, PAIRS)
            for i in range(GRID + 1):
                if i < GRID:
                    resid(i)
                if i:
                    n_norm(i - 1)
            dve.tensor_scalar(nbr[:, :], brs[:, :], -1.0, None, ALU.mult).then_inc(nbr_ready, 1)

            dve.wait_ge(v2_ready, NT)
            for e in range(2):
                ins = dve.tensor_scalar(zz[:, e, :], v2s[:, :, D], sidem[:, e:e + 1], None, ALU.mult)
            ins.then_inc(zz_ready, 1)
            dve.wait_ge(z_exp, 1)
            step(dve.tensor_scalar(rt[:, :], rt[:, :], 1.0, None, ALU.add))
            settle()
            step(dve.reciprocal(sc[:, :].rearrange("p (n e) -> p e n", e=2), rt[:, :].rearrange("p (e n) -> p e n", e=2)))
            settle()
            inner = sc[:, :].unsqueeze(1).to_broadcast([P, T, T])
            outer = sc[:, :].unsqueeze(2).to_broadcast([P, T, T])
            step(dve.tensor_tensor(less, inner, outer, ALU.is_lt))
            step(dve.tensor_tensor(same, inner, outer, ALU.is_equal))
            step(dve.tensor_reduce(rsum[:, 0:1], sc[:, :], AX.X, ALU.add))
            settle()
            dve.wait_ge(s_low, 16)
            step(dve.tensor_tensor(same, same, lows, ALU.mult))
            step(dve.tensor_scalar(rsum[:, 1:2], rsum[:, 0:1], 1e-6, None, ALU.add))
            settle()
            step(dve.tensor_tensor(less, less, same, ALU.add))
            step(dve.reciprocal(rsum[:, 0:1], rsum[:, 1:2]))
            settle()
            step(dve.tensor_reduce(rt[:, :], less, AX.X, ALU.add))
            settle()
            step(dve.tensor_scalar(rt2[:, :], rt[:, :], sidem[:, 1:2], None, ALU.subtract))
            settle()
            for k in range(3):
                step(dve.scalar_tensor_tensor(ohs[:, k, :], rt2[:, :], float(2 * k), rowc, ALU.is_equal, ALU.mult))
            settle()
            step(dve.tensor_reduce(idxf[:, 0:3], ohs[:, :, :], AX.X, ALU.add))
            settle()
            dve.tensor_scalar(idx[:, 0:3], idxf[:, 0:3], imgc, float(TOK - 1), ALU.add, ALU.min).then_inc(idx_ready, 1)
            for e in range(2):
                lo, hi = 64 * e, 64 * e + 64
                step(dve.tensor_scalar(pw[lo:hi, :], sc[lo:hi, e:T:2], rsum[lo:hi, 0:1], None, ALU.mult))
            settle()
            step(dve.tensor_reduce(wsum[:, :], pw[:, :], AX.X, ALU.add))
            dve.tensor_tensor(pwd, ident2[:, 0:B].unsqueeze(1).to_broadcast([P, NT, B]),
                              pw[:, :].unsqueeze(2).to_broadcast([P, NT, B]), ALU.mult).then_inc(oh_ready, 1)
            settle()
            dve.tensor_scalar(wdiag, ident2[:, 0:B], wsum[:, 0:1], None, ALU.mult).then_inc(oh_ready, 1)
            for e in range(2):
                lo, hi = 64 * e, 64 * e + 64
                step(dve.tensor_copy(own[lo:hi, 0, :], sc[lo:hi, e:T:2]))
                step(dve.tensor_scalar(own[lo:hi, 1, :], rt[lo:hi, e:T:2], float(NSEL), None, ALU.is_ge))
            dve.memset(qe[:, :, :, 30:32], 0.0).then_inc(qe_ready, 1)

            dve.wait_ge(gt_ps, 1)
            for m in range(2):
                dve.tensor_scalar(gt[:, m, 0:NSEL, :], bank[0:HALF, 4 + m, 0:NSEL * B].rearrange("p (s b) -> p s b", b=B),
                                  fcol("g1", m), fcol("b1", m), ALU.mult, ALU.add).then_inc(g_ready, 1)
            step(dve.tensor_copy(gt[:, :, SLOT, :], bank[0:HALF, 4:6, SLOT * B:(SLOT + 1) * B]))
            settle()
            for m in range(2):
                step(dve.scalar_tensor_tensor(gt[:, m, NSEL, :], bank[0:HALF, 4 + m, NSEL * B:SLOT * B], fcol("g1", m),
                                              gt[:, m, SLOT, :], ALU.mult, ALU.add))
            settle()
            dve.tensor_copy(gt[:, :, SLOT, :], gt[:, :, NSEL, :]).then_inc(pg_ready, 1)
            dve.wait_ge(q2_sb, 2)
            for k in range(6):
                dve.tensor_scalar(qe[:, :, :, NSEL * k:NSEL * k + NSEL].rearrange("p m b s -> p m s b"), qs[:, :, :, :],
                                  hmask[:, k:k + 1], None, ALU.mult).then_inc(qe_ready, 1)
            dve.wait_ge(pm_ps, 1)
            dve.tensor_copy(pm, bank[:, 3, 0:D]).then_inc(pm_ready, 1)

            for k in range(3):
                n0, n1 = 12 * k, min(12 * k + 12, PAIRS)
                raw = bank[:, k, 0:(n1 - n0) * T].rearrange("p (n j) -> p n j", j=T)
                dve.wait_ge(l2_ps, k + 1)
                step(dve.tensor_reduce(mx2[:, 0, n0:n1], raw, AX.X, ALU.max))
                settle()
                dve.tensor_tensor(s2[:, n0:n1, :], raw, mx2[:, 0, n0:n1].unsqueeze(2).to_broadcast([P, n1 - n0, T]),
                                  ALU.subtract).then_inc(l2_cent, 1)
            for k in range(3):
                n0, n1 = 12 * k, min(12 * k + 12, PAIRS)
                dve.wait_ge(l2_exp, k + 1)
                step(dve.tensor_reduce(mx2[:, 1, n0:n1], s2[:, n0:n1, :], AX.X, ALU.add))
                settle()
                step(dve.reciprocal(mx2[:, 1, n0:n1], mx2[:, 1, n0:n1]))
                settle()
                if k == 0:
                    dve.wait_ge(sx_zero, 1)
                for ib in range(2):
                    p0, p1 = 64 * ib, 64 * ib + 64
                    dve.tensor_tensor(s2x[p0:p1, n0:n1, p0:p0 + T], s2[p0:p1, n0:n1, :],
                                      mx2[p0:p1, 1, n0:n1].unsqueeze(2).to_broadcast([64, n1 - n0, T]),
                                      ALU.mult).then_inc(l2_ready, 1)
            for k in range(PAIRS // 4):
                dve.wait_ge(c2_ps, k + 1)
                step(dve.tensor_tensor(otmp[:, k % 2, :, :].rearrange("p n (h s) -> p n h s", s=NSEL),
                                       bank[0:HALF, 6 + k % 2, :].rearrange("p (n c) -> p n c", c=32)[:, :, 0:30].rearrange("p n (h s) -> p n h s", s=NSEL),
                                       hmask.unsqueeze(1).unsqueeze(3).to_broadcast([HALF, 16, 6, NSEL]), ALU.mult))
                settle()
                for m in range(2):
                    ins = dve.tensor_reduce(o2t[:, m, :, 8 * k:8 * k + 8].rearrange("p s b -> p b s"),
                                            otmp[:, k % 2, 8 * m:8 * m + 8, :].rearrange("p n (h s) -> p n s h", s=NSEL),
                                            AX.X, ALU.add)
                    ins.then_inc(c2_ready, 1)
            dve.wait_ge(c2_ready, PAIRS // 2)
            for m in range(2):
                o = o2t[:, m, :, :].rearrange("p s b -> p (s b)")
                dve.tensor_scalar(o, o, fcol("bv2", m), None, ALU.add).then_inc(ctx_ready, 1)
            for k in range(3):
                rows = P if k < 2 else B
                dve.wait_ge(as_ps, k + 1)
                dve.tensor_tensor(asel[0:rows, k, :], bank[0:rows, 3 + k, 0:D], brow_bc("bo2")[0:rows, :], ALU.add).then_inc(as_ready, 1)

            def merged(i):
                tiles = range(TPR * i, TPR * i + TPR)
                dve.wait_ge(mb_ready, TPR * (i + 1))
                dve.wait_ge(h1_ready, TPR * (i + 1))
                for n in tiles:
                    step(dve.scalar_tensor_tensor(mrg[:, 0, n % TPR, :], pm, own[:, 0, n:n + 1], mixed[:, n, :], ALU.mult, ALU.add))
                settle()
                for n in tiles:
                    step(dve.scalar_tensor_tensor(mrg[:, 1, n % TPR, :], mrg[:, 0, n % TPR, :], own[:, 1, n:n + 1], nat[:, n, :],
                                                  ALU.mult, ALU.add))
                settle()
                dve.wait_ge(sc_in[i % 4], 16 * (i // 4 + 1))
                for n in tiles:
                    dve.tensor_tensor(norm[:, n, :], scr[:, n % 12, :], mrg[:, 1, n % TPR, :], ALU.add).then_inc(h2_ready, 1)
                dve.wait_ge(h2_ready, TPR * (i + 1))
                moments(1, i, norm)
                dve.tensor_scalar(lnv(1, i, 2), lnv(1, i, 1), EPS, None, ALU.add).then_inc(ln2_var, 1)

            def n2_norm(i):
                dve.wait_ge(ln2_rstd, i + 1)
                if i >= 2:
                    dve.wait_ge(n2_ps, i - 1)
                for n in range(TPR * i, TPR * i + TPR):
                    centre(1, mrg[:, 2 + i % 2, n % TPR, :], norm[:, n, :], n).then_inc(n2_ready, 1)

            def final(i):
                for n in range(TPR * i, TPR * i + TPR):
                    dve.wait_ge(f2_ps, n + 1)
                    dve.wait_ge(res_ready, n + 1)
                    dve.tensor_tensor(nat[:, n, :], bank[:, 6 + n % 2, 0:D], nat[:, n, :], ALU.add).then_inc(y_ready, 1)
                dve.wait_ge(y_ready, TPR * (i + 1))
                moments(2, i, nat)
                dve.tensor_scalar(lnv(2, i, 2), lnv(2, i, 1), EPS, None, ALU.add).then_inc(ln3_var, 1)

            def out_norm(i):
                dve.wait_ge(ln3_rstd, i + 1)
                for n in range(TPR * i, TPR * i + TPR):
                    centre(2, nat[:, n, :], nat[:, n, :], n).then_inc(y_out, 1)

            for i in range(GRID + 2):
                if i < GRID:
                    merged(i)
                    n2_norm(i)
                if i >= 2:
                    final(i - 2)
                    out_norm(i - 2)

        @block.scalar
        def _(act):
            for k in (1, 0):
                load_x(act, k)
            act.dma_start(cs[:, :], cst).then_inc(s_cst, 16)
            act.wait_ge(pads_left, 1)
            act.wait_ge(pads_right, 1)

            def squares(r):
                act.wait_ge(s_x[(r + 1) // 2], 32)
                if r >= 2:
                    act.wait_ge(rsq_ready, r - 1)
                act.activation(sq[:, r % 2, :, :].rearrange("p c q -> p (c q)"),
                               xs[:, r, :, :, :].rearrange("p c q b -> p (c q b)"), ACT.Square).then_inc(sq_ready, 1)

            for r in range(3):
                squares(r)
            for i in range(GRID + 1):
                for r in (2 * i + 3, 2 * i + 4):
                    if r < NB:
                        squares(r)
                if i:
                    for n in range(TPR * (i - 1), TPR * i):
                        act.wait_ge(htr_ps, n + 1)
                        act.copy(ht[:, :, n * P:(n + 1) * P],
                                 bank[0:HALF, 6 + n % 2, 0:2 * P].rearrange("p (m c) -> p m c", m=2)).then_inc(ht_ready, 1)
            for i in range(GRID):
                for m in range(2):
                    act.wait_ge(qk_ps, 4 * i + 1 + m)
                    act.activation(qt[:, m, GRID * i:GRID * i + GRID, :],
                                   bank[0:HALF, (4 * i + m) % 6, 0:CHUNK].rearrange("p (t b) -> p t b", b=B),
                                   ACT.Identity, bias=colb[:, m:m + 1]).then_inc(q_ready, 1)
            for jp in range(T // 2):
                act.wait_ge(p2c_ps, jp + 1)
                w = bank[0:64, jp % 4, 0:H * WIN].rearrange("p (h w) -> p h w", w=WIN)
                act.copy(cmat[:, :, :, 2 * jp].rearrange("p i h -> p h i"), w[:, :, 1:1 + T]).then_inc(p2c_act, 1)
            for i in range(GRID):
                act.wait_ge(vz_ready, TPR * (i + 1))
                act.dma_start(vd[i * CHUNK:(i + 1) * CHUNK, :].rearrange("(n p) o -> p n o", p=P),
                              vn[:, TPR * (i % 3):TPR * (i % 3) + TPR, :]).then_inc(vz_out[i % 3], 16)

            def pt_copy(n):
                act.wait_ge(pt_ps, n + 1)
                if n >= 2:
                    act.wait_ge(o_ps, n - 1)
                act.copy(ptr[0:H3 * T, n % 2, :, :], bank[0:H3 * T, 6, :].rearrange("p (k c) -> p k c", k=4)[:, :, 0:100]).then_inc(pt_sb, 1)

            def o_copy(n):
                act.wait_ge(o_ps, n + 1)
                act.copy(ot[:, :, :, 2 * n:2 * n + 2].rearrange("p m t b -> p m b t"),
                         bank[0:OROWS, 7, 0:4 * T].rearrange("p (m b t) -> p m b t", m=2, b=2)).then_inc(o_sb, 1)

            act.wait_ge(v_ps, NT)
            act.wait_ge(pad_zero, 1)
            for n in range(PAIRS + 4):
                if 0 <= n - 3 < PAIRS:
                    pt_copy(n - 3)
                if n >= 4:
                    o_copy(n - 4)
                if n < PAIRS:
                    act.wait_ge(s_sub, n + 1)
                    act.activation(sring[0:100, n % NR, :], sring[0:100, n % NR, :], ACT.Exp,
                                   scale=float((3 * DH) ** -0.5)).then_inc(s_exp, 1)

            def router_exp():
                act.wait_ge(z_ps, 1)
                act.wait_ge(nbr_ready, 1)
                act.activation(rt[:, :], bank[:, 6, 0:T], ACT.Exp, scale=-1.0, bias=nbr[:, :]).then_inc(z_exp, 1)

            def turned(i, ps_ready, sb_ready, b, gain, shift):
                act.wait_ge(ps_ready, i + 1)
                for m in range(2):
                    act.activation(nt_[:, m, i * CHUNK:(i + 1) * CHUNK], bank[0:HALF, b + m, 0:CHUNK], ACT.Identity,
                                   scale=fcol(gain, m), bias=fcol(shift, m)).then_inc(sb_ready, 1)

            for i in range(GRID):
                turned(i, n_ps, nt_ready, 4 + 2 * (i % 2), "g1", "b1")
                act.wait_ge(nb_ready, i + 1)
                for n in range(TPR * i, TPR * i + TPR):
                    act.activation(nat[:, n, :], nat[:, n, :], ACT.Identity, scale=lnb[:, 0, n, 2:3],
                                   bias=nb1[:, n:n + 1]).then_inc(h1_ready, 1)
                for n in range(TPR * i, TPR * i + TPR):
                    act.wait_ge(v2_ps, n + 1)
                    act.copy(v2s[:, n, :], bank[:, 2 + n % 2, 0:D + 1]).then_inc(v2_ready, 1)
            for u in range(2 * GRID):
                i, m = u // 2, u % 2
                act.wait_ge(k2_ps, u + 1)
                act.activation(ktf[:, m, i * CHUNK:(i + 1) * CHUNK], bank[0:HALF, u % 2, 0:CHUNK], ACT.Identity,
                               bias=fcol("bk2", m)).then_inc(k2_ready, 1)
                if u == 3:
                    router_exp()

            def mix_out(n):
                act.wait_ge(x2_ps, n + 1)
                act.copy(mixed[:, n, :], bank[:, (2 if n < NMIX else 4) + n % 2, 0:D]).then_inc(x2_ready, 1)

            for n in range(NMIX):
                mix_out(n)
            for m in range(2):
                act.wait_ge(q2_ps, m + 1)
                act.activation(qs[:, m, :, :].rearrange("p s b -> p (s b)"), bank[0:HALF, 6 + m, 0:NSEL * B], ACT.Identity,
                               bias=fcol("bq2", m)).then_inc(q2_sb, 1)
            for n in range(NMIX, NMIX2):
                mix_out(n)
            for k in range(3):
                n0, n1 = 12 * k, min(12 * k + 12, PAIRS)
                act.wait_ge(l2_cent, k + 1)
                act.activation(s2[:, n0:n1, :], s2[:, n0:n1, :], ACT.Exp, scale=float(DH ** -0.5)).then_inc(l2_exp, 1)
            for k in range(PAIRS // 4):
                act.wait_ge(t2_ps, k + 1)
                if k >= 2:
                    act.wait_ge(c2_ps, k - 1)
                act.copy(pt2[:, k % 2, :, :].rearrange("p n c -> p (n c)"), bank[0:W2X, 4 + k % 2, :]).then_inc(t2_ready, 1)
            for n in range(NMIX2, NT):
                mix_out(n)
            for i in range(GRID):
                turned(i, n2_ps, n2t_ready, 2, "g2", "b2")
                for k in range(FF // P):
                    u = 6 * i + k
                    act.wait_ge(f1_ps, u + 1)
                    act.activation(hid[:, i % 3, k, :], bank[:, 4 + u % 2, 0:CHUNK], ACT.Gelu,
                                   bias=bf1s[:, k:k + 1]).then_inc(f1_ready, 1)

        @block.gpsimd
        def _(pool):
            def rstd_tok(i):
                pool.wait_ge(tvar, i + 1)
                pool.tensor_tensor(rst[:, :], st[:, 3 * TPR:4 * TPR], nhalf[:, 0:TPR], ALU.pow).then_inc(trstd, 1)

            pool.memset(ones[:, :], 1.0).then_inc(ones_set, 1)
            pool.memset(nhalf[:, :], -0.5).then_inc(nhalf_set, 1)
            pool.wait_ge(ones_set, 1)
            pool.wait_ge(nhalf_set, 1)
            pool.memset(xs[64:128, :, :, NQ - 1, :].rearrange("p r c b -> p (r c) b"), 0.0).then_inc(pads_right, 1)
            pool.wait_ge(pads_right, 1)

            def beta_w():
                pool.wait_ge(wg_ready, 8)
                pool.wait_ge(wc_ready, 4)
                pool.wait_ge(s_gb, 32)
                pool.tensor_tensor(wraw, wraw, bets[:, :].unsqueeze(2).to_broadcast([P, WRAW, D]), ALU.mult).then_inc(wb_ready, 1)
            for i in range(GRID):
                pool.wait_ge(rsq_ready, min(2 * i + 3, NB))
                if i >= 2:
                    pool.wait_ge(ss_ready, i - 1)
                pool.tensor_tensor(esum[i % 2], rsq[:, 2 * i % 6, :], rsq[:, (2 * i + 1) % 6, :], ALU.add).then_inc(esum_set, 1)
                outer = [r for r in (2 * i - 1, 2 * i + 2) if 0 <= r < NB]
                if len(outer) == 2:
                    pool.tensor_tensor(usum[i % 2], rsq[:, outer[0] % 6, :], rsq[:, outer[1] % 6, :], ALU.add).then_inc(esum_set, 1)
                    pool.wait_ge(esum_set, 2 * i + 1)
                    pool.tensor_tensor(usum[i % 2], usum[i % 2], esum[i % 2], ALU.add).then_inc(eu_ready, 1)
                else:
                    pool.wait_ge(esum_set, max(2 * i, 1))
                    pool.tensor_tensor(usum[i % 2], rsq[:, outer[0] % 6, :], esum[i % 2], ALU.add).then_inc(eu_ready, 1)
                if i == 0:
                    beta_w()
                else:
                    rstd_tok(i - 1)
            rstd_tok(GRID - 1)

            for n in range(NT):
                pool.wait_ge(htr_ps, n + 1)
                pool.tensor_tensor(nat[:, n, :], nat[:, n, :], brow_bc("bo1"), ALU.add).then_inc(hb_ready, 1)
            for n in range(PAIRS + 1):
                if n < PAIRS:
                    pool.wait_ge(s_max, n + 1)
                    sv = sring[0:100, n % NR, :].rearrange("p (h j) -> p h j", j=T)
                    pool.tensor_tensor(sv, sv, mx[0:100, n % NR, :].unsqueeze(2).to_broadcast([100, H, T]),
                                       ALU.subtract).then_inc(s_sub, 1)
                if n:
                    k = n - 1
                    pool.wait_ge(s_inv, k + 1)
                    sv = sring[0:100, k % NR, :].rearrange("p (h j) -> p h j", j=T)
                    pool.tensor_tensor(sv, sv, rs[0:100, k % NR, :].unsqueeze(2).to_broadcast([100, H, T]),
                                       ALU.mult).then_inc(s_nrm, 1)

            def rstd(k, i, var_ready, rstd_ready):
                pool.wait_ge(var_ready, i + 1)
                pool.tensor_tensor(lnb[:, k, TPR * i:TPR * i + TPR, 2], lnb[:, k, TPR * i:TPR * i + TPR, 2], nhalf[:, 0:TPR],
                                   ALU.pow).then_inc(rstd_ready, 1)

            for i in range(GRID):
                pool.wait_ge(ln_var, 2 * (i + 1))
                v = lnb[:, 0, TPR * i:TPR * i + TPR, 2:4]
                pool.tensor_tensor(v, v, nhalf[:, :].rearrange("p (n c) -> p n c", c=2), ALU.pow).then_inc(ln_rstd, 1)
            pool.wait_ge(ln_rstd, GRID)
            pool.memset(vj[32:64, :, :], 0.0).then_inc(vj_zero, 1)
            pool.wait_ge(v2_out, 16 * GRID)
            pool.wait_ge(zz_ready, 1)
            pool.wait_ge(vj_zero, 1)
            pool.memset(s2x, 0.0).then_inc(sx_zero, 1)
            pool.wait_ge(nd_out, 16 * GRID)
            pool.wait_ge(idx_ready, 1)
            for k in range(3):
                rows = P if k < 2 else B
                pool.indirect_dma_start(gsb[0:rows, k, :], None, nd, bass.IndirectOffsetOnAxis(ap=idx[0:rows, k:k + 1], axis=0)
                                        ).then_inc(g_in, 16)

            def shift_mix(n):
                pool.wait_ge(x2_ready, n + 1)
                pool.tensor_tensor(mixed[:, n, :], mixed[:, n, :], brow_bc("bm"), ALU.add).then_inc(mb_ready, 1)

            for n in range(NMIX2):
                shift_mix(n)
            for k in range(3):
                rows = P if k < 2 else B
                pool.wait_ge(as_ready, k + 1)
                pool.indirect_dma_start(sd, bass.IndirectOffsetOnAxis(ap=idx[0:rows, k:k + 1], axis=0), asel[0:rows, k, :], None
                                        ).then_inc(sc_out, 16)
            for n in range(NMIX2, NT):
                shift_mix(n)

            def residual(n):
                pool.wait_ge(h2_ready, n + 1)
                pool.tensor_tensor(nat[:, n, :], nat[:, n, :], norm[:, n, :], ALU.add).then_inc(res_part, 1)
                pool.wait_ge(res_part, n + 1)
                pool.tensor_tensor(nat[:, n, :], nat[:, n, :], brow_bc("bf2"), ALU.add).then_inc(res_ready, 1)

            for i in range(GRID + 2):
                if i < GRID:
                    rstd(1, i, ln2_var, ln2_rstd)
                if i >= 2:
                    rstd(2, i - 2, ln3_var, ln3_rstd)
                if i < GRID:
                    for n in range(TPR * i, TPR * i + TPR):
                        residual(n)


def kernel(**a):
    import numpy as np
    import concourse.bacc as bacc
    from concourse.bass_utils import run_bass_kernel_spmd

    x = a["x"].reshape(B, CH, NB, 8, NQ - 1, 2, 8)
    xh = np.stack([x[:, :, :, :, :, 1, :], x[:, :, :, :, :, 0, :]]).transpose(0, 4, 6, 3, 2, 5, 1)
    xh = xh.reshape(P, NB, CH, NQ - 1, B)

    def pack(w):
        o = w.shape[0]
        w = w.reshape(o, 2, 8, 2, 8, 5, CH)
        quad = {(0, 0): 1, (0, 1): 3, (1, 0): 4, (1, 1): 2}
        chunks = []
        for r in range(4):
            for s in range(2):
                q = w[:, r % 2, :, :, :, quad[(r // 2, s)], :]
                chunks.append(q.transpose(2, 1, 3, 4, 0).reshape(P, CH, o))
        for r in range(2):
            q = w[:, r, :, ::-1, :, 0, :]
            chunks.append(q.transpose(2, 1, 3, 4, 0).reshape(P, CH, o))
        return np.concatenate(chunks, axis=1)

    def split(w):
        return w.reshape(2, HALF, -1).transpose(1, 0, 2)

    A, F = "L0_attn_", "L0_ffn_"
    rel = a[A + "rel_table"][127 - (T - 1):127 + T]
    consts = np.zeros((P, 2 * P + 11 + T), np.float32)
    p = np.arange(P)
    consts[:, 0:P] = np.eye(P)
    consts[:, P:2 * P] = p[:, None] % 64 == p[None, :] % 64
    consts[:, 2 * P:2 * P + 6] = (p[:, None] // DH) % 8 == np.arange(6)[None, :]
    consts[:, 2 * P + 6:2 * P + 8] = (p[:, None] // DH) % 2 == np.arange(2)[None, :]
    consts[:, 2 * P + 8] = p < 64
    consts[:, 2 * P + 9] = p >= 64
    t = np.arange(T)
    consts[:, 2 * P + 10] = p % B
    consts[:, 2 * P + 11:] = B * t
    rows = {"tok_b": "L0_tok_b", "bv1": A + "bv", "bo1": A + "bo", "b1": F + "b1",
            "bm": F + "bm", "bo2": F + "bo", "bf2": F + "bf2"}
    by_feature = {"bq1": A + "bq", "bk1": A + "bk", "bpk": A + "bpk", "bpq": A + "bpq", "bq2": F + "bq", "bk2": F + "bk",
                  "g1": F + "g1", "b1": F + "b1", "g2": F + "g2", "b2": F + "b2", "bv2": F + "bv"}
    wout = np.zeros((OROWS, 2, D), np.float32)
    for k in range(4):
        wout[64 * (k % 2):64 * (k % 2) + GW, k // 2, :] = a[A + "Wo"][k * GW:(k + 1) * GW]
    arrays = {
        "x": xh,
        "wtok": pack(a["L0_tok_W"]),
        "gam": pack(a["L0_tok_ln_gamma"].reshape(1, PDIM))[:, :, 0],
        "bet": pack(a["L0_tok_ln_beta"].reshape(1, PDIM))[:, :, 0],
        "watt": np.stack([split(a[A + n]) for n in ("Wq", "Wk", "Wv", "Wpk", "Wpq")], axis=1),
        "wout": wout,
        "relt": np.stack([split(rel[::-1].T), split(rel.T)], axis=1),
        "wffn": np.concatenate([split(a[F + n]) for n in ("Wq", "Wk", "Wv", "Wr", "Wo", "Wm", "W1")], axis=2),
        "w2": a[F + "W2"].reshape(FF // P, P, D).transpose(1, 0, 2),
        "brow": np.stack([a[rows[n]] for n in BIAS_ROWS]),
        "col": np.concatenate([a[by_feature[n]].reshape(2, HALF).T for n in COLS], axis=1),
        "bf1": a[F + "bf1"].reshape(FF // P, P).T,
        "br": a[F + "br"].reshape(1, 1),
        "cst": consts,
        "lower": (t[None, :] < t[:, None]).astype(np.float32).reshape(1, T, T),
    }
    nc = bacc.Bacc("TRN2", target_bir_lowering=False, num_devices=1)
    args, feed = [], {}
    for name, v in arrays.items():
        feed[f"in_{name}"] = np.ascontiguousarray(v)
        args.append(nc.dram_tensor(f"in_{name}", feed[f"in_{name}"].shape, F32, kind="ExternalInput").ap())
    args.append(nc.dram_tensor("out_0", (B, T, D), F32, kind="ExternalOutput").ap())
    build(nc, *args)
    r = run_bass_kernel_spmd(nc, [feed], core_ids=[0])
    return r.results[0]["out_0"]
```
